# Optimizing a Trainium2 kernel written in Bass

```python
import numpy as np
import jax
import jax.numpy as jnp

def _softmax(x, axis=-1):
    return jax.nn.softmax(x, axis=axis)

def _gelu(x):
    return jax.nn.gelu(x, approximate=True)

def _silu(x):
    return jax.nn.silu(x)

def _sigmoid(x):
    return jax.nn.sigmoid(x)

def _layernorm(x, axis=-1, eps=1e-05):
    m = jnp.mean(x, axis=axis, keepdims=True)
    v = jnp.var(x, axis=axis, keepdims=True)
    return (x - m) / jnp.sqrt(v + eps)

def _scatter_add(tgt, idx, src, axis=0):
    return tgt.at[idx].add(src)

def _segment_sum(src, seg, n):
    return jax.ops.segment_sum(src, seg, n)
kernel_name = 'mk_xattn_ffn_d1_seqx_r4_bb3742'

def setup_inputs(seed: int=0):
    np.random.seed(seed)
    _w = jnp.asarray

    def _rec_inputs():
        import jax
        import jax.numpy as jnp
        _rk = jax.random.key(seed)
        x = 0.01048 + 0.1018 * jax.random.normal(jax.random.fold_in(_rk, 1), (4, 512, 512), jnp.float32)
        _lenS = 512 - jax.random.randint(jax.random.fold_in(_rk, 7), (4,), 0, max(1, 512 // 4) + 1, jnp.int32)
        _lenS2 = 512 - jax.random.randint(jax.random.fold_in(_rk, 8), (4,), 0, max(1, 512 // 4) + 1, jnp.int32)
        _ctx_512P = jax.random.normal(jax.random.fold_in(_rk, 11), (4, 16, 128), jnp.float32)
        _ctx_512c = jax.random.dirichlet(jax.random.fold_in(_rk, 511), 0.3 * jnp.ones((16,), jnp.float32), (4, 512))
        _ctx_512t = jnp.einsum('bsk,bkd->bsd', _ctx_512c, _ctx_512P)
        _ctx_512t = _ctx_512t * jax.lax.rsqrt(jnp.mean(jnp.square(_ctx_512t)) + 1e-12) * 0.953939
        ctx_512 = -0.000292821 + 1.00034 * (_ctx_512t + 0.3 * jax.random.normal(jax.random.fold_in(_rk, 611), (4, 512, 128), jnp.float32))
        return (x, ctx_512)
    x, ctx_512 = _rec_inputs()

    def _L0_xattn_setup():
        import jax, jax.numpy as jnp
        import numpy as np
        LRELU_ALPHA = 0.2
        MASK_VAL = -10000000000.0
        B, N, F_IN = (4, 512, 128)
        H, F_OUT = (8, 64)
        F_HID = H * F_OUT

        def gat_layer(x, adj, W, a_self, a_neigh, b):
            feat = jnp.einsum('nf,hfo->hno', x, W)
            attn_self = jnp.einsum('hno,ho->hn', feat, a_self)
            attn_neigh = jnp.einsum('hno,ho->hn', feat, a_neigh)
            e = attn_self[:, :, None] + attn_neigh[:, None, :]
            e = jax.nn.leaky_relu(e, LRELU_ALPHA)
            e = e + MASK_VAL * (1.0 - adj)[None, :, :]
            alpha = jax.nn.softmax(e, axis=-1)
            out = jnp.einsum('hnm,hmo->hno', alpha, feat) + b[:, None, :]
            out = jnp.transpose(out, (1, 0, 2)).reshape(out.shape[1], -1)
            return jax.nn.elu(out)
        key = jax.random.key(seed)
        ks = jax.random.split(key, 10)
        feats = jax.random.normal(ks[0], (B, N, F_IN), dtype=jnp.float32)
        a = (jax.random.uniform(ks[1], (B, N, N)) < 0.01).astype(jnp.float32)
        adj = jnp.maximum(a, jnp.eye(N, dtype=jnp.float32)[None])
        s0 = 1.0 / np.sqrt(F_IN)
        s1 = 1.0 / np.sqrt(F_HID)
        return {'feats': feats, 'adj': adj, 'W0': jax.random.normal(ks[2], (H, F_IN, F_OUT), dtype=jnp.float32) * s0, 'a_self0': jax.random.normal(ks[3], (H, F_OUT), dtype=jnp.float32) * 0.1, 'a_neigh0': jax.random.normal(ks[4], (H, F_OUT), dtype=jnp.float32) * 0.1, 'b0': jnp.zeros((H, F_OUT), dtype=jnp.float32), 'W1': jax.random.normal(ks[5], (H, F_HID, F_OUT), dtype=jnp.float32) * s1, 'a_self1': jax.random.normal(ks[6], (H, F_OUT), dtype=jnp.float32) * 0.1, 'a_neigh1': jax.random.normal(ks[7], (H, F_OUT), dtype=jnp.float32) * 0.1, 'b1': jnp.zeros((H, F_OUT), dtype=jnp.float32)}
    _L0_xattn_all = _L0_xattn_setup()
    _L0_xattn_in = {k: v for k, v in _L0_xattn_all.items() if k in ('W0', 'a_self0', 'a_neigh0', 'b0', 'W1', 'a_self1', 'a_neigh1', 'b1')}
    del _L0_xattn_all

    def _L0_ffn_setup():
        import jax, jax.numpy as jnp
        import numpy as np
        H = 512
        I = 352
        E = 16
        G = 4
        TOPK_GROUP = 2
        K = 4
        SI = 2 * I
        SCALE = 1.0
        NORM = True
        B, S = (4, 128)

        def _swiglu(h):
            g, u = jnp.split(h, 2, axis=-1)
            return jax.nn.silu(g) * u

        def _combine_weights(xt, gate_w):
            T = xt.shape[0]
            scores = jax.nn.softmax(xt @ gate_w.T, axis=-1)
            group_scores = scores.reshape(T, G, E // G).max(axis=-1)
            _, gidx = jax.lax.top_k(group_scores, TOPK_GROUP)
            gmask = jnp.zeros((T, G), bool).at[jnp.arange(T)[:, None], gidx].set(True)
            emask = jnp.repeat(gmask, E // G, axis=1)
            masked = jnp.where(emask, scores, 0.0)
            w, eidx = jax.lax.top_k(masked, K)
            if NORM:
                w = w / (w.sum(-1, keepdims=True) + 1e-20)
            w = w * SCALE
            return jnp.zeros((T, E), xt.dtype).at[jnp.arange(T)[:, None], eidx].add(w)
        key = jax.random.key(seed)
        ks = jax.random.split(key, 6)
        sc = lambda fan_in: 1.0 / np.sqrt(fan_in)
        return {'x': jax.random.normal(ks[0], (B, S, H), jnp.float32), 'gate_w': jax.random.normal(ks[1], (E, H), jnp.float32) * sc(H), 'expert_up_w': jax.random.normal(ks[2], (E, 2 * I, H), jnp.float32) * sc(H), 'expert_down_w': jax.random.normal(ks[3], (E, H, I), jnp.float32) * sc(I), 'shared_up_w': jax.random.normal(ks[4], (2 * SI, H), jnp.float32) * sc(H), 'shared_down_w': jax.random.normal(ks[5], (H, SI), jnp.float32) * sc(SI)}
    _L0_ffn_all = _L0_ffn_setup()
    _L0_ffn_in = {k: v for k, v in _L0_ffn_all.items() if k in ('gate_w', 'expert_up_w', 'expert_down_w', 'shared_up_w', 'shared_down_w')}
    del _L0_ffn_all
    return {'x': x, 'ctx_512': ctx_512, 'L0_xattn_W0': _L0_xattn_in['W0'], 'L0_xattn_a_self0': _L0_xattn_in['a_self0'], 'L0_xattn_a_neigh0': _L0_xattn_in['a_neigh0'], 'L0_xattn_b0': _L0_xattn_in['b0'], 'L0_xattn_W1': _L0_xattn_in['W1'], 'L0_xattn_a_self1': _L0_xattn_in['a_self1'], 'L0_xattn_a_neigh1': _L0_xattn_in['a_neigh1'], 'L0_xattn_b1': _L0_xattn_in['b1'], 'L0_ffn_gate_w': _L0_ffn_in['gate_w'], 'L0_ffn_expert_up_w': _L0_ffn_in['expert_up_w'], 'L0_ffn_expert_down_w': _L0_ffn_in['expert_down_w'], 'L0_ffn_shared_up_w': _L0_ffn_in['shared_up_w'], 'L0_ffn_shared_down_w': _L0_ffn_in['shared_down_w']}

def reference(x, ctx_512, L0_xattn_W0, L0_xattn_a_self0, L0_xattn_a_neigh0, L0_xattn_b0, L0_xattn_W1, L0_xattn_a_self1, L0_xattn_a_neigh1, L0_xattn_b1, L0_ffn_gate_w, L0_ffn_expert_up_w, L0_ffn_expert_down_w, L0_ffn_shared_up_w, L0_ffn_shared_down_w):
    import jax
    import jax.numpy as jnp

    def _L0_xattn_ref(feats, adj, W0, a_self0, a_neigh0, b0, W1, a_self1, a_neigh1, b1):
        import jax, jax.numpy as jnp
        import numpy as np
        LRELU_ALPHA = 0.2
        MASK_VAL = -10000000000.0
        B, N, F_IN = (4, 512, 128)
        H, F_OUT = (8, 64)
        F_HID = H * F_OUT

        def gat_layer(x, adj, W, a_self, a_neigh, b):
            feat = jnp.einsum('nf,hfo->hno', x, W)
            attn_self = jnp.einsum('hno,ho->hn', feat, a_self)
            attn_neigh = jnp.einsum('hno,ho->hn', feat, a_neigh)
            e = attn_self[:, :, None] + attn_neigh[:, None, :]
            e = jax.nn.leaky_relu(e, LRELU_ALPHA)
            e = e + MASK_VAL * (1.0 - adj)[None, :, :]
            alpha = jax.nn.softmax(e, axis=-1)
            out = jnp.einsum('hnm,hmo->hno', alpha, feat) + b[:, None, :]
            out = jnp.transpose(out, (1, 0, 2)).reshape(out.shape[1], -1)
            return jax.nn.elu(out)

        def per_graph(x, a):
            h = gat_layer(x, a, W0, a_self0, a_neigh0, b0)
            return gat_layer(h, a, W1, a_self1, a_neigh1, b1)
        return jax.vmap(per_graph)(feats, adj)

    def _L0_ffn_ref(x, gate_w, expert_up_w, expert_down_w, shared_up_w, shared_down_w):
        import jax, jax.numpy as jnp
        import numpy as np
        H = 512
        I = 352
        E = 16
        G = 4
        TOPK_GROUP = 2
        K = 4
        SI = 2 * I
        SCALE = 1.0
        NORM = True
        B, S = (4, 128)

        def _swiglu(h):
            g, u = jnp.split(h, 2, axis=-1)
            return jax.nn.silu(g) * u

        def _combine_weights(xt, gate_w):
            T = xt.shape[0]
            scores = jax.nn.softmax(xt @ gate_w.T, axis=-1)
            group_scores = scores.reshape(T, G, E // G).max(axis=-1)
            _, gidx = jax.lax.top_k(group_scores, TOPK_GROUP)
            gmask = jnp.zeros((T, G), bool).at[jnp.arange(T)[:, None], gidx].set(True)
            emask = jnp.repeat(gmask, E // G, axis=1)
            masked = jnp.where(emask, scores, 0.0)
            w, eidx = jax.lax.top_k(masked, K)
            if NORM:
                w = w / (w.sum(-1, keepdims=True) + 1e-20)
            w = w * SCALE
            return jnp.zeros((T, E), xt.dtype).at[jnp.arange(T)[:, None], eidx].add(w)
        Bq, Sq, _ = x.shape
        xt = x.reshape(-1, H)
        cw = _combine_weights(xt, gate_w)
        out = jnp.zeros_like(xt)
        for e in range(E):
            a = _swiglu(xt @ expert_up_w[e].T)
            out = out + cw[:, e:e + 1] * (a @ expert_down_w[e].T)
        out = out + _swiglu(xt @ shared_up_w.T) @ shared_down_w.T
        return out.reshape(Bq, Sq, H)
    x = x + _L0_xattn_ref(ctx_512, _layernorm(x, axis=-1), L0_xattn_W0, L0_xattn_a_self0, L0_xattn_a_neigh0, L0_xattn_b0, L0_xattn_W1, L0_xattn_a_self1, L0_xattn_a_neigh1, L0_xattn_b1)
    x = x + _L0_ffn_ref(_layernorm(x, axis=-1), L0_ffn_gate_w, L0_ffn_expert_up_w, L0_ffn_expert_down_w, L0_ffn_shared_up_w, L0_ffn_shared_down_w)
    return x

_drawn_inputs = setup_inputs


def setup_inputs(seed=0):
    import zlib

    import numpy as np

    out = dict(_drawn_inputs(seed))
    spreads = {'L0_xattn_b0': (0.0, 0.1), 'L0_xattn_b1': (0.0, 0.1)}
    factors = {}
    for name, (base, spread) in spreads.items():
        noise = np.random.default_rng([zlib.crc32(name.encode()), seed]).standard_normal(out[name].shape)
        drawn = base * np.exp(spread * noise) if base else spread * noise
        out[name] = jnp.asarray(drawn.astype(out[name].dtype))
    for name, factor in factors.items():
        out[name] = (out[name] * factor).astype(out[name].dtype)
    return out
```

```python
import concourse.bass as bass
from concourse import mybir
from contextlib import ExitStack


def gat_then_experts(nc, x, ctxT, W0, as0, an0, b0, W1, as1, an1, b1, gateT, experts, out):
    f32 = mybir.dt.float32
    ALU = mybir.AluOpType
    ACT = mybir.ActivationFunctionType
    AX = mybir.AxisListType
    i32 = mybir.dt.int32

    G, N, D = x.shape
    P = 128
    NC = N // P
    H, F_IN, O = W0.shape
    KC = D // P
    TT = G * NC
    R = H * NC
    SLOPE = 0.2
    MASK = 1e10
    EPS = 1e-5
    RING = 2 * NC
    HP = H // 2
    AHEAD_X = 6
    AHEAD_E = 4
    FREE = 2

    T = G * N
    E = gateT.shape[1]
    NGR, TOPG, TOPK = 4, 2, 4
    EG = E // NGR
    U = experts.shape[0]
    SH = U - E
    WL = experts.shape[2]
    DC = 3
    I = (WL - DC * D) // (2 * KC)
    LASTD = I - (DC - 1) * P
    SS = SH * TT
    RS = T * TOPK // P + E - 1
    NS = SS + RS
    RT = RS + 1
    NT = NS + 1
    PADS = P
    UP = KC * 2 * I

    x_v = x.rearrange("g (c p) d -> p (g c) d", p=P)
    out_v = out[0:T, :].rearrange("(t p) d -> p t d", p=P)

    ctx = ExitStack()
    with ctx:
        def sb(name, shape, dt=f32):
            return ctx.enter_context(nc.sbuf_tensor(name, shape, dt))

        def pb(name, shape, dt=f32):
            return ctx.enter_context(nc.psum_tensor(name, shape, dt))

        def sem(name):
            return ctx.enter_context(nc.semaphore(name))

        x_sb = sb("x_sb", [P, TT, D])
        ctx_sb = sb("ctx_sb", [P, N])
        w0_sb = sb("w0_sb", [P, 1, H, O])
        w1_sb = sb("w1_sb", [P, KC, H, O])
        att_bc = sb("att_bc", [P, 4, H * O])
        b_col = sb("b_col", [P, 2, HP])
        b_neg = sb("b_neg", [P, 2, HP])
        prod = sb("prod", [P, H * O])
        wa = sb("wa", [P, 1 + KC, 2 * H])
        ident = sb("ident", [P, P])
        stats = sb("stats", [P, TT, 6])
        mv = sb("mv", [P, TT, 2])
        rstd = sb("rstd", [P, TT])
        nmask = sb("nmask", [P, NC, N])
        feat = sb("feat", [P, NC, H * O])
        head_feat = sb("head_feat", [P, 2, NC, O])
        hT = sb("hT", [P, KC, N])
        st_sb = sb("st_sb", [2 * H, N])
        negs = sb("negs", [P, NC, H])
        scol = sb("scol", [P, 2, NC])
        t_sb = sb("t_sb", [P, 2, N])
        wbuf = sb("wbuf", [P, 2 * WL])
        ring = wbuf[:, 0:RING * N].rearrange("p (s n) -> p s n", n=N)
        mx = sb("mx", [P, RING])
        rsum = sb("rsum", [P, RING])
        rec = sb("rec", [P, RING])
        eT = wbuf[:, RING * N:(RING + 2 * NC) * N].rearrange("p (i c n) -> p i c n", i=2, n=N)
        pos = sb("pos", [P, N])
        neg = sb("neg", [P, N])
        t_rows = nc.dram_tensor("t_rows", [H, N], f32, kind="Internal").ap()

        tri = sb("tri", [P, P])
        ones = sb("ones", [P, P])
        count = sb("count", [P, P])
        count_p = sb("count_p", [P, E])
        below = sb("below", [P, E, E])
        token = sb("token", [P, TT])
        pad_row = sb("pad_row", [P, 1])
        shared_rows = sb("shared_rows", [P, SH, TT])
        gate_sb = sb("gate_sb", [P, KC, E])
        xg = sb("xg", [P, 2, D])
        xT = sb("xT", [P, 2, KC, P])
        score = sb("score", [P, TT, E])
        rmax = sb("rmax", [P, TT])
        rtot = sb("rtot", [P, TT])
        gtop = sb("gtop", [P, TT, NGR])
        grank = sb("grank", [P, TT, NGR])
        gcmp = sb("gcmp", [P, TT, NGR])
        rank = sb("rank", [P, TT, E])
        cmp = sb("cmp", [P, TT, E])
        sel = sb("sel", [P, TT, E])
        comb = sb("comb", [P, TT, E])
        place = sb("place", [P, TT, E])
        eq = sb("eq", [P, TT, E])
        load = sb("load", [P, E])
        tiles = sb("tiles", [P, E])
        first = sb("first", [P, E])
        first_row = sb("first_row", [P, E])
        sq = sb("sq", [P, E, E])
        place_k = sb("place_k", [P, TT, TOPK])
        w_k = sb("w_k", [P, TT, TOPK])
        place_i = sb("place_i", [P, TT, TOPK], i32)
        slot_i = sb("slot_i", [P, TT, TOPK], i32)
        row_i = sb("row_i", [P, TT, TOPK], i32)
        slot_f = sb("slot_f", [P, TT, TOPK])
        row_f = sb("row_f", [P, TT, TOPK])
        tok_k = sb("tok_k", [P, TT, TOPK])
        row_hot = sb("row_hot", [P, 2, TOPK, P])
        slot_hot = sb("slot_hot", [P, 2, TOPK, RT])
        entry = sb("entry", [P, 2, TOPK, 2, RT])
        idx_f = sb("idx_f", [P, RT])
        idx_tab = sb("idx_tab", [P, NT], i32)
        w_tab = sb("w_tab", [P, NT])
        owner = sb("owner", [1, RS, E])
        present = sb("present", [1, E])
        ctl = sb("ctl", [1, 3, NS], i32)
        ctl_f = sb("ctl_f", [1, 3, NS])
        gidx = sb("gidx", [P, 2], i32)
        sidx = sb("sidx", [P, 2], i32)
        sg = sb("sg", [P, I])
        hid = sb("hid", [P, I])
        hidT = sb("hidT", [P, DC, P])
        y_sb = sb("y_sb", [P, 2, D])
        zrow = sb("zrow", [PADS, D])
        xn_rows = nc.dram_tensor("xn_rows", [T + PADS, D], f32, kind="Internal").ap()

        tr_ps = pb("tr_ps", [P, 2, NC, P])
        o_ps = pb("o_ps", [P, 2, N])
        f_ps = pb("f_ps", [P, NC, H * O])

        w_in = sem("w_in")
        x_in = [sem(f"x_in{g}") for g in range(G)]
        ctx_in = sem("ctx_in")
        t_out = sem("t_out")
        t_in = [sem(f"t_in{i}") for i in range(2)]
        setup_pool = sem("setup_pool")
        consts = sem("consts")
        setup_dve = sem("setup_dve")
        var_done = sem("var_done")
        std_done = sem("std_done")
        wa_ready = sem("wa_ready")
        mask_step = sem("mask_step")
        st_done = sem("st_done")
        st_copied = sem("st_copied")
        s_turned = sem("s_turned")
        s_copied = sem("s_copied")
        feat_done = sem("feat_done")
        feat_copied = sem("feat_copied")
        scol_ready = sem("scol_ready")
        head_feat_ready = sem("head_feat_ready")
        x_ready = sem("x_ready")
        z_ready = sem("z_ready")
        e_ready = sem("e_ready")
        p_ready = sem("p_ready")
        rec_ready = sem("rec_ready")
        alpha_ready = sem("alpha_ready")
        T_done = sem("T_done")
        evac_done = sem("evac_done")
        mixed = sem("mixed")
        parts_ready = sem("parts_ready")
        elu_parts = sem("elu_parts")
        hT_ready = sem("hT_ready")
        h_turned = sem("h_turned")
        x2_ready = sem("x2_ready")
        stored = sem("stored")
        moe_set = sem("moe_set")
        moe_consts = sem("moe_consts")
        MC = 9 + 3 * SH
        var2_done = sem("var2_done")
        std2_done = sem("std2_done")
        xn_ready = sem("xn_ready")
        xn_out = [sem(f"xn_out{i}") for i in range(2)]
        pads_out = sem("pads_out")
        x2_out = sem("x2_out")
        gate_in = sem("gate_in")
        turned = sem("turned")
        xT_ready = sem("xT_ready")
        logits_done = sem("logits_done")
        route_step = sem("route_step")
        shift_done = sem("shift_done")
        exp_done = sem("exp_done")
        sel_ready = sem("sel_ready")
        counted = sem("counted")
        entry_ready = sem("entry_ready")
        entered = sem("entered")
        tables_ready = sem("tables_ready")
        idx_copied = sem("idx_copied")
        xg_in = [sem(f"xg_in{i}") for i in range(2)]
        w_ready = sem("w_ready")
        up_done = sem("up_done")
        silu_done = sem("silu_done")
        hid_ready = sem("hid_ready")
        hid_turned = sem("hid_turned")
        hidT_ready = sem("hidT_ready")
        down_done = sem("down_done")
        y_ready = sem("y_ready")
        added = sem("added")

        sp_waited, pool_waited, dve_waited, pe_waited = [sem(f"{n}_waited") for n in ("sp", "pool", "dve", "pe")]
        block = ctx.enter_context(nc.Block())

        @block.sync
        def _(sp):
            sp.dma_start(w0_sb[:, 0, :, :], W0.rearrange("h f o -> f h o")).then_inc(w_in, 16)
            for n, a in enumerate((as0, an0, as1, an1)):
                sp.dma_start(att_bc[:, n, :], a.rearrange("h o -> (h o)").partition_broadcast(P)).then_inc(w_in, 16)
            for k in range(KC):
                sp.dma_start(w1_sb[:, k, :, :], W1[:, k * P:(k + 1) * P, :].rearrange("h f o -> f h o")).then_inc(w_in, 16)
            for n, a in enumerate((b0, b1)):
                sp.dma_start(b_col[:, n, :], a.rearrange("(j i) o -> (i o) j", i=2),
                             allow_slow_non_contiguous=True).then_inc(w_in, 16)
            for g in range(G):
                sp.dma_start(x_sb[:, NC * g:NC * (g + 1), :], x_v[:, NC * g:NC * (g + 1), :]).then_inc(x_in[g], 16)
            with sp.Fori(0, G) as g:
                sp.wait_ge(feat_done, 2 * g + FREE)
                sp.dma_start(ctx_sb[:], ctxT[bass.ds(g, 1), :, :].rearrange("a f n -> f (a n)")).then_inc(ctx_in, 16)
                for l in range(2):
                    L = 2 * g + l
                    sp.wait_ge(st_copied, L + 1)
                    sp.dma_start(t_rows, st_sb[H:2 * H, :]).then_inc(t_out, 16)
                    sp.wait_ge(t_out, 16 * L + 16)
                    for i in range(2):
                        sp.dma_start(t_sb[:, i, :], t_rows[i, :].partition_broadcast(P)).then_inc(t_in[i], 16)
                    with sp.Fori(1, HP) as j:
                        for i in range(2):
                            sp.wait_ge(x_ready, R * L + NC * (2 * j + i - 1))
                            sp.dma_start(t_sb[:, i, :], t_rows[bass.ds(2 * j + i, 1), :].rearrange("a n -> (a n)").partition_broadcast(P)).then_inc(t_in[i], 16)
            sp.dma_start(gate_sb[:], gateT.rearrange("(k p) e -> p k e", p=P)).then_inc(gate_in, 16)
            sp.wait_ge(moe_consts, MC)
            sp.dma_start(xn_rows[T:T + PADS, :], zrow[:]).then_inc(pads_out, 16)
            sp.dma_start(out[T:T + PADS, :], zrow[:]).then_inc(pads_out, 16)
            sp.wait_ge(x2_ready, G * HP)
            sp.dma_start(out_v, x_sb[:]).then_inc(x2_out, 16)
            with sp.Fori(0, TT // 2) as j:
                for i in range(2):
                    sp.wait_ge(xn_ready, 2 * j + i + 1)
                    sp.dma_start(xn_rows[bass.ds((2 * j + i) * P, P), :], xg[:, i, :]).then_inc(xn_out[i], 16)
            sp.wait_ge(tables_ready, 1)
            with sp.Fori(0, NS) as t:
                expert = sp.value_load(ctl[0:1, 0, bass.ds(t, 1)], min_val=0, max_val=U - 1)
                new = sp.value_load(ctl[0:1, 1, bass.ds(t, 1)], min_val=0, max_val=1)
                half = sp.value_load(ctl[0:1, 2, bass.ds(t, 1)], min_val=0, max_val=1)
                sp.wait_ge(w_ready, 16 * t + 16)
                sp.sem_inc(sp_waited, 1)
                sp.wait_ge(down_done, t + 1)
                sp.sem_inc(sp_waited, 1)
                with sp.If(new):
                    sp.dma_start(wbuf[:, bass.ds(half * WL, WL)],
                                 experts[bass.ds(expert, 1), :, :].rearrange("a p w -> p (a w)")).then_inc(w_ready, 16)
                with sp.Else():
                    sp.sem_inc(w_ready, 16)

        @block.gpsimd
        def _(pool):
            nc.gpsimd.memset(ident[:], 0.0).then_inc(setup_pool, 1)
            pool.wait_ge(setup_pool, 1)
            nc.gpsimd.affine_select(out=ident[:], in_=ident[:], compare_op=ALU.not_equal, fill=1.0,
                                    base=0, pattern=[[-1, P]], channel_multiplier=1).then_inc(consts, 1)
            pool.sem_inc(T_done, RING)
            pool.sem_inc(parts_ready, FREE)
            pool.sem_inc(feat_done, FREE)
            pool.sem_inc(hT_ready, 1)

            nc.gpsimd.memset(ones[:], 1.0).then_inc(moe_set, 1)
            nc.gpsimd.memset(below[:], 1.0).then_inc(moe_set, 1)
            nc.gpsimd.memset(zrow[:], 0.0).then_inc(moe_consts, 1)
            pool.wait_ge(moe_set, 2)
            nc.gpsimd.affine_select(out=tri[:], in_=ones[:], compare_op=ALU.is_gt, fill=0.0, base=0,
                                    pattern=[[1, P]], channel_multiplier=-1).then_inc(moe_consts, 1)
            nc.gpsimd.affine_select(out=below[:], in_=below[:], compare_op=ALU.is_gt, fill=0.0, base=0,
                                    pattern=[[1, E], [-1, E]], channel_multiplier=0).then_inc(moe_consts, 1)
            exact = dict(allow_small_or_imprecise_dtypes=True)
            nc.gpsimd.iota(count[:], pattern=[[1, P]], base=0, channel_multiplier=0, **exact).then_inc(moe_consts, 1)
            nc.gpsimd.iota(count_p[:], pattern=[[P, E]], base=0, channel_multiplier=0, **exact).then_inc(moe_consts, 1)
            nc.gpsimd.iota(token[:], pattern=[[P, TT]], base=0, channel_multiplier=1, **exact).then_inc(moe_consts, 1)
            nc.gpsimd.iota(pad_row[:], pattern=[[1, 1]], base=T, channel_multiplier=1, **exact).then_inc(moe_consts, 1)
            nc.gpsimd.iota(idx_tab[:, 0:SS].rearrange("p (u t) -> p u t", u=SH), pattern=[[0, SH], [P, TT]], base=0,
                           channel_multiplier=1).then_inc(moe_consts, 1)
            nc.gpsimd.memset(w_tab[:, 0:SS], 1.0).then_inc(moe_consts, 1)
            nc.gpsimd.memset(ctl_f[:], 0.0).then_inc(moe_set, 1)
            pool.wait_ge(moe_set, 3)
            for u in range(SH):
                nc.gpsimd.memset(ctl_f[0:1, 0, u * TT:(u + 1) * TT], float(E + u)).then_inc(moe_consts, 1)
                nc.gpsimd.memset(ctl_f[0:1, 1, u * TT:u * TT + 1], 1.0).then_inc(moe_consts, 1)
                nc.gpsimd.memset(ctl_f[0:1, 2, u * TT:(u + 1) * TT], float(u % 2)).then_inc(moe_consts, 1)
            pool.sem_inc(w_ready, 16)
            pool.sem_inc(down_done, 2)
            pool.sem_inc(y_ready, 1)
            pool.sem_inc(turned, FREE)
            for i in range(2):
                pool.sem_inc(xn_out[i], 16)

            def sum_step(L, j, s):
                h, c = 2 * j + s // NC, s % NC
                i, slot = (s // NC) % 2, s % RING
                if c == 0:
                    pool.wait_ge(t_in[i], 16 * (HP * L + j + s // RING + 1))
                    pool.wait_ge(scol_ready, H * L + h + 1)
                pool.wait_ge(T_done, R * L + RING * j + s + 1)
                pool.sem_inc(pool_waited, 1)
                nc.gpsimd.tensor_scalar(ring[:, slot, :], t_sb[:, i, :], scol[:, i, c:c + 1], 1.0,
                                        ALU.add, ALU.mult).then_inc(x_ready, 1)

            def head_pair(L, j, last):
                for s in range(RING):
                    if not (last and s + AHEAD_X >= RING):
                        sum_step(L, j, s + AHEAD_X)
                    if s % 2 == 0:
                        pool.wait_ge(rec_ready, R // 2 * L + HP * j + s // 2 + 1)
                        pool.sem_inc(pool_waited, 1)
                    nc.gpsimd.tensor_scalar(ring[:, s, :], ring[:, s, :], rec[:, s:s + 1], 1.0,
                                            ALU.mult, ALU.mult).then_inc(alpha_ready, 1)

            with pool.Fori(0, G) as g:
                for l in range(2):
                    L = 2 * g + l
                    for s in range(AHEAD_X):
                        sum_step(L, 0, s)
                    with pool.Fori(0, HP - 1) as j:
                        head_pair(L, j, False)
                    head_pair(L, HP - 1, True)

            def gather(t, i, copies):
                pool.wait_ge(turned, TT + t - 1 + FREE)
                nc.gpsimd.tensor_copy(gidx[:, i:i + 1], idx_tab[:, bass.ds(t, 1)]).then_inc(idx_copied, 1)
                pool.wait_ge(idx_copied, copies)
                pool.sem_inc(pool_waited, 1)
                nc.gpsimd.indirect_dma_start(xg[:, i, :], None, xn_rows, bass.IndirectOffsetOnAxis(ap=gidx[:, i:i + 1], axis=0),
                                             bounds_check=T + PADS - 1, oob_is_err=True).then_inc(xg_in[i], 16)

            def scatter(t, i, copies, first=False):
                if not first:
                    pool.wait_ge(added, 16 * t)
                nc.gpsimd.tensor_copy(sidx[:, i:i + 1], idx_tab[:, bass.ds(t, 1)]).then_inc(idx_copied, 1)
                pool.wait_ge(idx_copied, copies)
                pool.wait_ge(y_ready, t + 2)
                pool.sem_inc(pool_waited, 1)
                nc.gpsimd.indirect_dma_start(out, bass.IndirectOffsetOnAxis(ap=sidx[:, i:i + 1], axis=0), y_sb[:, i, :], None,
                                             bounds_check=T + PADS - 1, oob_is_err=True, compute_op=ALU.add).then_inc(added, 16)

            pool.wait_ge(tables_ready, 1)
            for i in range(2):
                pool.wait_ge(xn_out[i], 16 * (TT // 2 + 1))
            pool.wait_ge(pads_out, 32)
            pool.wait_ge(x2_out, 16)
            gather(0, 0, 1)
            gather(1, 1, 2)

            def slot_pair(j, first):
                for i in range(2):
                    t = 2 * j + 1 + i
                    gather(t + 1, i, 2 * t + 1)
                    scatter(t - 1, i, 2 * t + 2, first and i == 0)

            slot_pair(0, True)
            with pool.Fori(1, (NS - 1) // 2) as j:
                slot_pair(j, False)
            scatter(NS - 1, (NS - 1) % 2, 2 * NS + 1)
            pool.wait_ge(added, 16 * NS)

        @block.scalar
        def _(act):
            act.wait_ge(wa_ready, 1)
            act.wait_ge(var_done, 1)
            nc.scalar.activation(rstd[:], rstd[:], ACT.Sqrt).then_inc(std_done, 1)

            def exp_step(L, r, slot):
                act.wait_ge(e_ready, R * L + r + 1)
                nc.scalar.activation(ring[:, slot, :], ring[:, slot, :], ACT.Exp, bias=mx[:, slot:slot + 1], scale=-1.0,
                                     accum_out=rsum[:, slot:slot + 1]).then_inc(p_ready, 1)

            def elu_parts_step(L, l, j, i):
                half = slice(O * i, O * i + O)
                act.wait_ge(mixed, H * L + 2 * j + i + 1)
                if i == 0:
                    act.wait_ge(hT_ready, HP * L + j + 1)
                nc.scalar.activation(pos[half, :], o_ps[half, i, :], ACT.Relu, bias=b_col[half, l, bass.ds(j, 1)])
                nc.scalar.activation(neg[half, :], o_ps[half, i, :], ACT.Relu, scale=-1.0,
                                     bias=b_neg[half, l, bass.ds(j, 1)]).then_inc(parts_ready, 1)
                if i == 1:
                    act.wait_ge(parts_ready, H * L + 2 * j + 2 + FREE)
                    nc.scalar.activation(neg[:], neg[:], ACT.Exp, scale=-1.0).then_inc(elu_parts, 1)

            def head_pair(L, l, j, first, last):
                for s in range(RING):
                    r = RING * j + s
                    act.wait_ge(T_done, R * L + r + 1 + RING)
                    c = s % NC
                    nc.scalar.activation(eT[:, s // NC, :, c * P:(c + 1) * P], tr_ps[:, s % 2, :, :], ACT.Copy).then_inc(evac_done, 1)
                    if c == 0 and not first:
                        elu_parts_step(L, l, j - 1, s // NC)
                    if not (last and s + AHEAD_E >= RING):
                        exp_step(L, r + AHEAD_E, (s + AHEAD_E) % RING)

            with act.Fori(0, G) as g:
                for l in range(2):
                    L = 2 * g + l
                    for s in range(AHEAD_E):
                        exp_step(L, s, s)
                    head_pair(L, l, 0, True, False)
                    with act.Fori(1, HP - 1) as j:
                        head_pair(L, l, j, False, False)
                    head_pair(L, l, HP - 1, False, True)
                    elu_parts_step(L, l, HP - 1, 0)
                    elu_parts_step(L, l, HP - 1, 1)

            act.wait_ge(var2_done, 1)
            nc.scalar.activation(rstd[:], rstd[:], ACT.Sqrt).then_inc(std2_done, 1)

            def copy_turned(n, i):
                act.wait_ge(turned, n + 1 + FREE)
                nc.scalar.activation(xT[:, i, :, :], tr_ps[:, i, :, :], ACT.Copy).then_inc(xT_ready, 1)

            with act.Fori(0, TT // 2) as j:
                for i in range(2):
                    copy_turned(2 * j + i, i)
            act.wait_ge(shift_done, 1)
            nc.scalar.activation(score[:], score[:], ACT.Exp).then_inc(exp_done, 1)

            def slot(t, i):
                act.wait_ge(up_done, t + 1)
                nc.scalar.activation(sg[:], o_ps[:, 0, 0:I], ACT.Silu).then_inc(silu_done, 1)
                copy_turned(TT + t + 1, 1 - i)
                act.wait_ge(hid_turned, t + 1)
                nc.scalar.activation(hidT[:, 0:DC - 1, :], f_ps[:, 0, 0:(DC - 1) * P].rearrange("p (c q) -> p c q", q=P), ACT.Copy)
                nc.scalar.activation(hidT[0:LASTD, DC - 1, :], f_ps[0:LASTD, 0, (DC - 1) * P:DC * P], ACT.Copy).then_inc(hidT_ready, 1)

            copy_turned(TT, 0)
            slot(0, 0)
            with act.Fori(0, (NS - 1) // 2) as j:
                slot(2 * j + 1, 1)
                slot(2 * j + 2, 0)

        @block.vector
        def _(dve):
            made = [0]

            def then(ins):
                made[0] += 1
                ins.then_inc(setup_dve, 1)
                dve.wait_ge(setup_dve, made[0])

            dve.wait_ge(w_in, 16 * (1 + KC + 6))
            for l, w in ((0, w0_sb), (1, w1_sb)):
                for k in range(w.shape[1]):
                    for n in range(2):
                        then(nc.vector.tensor_tensor(prod[:], w[:, k, :, :].rearrange("p h o -> p (h o)"),
                                                     att_bc[:, 2 * l + n, :], ALU.mult))
                        then(nc.vector.tensor_reduce(out=wa[:, l + k, n * H:(n + 1) * H],
                                                     in_=prod[:].rearrange("p (h o) -> p h o", h=H),
                                                     op=ALU.add, axis=AX.X, negate=True))
            nc.vector.tensor_scalar(b_neg[:], b_col[:], -1.0, None, ALU.mult).then_inc(wa_ready, 1)
            for t in range(TT):
                if t % NC == 0:
                    dve.wait_ge(x_in[t // NC], 16)
                last = nc.vector.bn_stats(stats[:, t, :], x_sb[:, t, :])
            then(last)
            for t in range(TT):
                last = nc.vector.bn_aggr(mv[:, t, :], stats[:, t, :])
            then(last)
            nc.vector.tensor_scalar(rstd[:], mv[:, :, 1], EPS, None, ALU.add).then_inc(var_done, 1)
            dve.wait_ge(std_done, 1)
            then(nc.vector.reciprocal(rstd[:], rstd[:]))

            def score_step(L, j, k):
                s = 2 * k
                dve.wait_ge(x_ready, R * L + RING * j + s + 2)
                nc.vector.scalar_tensor_tensor(ring[:, s:s + 2, :], ring[:, s:s + 2, :], SLOPE,
                                               ring[:, s:s + 2, :], ALU.mult, ALU.min).then_inc(z_ready, 1)
                dve.wait_ge(z_ready, R // 2 * L + HP * j + k + 1)
                dve.sem_inc(dve_waited, 1)
                for m in range(2):
                    nc.vector.tensor_tensor_reduce(
                        out=ring[:, s + m, :], in0=ring[:, s + m, :], in1=nmask[:, (s + m) % NC, :],
                        scale=1.0, scalar=3.0e38, op0=ALU.add, op1=ALU.min,
                        accum_out=mx[:, s + m:s + m + 1]).then_inc(e_ready, 1)

            def reciprocal_step(L, j, k):
                s = (2 * k) % RING
                dve.wait_ge(p_ready, R * L + RING * j + 2 * k + 2)
                nc.vector.reciprocal(rec[:, s:s + 2], rsum[:, s:s + 2]).then_inc(rec_ready, 1)

            def column_step(h, i):
                nc.vector.tensor_copy(scol[:, i, :], negs[:, :, bass.ds(h, 1)].rearrange("p c a -> p (c a)")).then_inc(scol_ready, 1)

            def weight_step(L, h, i):
                dve.wait_ge(parts_ready, H * L + h - 1 + FREE)
                nc.vector.tensor_copy(head_feat[:, i, :, :], feat[:, :, bass.ds(O * h, O)]).then_inc(head_feat_ready, 1)

            def elu_step(L, j):
                dve.wait_ge(elu_parts, HP * L + j + 1)
                nc.vector.scalar_tensor_tensor(hT[:, bass.ds(j, 1), :].rearrange("p a n -> p (a n)"), neg[:], -1.0, pos[:],
                                               ALU.add, ALU.add).then_inc(hT_ready, 1)

            def head_pair(L, j, first, last):
                for k in range(HP):
                    score_step(L, j, k)
                    if not (first and k == 0):
                        reciprocal_step(L, j, k - 1)
                    if k % 2 == 1 and not last:
                        column_step(2 * j + k // 2 + 2, k // 2)
                    if k == 1 and not first:
                        weight_step(L, 2 * j - 1, 1)
                    if k == 3:
                        weight_step(L, 2 * j, 0)
                if not first:
                    elu_step(L, j - 1)

            with dve.Fori(0, G) as g:
                for c in range(NC):
                    t = NC * g + c
                    nc.vector.tensor_scalar(nmask[:, c, :], x_sb[:, bass.ds(t, 1), :].rearrange("p a d -> p (a d)"),
                                            mv[:, bass.ds(t, 1), 0:1].rearrange("p a d -> p (a d)"),
                                            rstd[:, bass.ds(t, 1)], ALU.subtract, ALU.mult).then_inc(mask_step, 1)
                for c in range(NC):
                    dve.wait_ge(mask_step, 2 * NC * g + c + 1)
                    nc.vector.tensor_scalar(nmask[:, c, :], nmask[:, c, :], -1.0, -MASK, ALU.add, ALU.mult).then_inc(mask_step, 1)
                for l in range(2):
                    L = 2 * g + l
                    dve.wait_ge(st_done, L + 1)
                    nc.vector.tensor_copy(st_sb[:], o_ps[0:2 * H, 0, :]).then_inc(st_copied, 1)
                    dve.wait_ge(s_turned, L + 1)
                    nc.vector.tensor_copy(negs[:], o_ps[:, 1, 0:NC * 2 * H].rearrange("p (c h) -> p c h", c=NC)[:, :, 0:H]).then_inc(s_copied, 1)
                    dve.wait_ge(s_copied, L + 1)
                    for i in range(2):
                        column_step(i, i)
                    dve.wait_ge(feat_done, L + 1 + FREE)
                    nc.vector.tensor_copy(feat[:], f_ps[:]).then_inc(feat_copied, 1)
                    dve.wait_ge(feat_copied, L + 1)
                    head_pair(L, 0, True, False)
                    with dve.Fori(1, HP - 1) as j:
                        head_pair(L, j, False, False)
                    head_pair(L, HP - 1, False, True)
                    reciprocal_step(L, HP - 1, HP - 1)
                    weight_step(L, H - 1, 1)
                    elu_step(L, HP - 1)
                for j in range(HP):
                    dve.wait_ge(h_turned, HP * g + j + 1)
                    xt = x_sb[:, bass.ds(NC * g, NC), j * P:(j + 1) * P]
                    nc.vector.tensor_tensor(xt, xt, f_ps[:, j, :].rearrange("p (c q) -> p c q", c=NC), ALU.add).then_inc(x2_ready, 1)

            steps = [0]

            def step(ins):
                steps[0] += 1
                ins.then_inc(route_step, 1)
                return steps[0]

            def after(n):
                dve.wait_ge(route_step, n)

            def wide(ap, n):
                return ap.unsqueeze(len(ap.shape)).to_broadcast(list(ap.shape) + [n])

            dve.wait_ge(x2_ready, G * HP)
            for t in range(TT):
                n = step(nc.vector.bn_stats(stats[:, t, :], x_sb[:, t, :]))
            after(n)
            for t in range(TT):
                n = step(nc.vector.bn_aggr(mv[:, t, :], stats[:, t, :]))
            after(n)
            nc.vector.tensor_scalar(rstd[:], mv[:, :, 1], EPS, None, ALU.add).then_inc(var2_done, 1)
            dve.wait_ge(std2_done, 1)
            after(step(nc.vector.reciprocal(rstd[:], rstd[:])))
            with dve.Fori(0, TT // 2) as j:
                for i in range(2):
                    t = 2 * j + i
                    dve.wait_ge(turned, t - 1 + FREE)
                    dve.wait_ge(xn_out[i], 16 * j + 16)
                    nc.vector.tensor_scalar(xg[:, i, :], x_sb[:, bass.ds(t, 1), :].rearrange("p a d -> p (a d)"),
                                            mv[:, bass.ds(t, 1), 0:1].rearrange("p a d -> p (a d)"),
                                            rstd[:, bass.ds(t, 1)], ALU.subtract, ALU.mult).then_inc(xn_ready, 1)

            dve.wait_ge(moe_consts, MC)
            dve.wait_ge(logits_done, TT)
            logits = f_ps[:, 2, 0:TT * E].rearrange("p (t e) -> p t e", e=E)
            after(step(nc.vector.tensor_reduce(out=rmax[:], in_=logits, op=ALU.max, axis=AX.X)))
            nc.vector.tensor_tensor(score[:], logits, wide(rmax[:], E), ALU.subtract).then_inc(shift_done, 1)
            dve.wait_ge(exp_done, 1)
            after(step(nc.vector.tensor_reduce(out=rtot[:], in_=score[:], op=ALU.add, axis=AX.X)))
            after(step(nc.vector.reciprocal(rtot[:], rtot[:])))
            after(step(nc.vector.tensor_tensor(score[:], score[:], wide(rtot[:], E), ALU.mult)))

            def ranks(out_, in_, scratch, n):
                last = step(nc.vector.memset(out_, 0.0))
                for f in range(n):
                    step(nc.vector.tensor_tensor(scratch[:, :, 0:f + 1], wide(in_[:, :, f], f + 1), in_[:, :, 0:f + 1], ALU.is_gt))
                    if f + 1 < n:
                        step(nc.vector.tensor_tensor(scratch[:, :, f + 1:n], wide(in_[:, :, f], n - f - 1), in_[:, :, f + 1:n], ALU.is_ge))
                    after(steps[0])
                    last = step(nc.vector.tensor_tensor(out_, out_, scratch, ALU.add))
                    after(last)

            after(step(nc.vector.tensor_reduce(out=gtop[:], in_=score[:].rearrange("p t (g e) -> p t g e", g=NGR), op=ALU.max, axis=AX.X)))
            ranks(grank[:], gtop[:], gcmp[:], NGR)
            after(step(nc.vector.tensor_scalar(grank[:], grank[:], float(TOPG), None, ALU.is_lt)))
            after(step(nc.vector.tensor_tensor(score[:].rearrange("p t (g e) -> p (t g) e", g=NGR),
                                               score[:].rearrange("p t (g e) -> p (t g) e", g=NGR),
                                               wide(grank[:].rearrange("p t g -> p (t g)"), EG), ALU.mult)))
            ranks(rank[:], score[:], cmp[:], E)
            nc.vector.tensor_scalar(sel[:], rank[:], float(TOPK), None, ALU.is_lt).then_inc(sel_ready, 1)
            dve.wait_ge(sel_ready, 1)
            after(step(nc.vector.tensor_tensor(comb[:], score[:], sel[:], ALU.mult)))
            after(step(nc.vector.tensor_reduce(out=rtot[:], in_=comb[:], op=ALU.add, axis=AX.X)))
            after(step(nc.vector.tensor_scalar(rtot[:], rtot[:], 1e-20, None, ALU.add)))
            after(step(nc.vector.reciprocal(rtot[:], rtot[:])))
            after(step(nc.vector.tensor_tensor(comb[:], comb[:], wide(rtot[:], E), ALU.mult)))

            dve.wait_ge(counted, 1)
            after(step(nc.vector.tensor_copy(load[:], f_ps[:, 0, 0:E])))
            after(step(nc.vector.tensor_tensor(sq[:], wide(load[:], E), count_p[:].unsqueeze(1).to_broadcast([P, E, E]), ALU.is_gt)))
            after(step(nc.vector.tensor_reduce(out=tiles[:], in_=sq[:], op=ALU.add, axis=AX.X)))
            after(step(nc.vector.tensor_tensor(sq[:], below[:], tiles[:].unsqueeze(1).to_broadcast([P, E, E]), ALU.mult)))
            after(step(nc.vector.tensor_reduce(out=first[:], in_=sq[:], op=ALU.add, axis=AX.X)))
            after(step(nc.vector.tensor_scalar(first_row[:], first[:], float(P), None, ALU.mult)))
            after(step(nc.vector.tensor_tensor(place[:], f_ps[:, 3, 0:TT * E].rearrange("p (t e) -> p t e", e=E),
                                               first_row[:].unsqueeze(1).to_broadcast([P, TT, E]), ALU.add)))
            for k in range(TOPK):
                after(step(nc.vector.tensor_scalar(eq[:], rank[:], float(k), None, ALU.is_equal)))
                step(nc.vector.tensor_tensor(cmp[:], eq[:], place[:], ALU.mult))
                after(step(nc.vector.tensor_tensor(sel[:], eq[:], comb[:], ALU.mult)))
                step(nc.vector.tensor_reduce(out=place_k[:, :, k], in_=cmp[:], op=ALU.add, axis=AX.X))
                after(step(nc.vector.tensor_reduce(out=w_k[:, :, k], in_=sel[:], op=ALU.add, axis=AX.X)))
            after(step(nc.vector.tensor_copy(place_i[:], place_k[:])))
            step(nc.vector.tensor_scalar(slot_i[:], place_i[:], 7, None, ALU.logical_shift_right))
            after(step(nc.vector.tensor_scalar(row_i[:], place_i[:], P - 1, None, ALU.bitwise_and)))
            step(nc.vector.tensor_copy(slot_f[:], slot_i[:]))
            after(step(nc.vector.tensor_copy(row_f[:], row_i[:])))
            after(step(nc.vector.tensor_tensor(tok_k[:], wide(token[:], TOPK), row_f[:], ALU.subtract)))
            after(step(nc.vector.tensor_scalar(tok_k[:], tok_k[:], float(-T), None, ALU.add)))
            for t in range(TT):
                i = t % 2
                if t >= 2:
                    dve.wait_ge(entered, t - 1)
                step(nc.vector.tensor_tensor(row_hot[:, i, :, :], count[:].unsqueeze(1).to_broadcast([P, TOPK, P]),
                                             wide(row_f[:, t, :], P), ALU.is_equal))
                after(step(nc.vector.tensor_tensor(slot_hot[:, i, :, :], count[:, 0:RT].unsqueeze(1).to_broadcast([P, TOPK, RT]),
                                                   wide(slot_f[:, t, :], RT), ALU.is_equal)))
                step(nc.vector.tensor_tensor(entry[:, i, :, 0, :], slot_hot[:, i, :, :], wide(tok_k[:, t, :], RT), ALU.mult))
                after(steps[0])
                nc.vector.tensor_tensor(entry[:, i, :, 1, :], slot_hot[:, i, :, :], wide(w_k[:, t, :], RT), ALU.mult).then_inc(entry_ready, 1)

            after(step(nc.vector.tensor_tensor(owner[:], wide(count[0:1, 0:RS], E), first[0:1, :].unsqueeze(1).to_broadcast([1, RS, E]), ALU.is_ge)))
            after(step(nc.vector.tensor_reduce(out=ctl_f[0:1, 0, SS:NS], in_=owner[:], op=ALU.add, axis=AX.X)))
            after(step(nc.vector.tensor_scalar(ctl_f[0:1, 0, SS:NS], ctl_f[0:1, 0, SS:NS], -1.0, None, ALU.add)))
            step(nc.vector.tensor_tensor(ctl_f[0:1, 1, SS:NS], ctl_f[0:1, 0, SS:NS], ctl_f[0:1, 0, SS - 1:NS - 1], ALU.not_equal))
            after(step(nc.vector.tensor_scalar(present[:], tiles[0:1, :], 0.0, None, ALU.is_gt)))
            after(step(nc.vector.tensor_tensor(owner[:, :, 1:E], owner[:, :, 1:E], present[0:1, 0:E - 1].unsqueeze(1).to_broadcast([1, RS, E - 1]), ALU.mult)))
            after(step(nc.vector.tensor_reduce(out=ctl_f[0:1, 2, SS:NS], in_=owner[:, :, 1:E], op=ALU.add, axis=AX.X)))
            after(step(nc.vector.tensor_copy(ctl[:], ctl_f[:])))
            after(step(nc.vector.tensor_scalar(ctl[0:1, 2, :], ctl[0:1, 2, :], 1, None, ALU.bitwise_and)))
            dve.wait_ge(entered, TT)
            after(step(nc.vector.tensor_scalar(idx_f[:], f_ps[:, 1, 0:RT], pad_row[:, 0:1], None, ALU.add)))
            step(nc.vector.tensor_copy(w_tab[:, SS:NT], f_ps[:, 1, RT:2 * RT]))
            after(steps[0])
            nc.vector.tensor_copy(idx_tab[:, SS:NT], idx_f[:]).then_inc(tables_ready, 1)
            dve.wait_ge(tables_ready, 1)

            def gate_step(t):
                dve.wait_ge(silu_done, t + 1)
                nc.vector.tensor_tensor(hid[:], sg[:], o_ps[:, 1, 0:I], ALU.mult).then_inc(hid_ready, 1)

            def weigh_step(t, i, first=False):
                dve.wait_ge(down_done, t + 1 + 2)
                if not first:
                    dve.wait_ge(added, 16 * t - 16)
                nc.vector.tensor_scalar(y_sb[:, i, :], f_ps[:, 2, :], w_tab[:, bass.ds(t, 1)], None, ALU.mult).then_inc(y_ready, 1)

            gate_step(0)
            for t in range(2):
                gate_step(t + 1)
                weigh_step(t, t, first=True)
            with dve.Fori(1, (NS - 1) // 2) as j:
                for i in range(2):
                    gate_step(2 * j + 1 + i)
                    weigh_step(2 * j + i, i)
            weigh_step(NS - 1, 0)

        @block.tensor
        def _(pe):
            pe.wait_ge(consts, 1)
            pe.wait_ge(w_in, 16 * (1 + KC + 6))
            pe.wait_ge(wa_ready, 1)

            def transpose_step(L, j, s, wait_copy=True):
                r = RING * j + s
                pe.wait_ge(alpha_ready, R * L + r + 1)
                if wait_copy:
                    pe.wait_ge(evac_done, R * L + r - 1)
                for m in range(NC):
                    last = nc.tensor.transpose(tr_ps[:, s % 2, m, :], ring[:, s % RING, m * P:(m + 1) * P], ident[:])
                last.then_inc(T_done, 1)

            def mix_step(L, h, i, m):
                if m == 0:
                    pe.wait_ge(evac_done, R * L + NC * h + NC)
                    pe.wait_ge(head_feat_ready, H * L + h + 1)
                    pe.wait_ge(parts_ready, H * L + h - 1 + FREE)
                done = nc.tensor.matmul(o_ps[O * i:O * i + O, i, :], head_feat[:, i, m, :], eT[:, i, m, :],
                                        start=(m == 0), stop=(m == NC - 1))
                if m == NC - 1:
                    done.then_inc(mixed, 1)

            def head_pair(L, j, last):
                for s in range(RING):
                    if not (last and s + NC >= RING):
                        transpose_step(L, j, s + NC)
                    mix_step(L, 2 * j + s // NC, s // NC, s % NC)

            with pe.Fori(0, G) as g:
                for l in range(2):
                    L = 2 * g + l
                    w = w0_sb if l == 0 else w1_sb
                    K = 1 if l == 0 else KC

                    def lhs(k):
                        return ctx_sb[:] if l == 0 else hT[:, k, :]

                    if l == 0:
                        pe.wait_ge(ctx_in, 16 * g + 16)
                    else:
                        for k in range(K - 1):
                            pe.wait_ge(hT_ready, HP * (L - 1) + k + 2)
                            for c in range(NC):
                                nc.tensor.matmul(f_ps[:, c, :], lhs(k)[:, c * P:(c + 1) * P],
                                                 w[:, k, :, :].rearrange("p h o -> p (h o)"), start=(k == 0), stop=False)
                        pe.wait_ge(hT_ready, HP * (L - 1) + K + 1)
                    for k in range(K):
                        last = nc.tensor.matmul(o_ps[0:2 * H, 0, :], wa[:, l + k, :], lhs(k), start=(k == 0), stop=(k == K - 1))
                    last.then_inc(st_done, 1)
                    for c in range(NC):
                        last = nc.tensor.matmul(f_ps[:, c, :], lhs(K - 1)[:, c * P:(c + 1) * P],
                                                w[:, K - 1, :, :].rearrange("p h o -> p (h o)"), start=(K == 1), stop=True)
                    last.then_inc(feat_done, 1)
                    pe.wait_ge(st_copied, L + 1)
                    pe.sem_inc(pe_waited, 1)
                    for c in range(NC):
                        last = nc.tensor.transpose(o_ps[:, 1, c * 2 * H:(c + 1) * 2 * H], st_sb[:, c * P:(c + 1) * P], ident[0:2 * H, 0:2 * H])
                    last.then_inc(s_turned, 1)
                    for s in range(NC):
                        transpose_step(L, 0, s, wait_copy=s >= 2)
                    with pe.Fori(0, HP - 1) as j:
                        head_pair(L, j, False)
                    head_pair(L, HP - 1, True)
                for j in range(HP):
                    pe.wait_ge(hT_ready, HP * (2 * g + 1) + j + 2)
                    for c in range(NC):
                        last = nc.tensor.transpose(f_ps[:, j, c * P:(c + 1) * P], hT[:, j, c * P:(c + 1) * P], ident[:])
                    last.then_inc(h_turned, 1)
                pe.wait_ge(x2_ready, HP * (g + 1))

            pe.wait_ge(gate_in, 16)
            with pe.Fori(0, TT // 2) as j:
                for i in range(2):
                    pe.wait_ge(xn_ready, 2 * j + i + 1)
                    for k in range(KC):
                        last = nc.tensor.transpose(tr_ps[:, i, k, :], xg[:, i, k * P:(k + 1) * P], ident[:])
                    last.then_inc(turned, 1)
                for i in range(2):
                    pe.wait_ge(xT_ready, 2 * j + i + 1)
                    for k in range(KC):
                        last = nc.tensor.matmul(f_ps[:, 2, bass.ds((2 * j + i) * E, E)], xT[:, i, k, :], gate_sb[:, k, :],
                                                start=(k == 0), stop=(k == KC - 1))
                    last.then_inc(logits_done, 1)

            pe.wait_ge(moe_consts, MC)
            pe.wait_ge(sel_ready, 1)
            nc.tensor.matmul(f_ps[:, 3, 0:E], tri[:], sel[:, 0, :], start=True, stop=True)
            nc.tensor.matmul(f_ps[:, 3, E:TT * E], tri[:], sel[:, 1:TT, :].rearrange("p t e -> p (t e)"), start=True, stop=False)
            for t in reversed(range(TT - 1)):
                nc.tensor.matmul(f_ps[:, 3, (t + 1) * E:TT * E].rearrange("p (t e) -> p t e", e=E), ones[:],
                                 sel[:, t:t + 1, :].to_broadcast([P, TT - 1 - t, E]), start=False, stop=(t == 0))
            for t in range(TT):
                last = nc.tensor.matmul(f_ps[:, 0, 0:E], ones[:], sel[:, t, :], start=(t == 0), stop=(t == TT - 1))
            last.then_inc(counted, 1)
            for t in range(TT):
                pe.wait_ge(entry_ready, t + 1)
                for k in range(TOPK):
                    last = nc.tensor.matmul(f_ps[:, 1, 0:2 * RT], row_hot[:, t % 2, k, :],
                                            entry[:, t % 2, k, :, :].rearrange("p a s -> p (a s)"),
                                            start=(t == 0 and k == 0), stop=(t == TT - 1 and k == TOPK - 1))
                last.then_inc(entered, 1)

            pe.wait_ge(tables_ready, 1)

            def turn(t, i, nth):
                pe.wait_ge(xg_in[i], 16 * nth)
                for k in range(KC):
                    last = nc.tensor.transpose(tr_ps[:, i, k, :], xg[:, i, k * P:(k + 1) * P], ident[:])
                last.then_inc(turned, 1)

            def up(t, i, half):
                pe.wait_ge(w_ready, 16 * t + 32)
                pe.wait_ge(xT_ready, TT + t + 1)
                for part in range(2):
                    for k in range(KC):
                        last = nc.tensor.matmul(o_ps[:, part, 0:I], xT[:, i, k, :], wbuf[:, bass.ds(half * WL + (2 * k + part) * I, I)],
                                                start=(k == 0), stop=(k == KC - 1))
                last.then_inc(up_done, 1)

            def down(t, half):
                pe.wait_ge(hidT_ready, t + 1)
                pe.wait_ge(y_ready, t + 1)
                for c in range(DC):
                    rows = P if c < DC - 1 else LASTD
                    last = nc.tensor.matmul(f_ps[:, 2, :], hidT[0:rows, c, :], wbuf[0:rows, bass.ds(half * WL + UP + c * D, D)],
                                            start=(c == 0), stop=(c == DC - 1))
                last.then_inc(down_done, 1)

            def turn_hidden(t):
                pe.wait_ge(hid_ready, t + 1)
                for c in range(DC):
                    rows = P if c < DC - 1 else LASTD
                    last = nc.tensor.transpose(f_ps[0:rows, 0, c * P:(c + 1) * P], hid[:, c * P:c * P + rows], ident[:])
                last.then_inc(hid_turned, 1)

            def half_of(t):
                return pe.value_load(ctl[0:1, 2, bass.ds(t, 1)], min_val=0, max_val=1)

            turn(0, 0, 1)
            up(0, 0, half_of(0))
            turn(1, 1, 1)
            turn_hidden(0)
            with pe.Fori(0, (NS - 1) // 2) as j:
                for i in range(2):
                    t = 2 * j + 1 + i
                    up(t, 1 - i, half_of(t))
                    turn(t + 1, i, j + 1 + 1)
                    down(t - 1, half_of(t - 1))
                    turn_hidden(t)
            down(NS - 1, half_of(NS - 1))


_IN = ("x", "ctxT", "W0", "as0", "an0", "b0", "W1", "as1", "an1", "b1", "gateT", "experts")


def kernel(**inputs):
    import numpy as np
    import concourse.bacc as bacc
    from concourse import mybir
    from concourse.bass_utils import run_bass_kernel_spmd

    a = {n.replace("L0_xattn_", "").replace("L0_ffn_", ""): np.asarray(v) for n, v in inputs.items()}
    P, D, I, E = 128, 512, 352, 16

    def up_rows(w):
        return w.T.reshape(D // P, P, 2 * I).transpose(1, 0, 2).reshape(P, -1)

    def down_rows(w):
        full = np.zeros((3 * P, D), w.dtype)
        full[:I] = w.T
        return full.reshape(3, P, D).transpose(1, 0, 2).reshape(P, -1)

    units = [(a["expert_up_w"][e], a["expert_down_w"][e]) for e in range(E)]
    S = 2 * I
    for u in range(2):
        rows = slice(u * I, (u + 1) * I)
        units.append((np.concatenate([a["shared_up_w"][0:S][rows], a["shared_up_w"][S:2 * S][rows]]),
                      a["shared_down_w"][:, rows]))
    experts = np.stack([np.concatenate([up_rows(u), down_rows(d)], axis=1) for u, d in units])
    arrays = dict(zip(_IN, (a["x"], a["ctx_512"].transpose(0, 2, 1), a["W0"], a["a_self0"], a["a_neigh0"], a["b0"],
                            a["W1"], a["a_self1"], a["a_neigh1"], a["b1"], a["gate_w"].T, experts)))
    arrays = {n: np.ascontiguousarray(v) for n, v in arrays.items()}
    nc = bacc.Bacc("TRN2", target_bir_lowering=False, num_devices=1)
    args = [nc.dram_tensor(f"in_{n}", v.shape, mybir.dt.from_np(v.dtype), kind="ExternalInput").ap() for n, v in arrays.items()]
    T = a["x"].shape[0] * a["x"].shape[1]
    out = nc.dram_tensor("out_rows", (T + P, D), mybir.dt.float32, kind="ExternalOutput").ap()
    gat_then_experts(nc, *args, out)
    r = run_bass_kernel_spmd(nc, [{f"in_{n}": v for n, v in arrays.items()}], core_ids=[0])
    return r.results[0]["out_rows"][:T].reshape(a["x"].shape)
```

```python
import concourse.bass as bass
from concourse import mybir
from contextlib import ExitStack


def gat_then_experts(nc, x, ctxT, W0, as0, an0, b0, W1, as1, an1, b1, gateT, experts, out):
    f32 = mybir.dt.float32
    ALU = mybir.AluOpType
    ACT = mybir.ActivationFunctionType
    AX = mybir.AxisListType
    i32 = mybir.dt.int32
    f32r = mybir.dt.float32r


    G, N, D = x.shape
    P = 128
    NC = N // P
    H, F_IN, O = W0.shape
    KC = D // P
    TT = G * NC
    R = H * NC
    SLOPE = 0.2
    MASK = 1e10
    EPS = 1e-5
    RING = 2 * NC
    HP = H // 2
    AHEAD_X = 6
    AHEAD_E = 4
    FREE = 2

    T = G * N
    E = gateT.shape[1]
    NGR, TOPG, TOPK = 4, 2, 4
    EG = E // NGR
    U = experts.shape[0]
    SH = U - E
    WL = experts.shape[2]
    DC = 3
    I = (WL - DC * D) // (2 * KC)
    LASTD = I - (DC - 1) * P
    SS = SH * TT
    RS = T * TOPK // P + E - 1
    PADS = P
    UP = KC * 2 * I
    PIECES = ((0, UP // 2), (UP // 2, UP), (UP, WL))
    NP_ = len(PIECES)

    x_v = x.rearrange("g (c p) d -> p (g c) d", p=P)

    ctx = ExitStack()
    with ctx:
        def sb(name, shape, dt=f32):
            return ctx.enter_context(nc.sbuf_tensor(name, shape, dt))

        def pb(name, shape, dt=f32):
            return ctx.enter_context(nc.psum_tensor(name, shape, dt))

        def sem(name):
            return ctx.enter_context(nc.semaphore(name))

        x_sb = sb("x_sb", [P, TT, D])
        ctx_sb = sb("ctx_sb", [P, N])
        w0_sb = sb("w0_sb", [P, 1, H, O])
        with nc.sbuf_tensor("attention", [P, 4 * WL], f32) as attention:
            pass
        split = ctx.enter_context(nc.sbuf_tensor("split", [P, 4 * WL], f32r))
        w_stage = sb("w_stage", [P, 2 * WL])
        at = [0]

        def shared_space(cols):
            at[0] += cols
            return attention[:, at[0] - cols:at[0]]

        w1_sb = shared_space(KC * H * O).rearrange("p (k h o) -> p k h o", k=KC, h=H)
        att_bc = sb("att_bc", [P, 4, H * O])
        b_col = sb("b_col", [P, 2, HP])
        b_neg = sb("b_neg", [P, 2, HP])
        prod = sb("prod", [P, H * O])
        wa = sb("wa", [P, 1 + KC, 2 * H])
        ident = sb("ident", [P, P])
        stats = sb("stats", [P, TT, 6])
        mv = sb("mv", [P, TT, 2])
        rstd = sb("rstd", [P, TT])
        nmask = shared_space(NC * N).rearrange("p (c n) -> p c n", c=NC)
        feat = shared_space(NC * H * O).rearrange("p (c n) -> p c n", c=NC)
        head_feat = sb("head_feat", [P, 2, NC, O])
        hT = shared_space(KC * N).rearrange("p (c n) -> p c n", c=KC)
        st_sb = sb("st_sb", [2 * H, N])
        negs = sb("negs", [P, NC, H])
        scol = sb("scol", [P, 2, NC])
        t_sb = sb("t_sb", [P, 2, N])
        ring = shared_space(RING * N).rearrange("p (s n) -> p s n", n=N)
        mx = sb("mx", [P, RING])
        rsum = sb("rsum", [P, RING])
        rec = sb("rec", [P, RING])
        eT = shared_space(2 * NC * N).rearrange("p (i c n) -> p i c n", i=2, n=N)
        pos = sb("pos", [P, N])
        neg = sb("neg", [P, N])
        t_rows = nc.dram_tensor("t_rows", [H, N], f32, kind="Internal").ap()

        tri = sb("tri", [P, P])
        ones = sb("ones", [P, P])
        count = sb("count", [P, P])
        count_p = sb("count_p", [P, E])
        below = sb("below", [P, E, E])
        token = sb("token", [P, TT])
        pad_row = sb("pad_row", [P, 1])
        gate_sb = sb("gate_sb", [P, KC, E])
        xg = sb("xg", [P, 2, D])
        xT_hi = sb("xT_hi", [P, 2, KC, P], f32r)
        xT = [a[:].rearrange("p (k q) -> p k q", k=KC) for a in (pos, neg)]
        xT_lo = sb("xT_lo", [P, 2, KC, P], f32r)
        score = sb("score", [P, TT, E])
        rmax = sb("rmax", [P, TT])
        rtot = sb("rtot", [P, TT])
        gtop = sb("gtop", [P, TT, NGR])
        grank = sb("grank", [P, TT, NGR])
        gcmp = sb("gcmp", [P, TT, NGR])
        rank = sb("rank", [P, TT, E])
        cmp = sb("cmp", [P, TT, E])
        sel = sb("sel", [P, TT, E])
        comb = sb("comb", [P, TT, E])
        place = sb("place", [P, TT, E])
        eq = sb("eq", [P, TT, E])
        load = sb("load", [P, E])
        tiles = sb("tiles", [P, E])
        first = sb("first", [P, E])
        first_row = sb("first_row", [P, E])
        sq = sb("sq", [P, E, E])
        place_k = sb("place_k", [P, TT, TOPK])
        w_k = sb("w_k", [P, TT, TOPK])
        place_i = sb("place_i", [P, TT, TOPK], i32)
        slot_i = sb("slot_i", [P, TT, TOPK], i32)
        row_i = sb("row_i", [P, TT, TOPK], i32)
        slot_f = sb("slot_f", [P, TT, TOPK])
        row_f = sb("row_f", [P, TT, TOPK])
        tok_k = sb("tok_k", [P, TT, TOPK])
        row_hot = sb("row_hot", [P, 2, TOPK, P])
        spare = att_bc[:].rearrange("p a n -> p (a n)")
        slot_hot = spare[:, 0:2 * TOPK * RS].rearrange("p (i k s) -> p i k s", i=2, k=TOPK)
        entry = spare[:, 2 * TOPK * RS:6 * TOPK * RS].rearrange("p (i k a s) -> p i k a s", i=2, k=TOPK, a=2)
        idx_f = sb("idx_f", [P, RS])
        idx_tab = sb("idx_tab", [P, RS], i32)
        w_tab = sb("w_tab", [P, RS])
        owner = sb("owner", [1, RS, E])
        prior = sb("prior", [1, RS])
        ctl = sb("ctl", [1, 3, RS], i32)
        ctl_f = sb("ctl_f", [1, 3, RS])
        gidx = sb("gidx", [P, 2], i32)
        sidx = sb("sidx", [P, 2], i32)
        sg = sb("sg", [P, I])
        hid = sb("hid", [P, I])
        hidT_hi = sb("hidT_hi", [P, DC, P], f32r)
        hidT_lo = sb("hidT_lo", [P, DC, P], f32r)
        up_sb = prod[:, 0:I]
        hidT = neg[:, 0:DC * P].rearrange("p (c q) -> p c q", q=P)
        xT_sb = pos[:].rearrange("p (c q) -> p c q", q=P)
        sum_sb = ctx_sb
        y_sb = t_sb
        zrow = sb("zrow", [PADS, D])
        xn_rows = nc.dram_tensor("xn_rows", [T + PADS, D], f32, kind="Internal").ap()

        BEFORE_COUNTS = TT // 2 - 1 - TT // 4

        tr_ps = pb("tr_ps", [P, 2, NC, P])
        o_ps = pb("o_ps", [P, 2, N])
        f_ps = pb("f_ps", [P, NC, H * O])

        def hidden_ps(a, b):
            return f_ps[:, 0, a * P:b * P].rearrange("p (c q) -> p c q", q=P)

        w_in = sem("w_in")
        x_in = [sem(f"x_in{g}") for g in range(G)]
        ctx_in = sem("ctx_in")
        t_out = sem("t_out")
        t_in = [sem(f"t_in{i}") for i in range(2)]
        setup_pool = sem("setup_pool")
        consts = sem("consts")
        setup_dve = sem("setup_dve")
        var_done = sem("var_done")
        std_done = sem("std_done")
        wa_ready = sem("wa_ready")
        mask_step = sem("mask_step")
        st_done = sem("st_done")
        st_copied = sem("st_copied")
        s_turned = sem("s_turned")
        s_copied = sem("s_copied")
        feat_done = sem("feat_done")
        feat_copied = sem("feat_copied")
        scol_ready = sem("scol_ready")
        head_feat_ready = sem("head_feat_ready")
        x_ready = sem("x_ready")
        z_ready = sem("z_ready")
        e_ready = sem("e_ready")
        p_ready = sem("p_ready")
        rec_ready = sem("rec_ready")
        alpha_ready = sem("alpha_ready")
        T_done = sem("T_done")
        evac_done = sem("evac_done")
        mixed = sem("mixed")
        parts_ready = sem("parts_ready")
        elu_parts = sem("elu_parts")
        hT_ready = sem("hT_ready")
        h_turned = sem("h_turned")
        x2_ready = sem("x2_ready")
        stored = sem("stored")
        moe_set = sem("moe_set")
        moe_consts = sem("moe_consts")
        MC = 7
        var2_done = sem("var2_done")
        std2_done = sem("std2_done")
        xn_ready = sem("xn_ready")
        xn_out = [sem(f"xn_out{i}") for i in range(2)]
        tile_in = [sem(f"tile_in{i}") for i in range(2)]
        pads_out = sem("pads_out")
        tile_out = [sem(f"tile_out{i}") for i in range(2)]
        gate_in = sem("gate_in")
        turned = sem("turned")
        xT_ready = sem("xT_ready")
        xT_split = sem("xT_split")
        logits_done = sem("logits_done")
        route_step = sem("route_step")
        shift_done = sem("shift_done")
        exp_done = sem("exp_done")
        sel_ready = sem("sel_ready")
        counted = sem("counted")
        entry_ready = sem("entry_ready")
        entered = sem("entered")
        tables_ready = sem("tables_ready")
        idx_copied = sem("idx_copied")
        xg_in = [sem(f"xg_in{i}") for i in range(2)]
        raw_in = sem("raw_in")
        hi_ready = sem("hi_ready")
        lo_ready = sem("lo_ready")
        up_done = sem("up_done")
        silu_done = sem("silu_done")
        hid_ready = sem("hid_ready")
        hid_turned = sem("hid_turned")
        hidT_ready = sem("hidT_ready")
        hidT_split = sem("hidT_split")
        down_done = sem("down_done")
        sum_copied = sem("sum_copied")
        y_ready = sem("y_ready")
        added = sem("added")

        sp_waited, pool_waited, dve_waited, pe_waited = [sem(f"{n}_waited") for n in ("sp", "pool", "dve", "pe")]
        block = ctx.enter_context(nc.Block())

        @block.sync
        def _(sp):
            sp.dma_start(w0_sb[:, 0, :, :], W0.rearrange("h f o -> f h o")).then_inc(w_in, 16)
            for n, a in enumerate((as0, an0, as1, an1)):
                sp.dma_start(att_bc[:, n, :], a.rearrange("h o -> (h o)").partition_broadcast(P)).then_inc(w_in, 16)
            for k in range(KC):
                sp.dma_start(w1_sb[:, k, :, :], W1[:, k * P:(k + 1) * P, :].rearrange("h f o -> f h o")).then_inc(w_in, 16)
            for n, a in enumerate((b0, b1)):
                sp.dma_start(b_col[:, n, :], a.rearrange("(j i) o -> (i o) j", i=2),
                             allow_slow_non_contiguous=True).then_inc(w_in, 16)
            for g in range(G):
                sp.dma_start(x_sb[:, NC * g:NC * (g + 1), :], x_v[:, NC * g:NC * (g + 1), :]).then_inc(x_in[g], 16)
            for u in range(SH):
                if u:
                    sp.wait_ge(raw_in, 16 * u)
                sp.dma_start(w_stage[:, u * WL:(u + 1) * WL], experts[E + u, :, :]).then_inc(raw_in, 16)
            with sp.Fori(0, G) as g:
                sp.wait_ge(feat_done, 2 * g + FREE)
                sp.dma_start(ctx_sb[:], ctxT[bass.ds(g, 1), :, :].rearrange("a f n -> f (a n)")).then_inc(ctx_in, 16)
                for l in range(2):
                    L = 2 * g + l
                    sp.wait_ge(st_copied, L + 1)
                    sp.dma_start(t_rows, st_sb[H:2 * H, :]).then_inc(t_out, 16)
                    sp.wait_ge(t_out, 16 * L + 16)
                    for i in range(2):
                        sp.dma_start(t_sb[:, i, :], t_rows[i, :].partition_broadcast(P)).then_inc(t_in[i], 16)
                    with sp.Fori(1, HP) as j:
                        for i in range(2):
                            sp.wait_ge(x_ready, R * L + NC * (2 * j + i - 1))
                            sp.dma_start(t_sb[:, i, :], t_rows[bass.ds(2 * j + i, 1), :].rearrange("a n -> (a n)").partition_broadcast(P)).then_inc(t_in[i], 16)
            sp.dma_start(gate_sb[:], gateT.rearrange("(k p) e -> p k e", p=P)).then_inc(gate_in, 16)
            sp.wait_ge(moe_consts, MC)
            sp.dma_start(xn_rows[T:T + PADS, :], zrow[:]).then_inc(pads_out, 16)
            sp.dma_start(out[T:T + PADS, :], zrow[:]).then_inc(pads_out, 16)
            with sp.Fori(0, TT // 2) as j:
                for i in range(2):
                    sp.wait_ge(xn_ready, 2 * j + i + 1)
                    sp.dma_start(xn_rows[bass.ds((2 * j + i) * P, P), :], xg[:, i, :]).then_inc(xn_out[i], 16)
            for i in range(2):
                sp.wait_ge(xn_out[i], 16 * (TT // 2 + 1))
            sp.wait_ge(turned, TT + FREE)

            def load_tile(t, i):
                sp.dma_start(xg[:, i, :], xn_rows[bass.ds(t * P, P), :]).then_inc(tile_in[i], 16)

            def load_expert(e, i, n):
                sp.wait_ge(raw_in, 16 * n)
                sp.sem_inc(sp_waited, 1)
                sp.wait_ge(lo_ready, NP_ * (n - 1))
                sp.dma_start(w_stage[:, i * WL:(i + 1) * WL],
                             experts[bass.ds(e, 1), :, :].rearrange("a p w -> p (a w)")).then_inc(raw_in, 16)

            load_tile(0, 0)
            load_tile(1, 1)
            for e in range(2):
                load_expert(e, e, SH + e)

            def store_tile(t, i):
                sp.wait_ge(y_ready, t + 1)
                sp.dma_start(out[bass.ds(t * P, P), :], y_sb[:, i, :]).then_inc(tile_out[i], 16)

            with sp.Fori(0, TT // 2 - 1) as j:
                for i in range(2):
                    sp.wait_ge(turned, TT + 2 * j + i + 1 + FREE)
                    load_tile(2 * j + i + 2, i)
                    store_tile(2 * j + i, i)
            for i in range(2):
                store_tile(TT - 2 + i, i)
            with sp.Fori(1, E // 2) as j:
                for i in range(2):
                    load_expert(2 * j + i, i, SH + 2 * j + i)

        @block.gpsimd
        def _(pool):
            nc.gpsimd.memset(ident[:], 0.0).then_inc(setup_pool, 1)
            pool.wait_ge(setup_pool, 1)
            nc.gpsimd.affine_select(out=ident[:], in_=ident[:], compare_op=ALU.not_equal, fill=1.0,
                                    base=0, pattern=[[-1, P]], channel_multiplier=1).then_inc(consts, 1)
            pool.sem_inc(T_done, RING)
            pool.sem_inc(parts_ready, FREE)
            pool.sem_inc(feat_done, FREE)
            pool.sem_inc(hT_ready, 1)

            nc.gpsimd.memset(ones[:], 1.0).then_inc(moe_set, 1)
            nc.gpsimd.memset(below[:], 1.0).then_inc(moe_set, 1)
            nc.gpsimd.memset(zrow[:], 0.0).then_inc(moe_consts, 1)
            pool.wait_ge(moe_set, 2)
            nc.gpsimd.affine_select(out=tri[:], in_=ones[:], compare_op=ALU.is_gt, fill=0.0, base=0,
                                    pattern=[[1, P]], channel_multiplier=-1).then_inc(moe_consts, 1)
            nc.gpsimd.affine_select(out=below[:], in_=below[:], compare_op=ALU.is_gt, fill=0.0, base=0,
                                    pattern=[[1, E], [-1, E]], channel_multiplier=0).then_inc(moe_consts, 1)
            exact = dict(allow_small_or_imprecise_dtypes=True)
            nc.gpsimd.iota(count[:], pattern=[[1, P]], base=0, channel_multiplier=0, **exact).then_inc(moe_consts, 1)
            nc.gpsimd.iota(count_p[:], pattern=[[P, E]], base=0, channel_multiplier=0, **exact).then_inc(moe_consts, 1)
            nc.gpsimd.iota(token[:], pattern=[[P, TT]], base=0, channel_multiplier=1, **exact).then_inc(moe_consts, 1)
            nc.gpsimd.iota(pad_row[:], pattern=[[1, 1]], base=T, channel_multiplier=1, **exact).then_inc(moe_consts, 1)
            for i in range(2):
                pool.sem_inc(tile_out[i], 16)
            pool.sem_inc(turned, FREE)
            for i in range(2):
                pool.sem_inc(xn_out[i], 16)

            def sum_step(L, j, s):
                h, c = 2 * j + s // NC, s % NC
                i, slot = (s // NC) % 2, s % RING
                if c == 0:
                    pool.wait_ge(t_in[i], 16 * (HP * L + j + s // RING + 1))
                    pool.wait_ge(scol_ready, H * L + h + 1)
                pool.wait_ge(T_done, R * L + RING * j + s + 1)
                pool.sem_inc(pool_waited, 1)
                nc.gpsimd.tensor_scalar(ring[:, slot, :], t_sb[:, i, :], scol[:, i, c:c + 1], 1.0,
                                        ALU.add, ALU.mult).then_inc(x_ready, 1)

            def head_pair(L, j, last):
                for s in range(RING):
                    if not (last and s + AHEAD_X >= RING):
                        sum_step(L, j, s + AHEAD_X)
                    if s % 2 == 0:
                        pool.wait_ge(rec_ready, R // 2 * L + HP * j + s // 2 + 1)
                        pool.sem_inc(pool_waited, 1)
                    nc.gpsimd.tensor_scalar(ring[:, s, :], ring[:, s, :], rec[:, s:s + 1], 1.0,
                                            ALU.mult, ALU.mult).then_inc(alpha_ready, 1)

            with pool.Fori(0, G) as g:
                for l in range(2):
                    L = 2 * g + l
                    for s in range(AHEAD_X):
                        sum_step(L, 0, s)
                    with pool.Fori(0, HP - 1) as j:
                        head_pair(L, j, False)
                    head_pair(L, HP - 1, True)

            pool.wait_ge(x2_ready, G * HP)
            for u in range(SH):
                for n, (a, b) in enumerate(PIECES):
                    pool.wait_ge(hi_ready, NP_ * u + n + 1)
                    hi, lo = 2 * u * WL, (2 * u + 1) * WL
                    nc.gpsimd.tensor_tensor(split[:, lo + a:lo + b], w_stage[:, u * WL + a:u * WL + b],
                                            split[:, hi + a:hi + b].bitcast(f32), ALU.subtract).then_inc(lo_ready, 1)

            def shared_gate(s):
                pool.wait_ge(silu_done, s + 1)
                nc.gpsimd.tensor_tensor(hid[:], sg[:], up_sb, ALU.mult).then_inc(hid_ready, 1)

            def shared_x_low(t, i):
                pool.wait_ge(xT_ready, TT + t + 1)
                nc.gpsimd.tensor_tensor(xT_lo[:, i, :, :], xT_sb, xT_hi[:, i, :, :].bitcast(f32), ALU.subtract).then_inc(xT_split, 1)

            def shared_hidden_low(s):
                pool.wait_ge(hidT_ready, s + 1)
                nc.gpsimd.tensor_tensor(hidT_lo[:, 0:DC - 1, :], hidT[:, 0:DC - 1, :], hidT_hi[:, 0:DC - 1, :].bitcast(f32), ALU.subtract)
                nc.gpsimd.tensor_tensor(hidT_lo[0:LASTD, DC - 1, :], hidT[0:LASTD, DC - 1, :],
                                        hidT_hi[0:LASTD, DC - 1, :].bitcast(f32), ALU.subtract).then_inc(hidT_split, 1)

            def shared_add(t, i, nth):
                pool.wait_ge(sum_copied, t + 1)
                pool.wait_ge(tile_out[i], 16 * nth + 16)
                pool.sem_inc(pool_waited, 1)
                nc.gpsimd.tensor_tensor(y_sb[:, i, :], sum_sb[:], x_sb[:, bass.ds(t, 1), :].rearrange("p a d -> p (a d)"),
                                        ALU.add).then_inc(y_ready, 1)

            def shared_tile(t, i, nth, first=False):
                shared_gate(2 * t)
                shared_hidden_low(2 * t)
                if not first:
                    shared_add(t - 1, 1 - i, nth)
                shared_gate(2 * t + 1)
                shared_x_low(t + 1, 1 - i)
                shared_hidden_low(2 * t + 1)

            def gather(r, i, copies):
                pool.wait_ge(turned, 2 * TT + r - 1 + FREE)
                nc.gpsimd.tensor_copy(gidx[:, i:i + 1], idx_tab[:, bass.ds(r, 1)]).then_inc(idx_copied, 1)
                pool.wait_ge(idx_copied, copies)
                pool.sem_inc(pool_waited, 1)
                nc.gpsimd.indirect_dma_start(xg[:, i, :], None, xn_rows, bass.IndirectOffsetOnAxis(ap=gidx[:, i:i + 1], axis=0),
                                             bounds_check=T + PADS - 1, oob_is_err=True).then_inc(xg_in[i], 16)

            def scatter(r, i, copies, first=False):
                nc.gpsimd.tensor_copy(sidx[:, i:i + 1], idx_tab[:, bass.ds(r, 1)]).then_inc(idx_copied, 1)
                if not first:
                    pool.wait_ge(added, 16 * r)
                pool.wait_ge(idx_copied, copies)
                pool.wait_ge(y_ready, TT + r + 1)
                pool.sem_inc(pool_waited, 1)
                nc.gpsimd.indirect_dma_start(out, bass.IndirectOffsetOnAxis(ap=sidx[:, i:i + 1], axis=0), y_sb[:, i, :], None,
                                             bounds_check=T + PADS - 1, oob_is_err=True, compute_op=ALU.add).then_inc(added, 16)

            shared_x_low(0, 0)
            shared_tile(0, 0, 0, first=True)
            with pool.Fori(0, TT // 2 - 1) as j:
                shared_tile(2 * j + 1, 1, j)
                shared_tile(2 * j + 2, 0, j)
            pool.wait_ge(pads_out, 32)
            pool.wait_ge(tables_ready, 1)
            gather(0, 0, 1)
            shared_gate(SS - 2)
            shared_hidden_low(SS - 2)
            shared_add(TT - 2, 0, TT // 2 - 1)
            gather(1, 1, 2)
            shared_gate(SS - 1)
            shared_hidden_low(SS - 1)
            gather(2, 0, 3)
            for i in range(2):
                pool.wait_ge(tile_out[i], 16 * (TT // 2 + 1))

            gather(3, 1, 4)
            scatter(0, 0, 5, first=True)
            gather(4, 0, 6)
            scatter(1, 1, 7)
            with pool.Fori(1, (RS - 5) // 2) as j:
                for i in range(2):
                    r = 2 * j + i
                    gather(r + 3, 1 - i, 2 * r + 4)
                    scatter(r, i, 2 * r + 5)
            for r in range(RS - 5, RS):
                if r + 3 < RS:
                    gather(r + 3, (r + 3) % 2, 2 * r + 4)
                scatter(r, r % 2, min(2 * r + 5, r + RS + 1))
            pool.wait_ge(added, 16 * RS)

        @block.scalar
        def _(act):
            act.wait_ge(wa_ready, 1)
            act.wait_ge(var_done, 1)
            nc.scalar.activation(rstd[:], rstd[:], ACT.Sqrt).then_inc(std_done, 1)

            def exp_step(L, r, slot):
                act.wait_ge(e_ready, R * L + r + 1)
                nc.scalar.activation(ring[:, slot, :], ring[:, slot, :], ACT.Exp, bias=mx[:, slot:slot + 1], scale=-1.0,
                                     accum_out=rsum[:, slot:slot + 1]).then_inc(p_ready, 1)

            def elu_parts_step(L, l, j, i):
                half = slice(O * i, O * i + O)
                act.wait_ge(mixed, H * L + 2 * j + i + 1)
                if i == 0:
                    act.wait_ge(hT_ready, HP * L + j + 1)
                nc.scalar.activation(pos[half, :], o_ps[half, i, :], ACT.Relu, bias=b_col[half, l, bass.ds(j, 1)])
                nc.scalar.activation(neg[half, :], o_ps[half, i, :], ACT.Relu, scale=-1.0,
                                     bias=b_neg[half, l, bass.ds(j, 1)]).then_inc(parts_ready, 1)
                if i == 1:
                    act.wait_ge(parts_ready, H * L + 2 * j + 2 + FREE)
                    nc.scalar.activation(neg[:], neg[:], ACT.Exp, scale=-1.0).then_inc(elu_parts, 1)

            def head_pair(L, l, j, first, last):
                for s in range(RING):
                    r = RING * j + s
                    act.wait_ge(T_done, R * L + r + 1 + RING)
                    c = s % NC
                    nc.scalar.activation(eT[:, s // NC, :, c * P:(c + 1) * P], tr_ps[:, s % 2, :, :], ACT.Copy).then_inc(evac_done, 1)
                    if c == 0 and not first:
                        elu_parts_step(L, l, j - 1, s // NC)
                    if not (last and s + AHEAD_E >= RING):
                        exp_step(L, r + AHEAD_E, (s + AHEAD_E) % RING)

            with act.Fori(0, G) as g:
                for l in range(2):
                    L = 2 * g + l
                    for s in range(AHEAD_E):
                        exp_step(L, s, s)
                    head_pair(L, l, 0, True, False)
                    with act.Fori(1, HP - 1) as j:
                        head_pair(L, l, j, False, False)
                    head_pair(L, l, HP - 1, False, True)
                    elu_parts_step(L, l, HP - 1, 0)
                    elu_parts_step(L, l, HP - 1, 1)

            act.wait_ge(var2_done, 1)
            nc.scalar.activation(rstd[:], rstd[:], ACT.Sqrt).then_inc(std2_done, 1)

            def copy_turned(n, i):
                act.wait_ge(turned, n + 1 + FREE)
                nc.scalar.activation(xT[i], tr_ps[:, i, :, :], ACT.Copy).then_inc(xT_ready, 1)

            for u in range(SH):
                act.wait_ge(raw_in, 16 * (u + 1))
                for a, b in PIECES:
                    nc.scalar.activation(split[:, 2 * u * WL + a:2 * u * WL + b], w_stage[:, u * WL + a:u * WL + b], ACT.Copy).then_inc(hi_ready, 1)
                with act.Fori(0, TT // 4) as j:
                    for i in range(2):
                        copy_turned(u * (TT // 2) + 2 * j + i, i)
            act.wait_ge(shift_done, 1)
            nc.scalar.activation(score[:], score[:], ACT.Exp).then_inc(exp_done, 1)

            def split_high(i, p):
                a, b = PIECES[p]
                nc.scalar.activation(split[:, bass.ds(i * 2 * WL + a, b - a)], w_stage[:, bass.ds(i * WL + a, b - a)], ACT.Copy).then_inc(hi_ready, 1)

            def silu(s):
                act.wait_ge(up_done, s + 1)
                nc.scalar.activation(sg[:], o_ps[:, 0, 0:I], ACT.Silu).then_inc(silu_done, 1)

            def x_high(n, i):
                act.wait_ge(turned, TT + n + 1 + FREE)
                nc.scalar.activation(xT_hi[:, i, :, :], tr_ps[:, i, :, :], ACT.Copy).then_inc(xT_ready, 1)

            def hidden_high(s):
                act.wait_ge(hid_turned, s + 1)
                nc.scalar.activation(hidT_hi[:, 0:DC - 1, :], hidden_ps(0, DC - 1), ACT.Copy)
                nc.scalar.activation(hidT_hi[0:LASTD, DC - 1, :], f_ps[0:LASTD, 0, (DC - 1) * P:DC * P], ACT.Copy).then_inc(hidT_ready, 1)

            def shared_silu(s):
                act.wait_ge(up_done, s + 1)
                nc.scalar.activation(sg[:], o_ps[:, 0, 0:I], ACT.Silu)
                nc.scalar.activation(up_sb, o_ps[:, 1, 0:I], ACT.Copy).then_inc(silu_done, 1)

            def shared_x(t, i):
                act.wait_ge(turned, TT + t + 1 + FREE)
                nc.scalar.activation(xT_sb, tr_ps[:, i, :, :], ACT.Copy)
                nc.scalar.activation(xT_hi[:, i, :, :], tr_ps[:, i, :, :], ACT.Copy).then_inc(xT_ready, 1)

            def shared_hidden(s):
                act.wait_ge(hid_turned, s + 1)
                for out_, in_ in ((hidT, hidden_ps), (hidT_hi, hidden_ps)):
                    nc.scalar.activation(out_[:, 0:DC - 1, :], in_(0, DC - 1), ACT.Copy)
                    last = nc.scalar.activation(out_[0:LASTD, DC - 1, :], in_(DC - 1, DC)[0:LASTD].rearrange("p c q -> p (c q)"), ACT.Copy)
                last.then_inc(hidT_ready, 1)

            def shared_sum(t, first=False):
                act.wait_ge(down_done, SH * (t + 1))
                if not first:
                    act.wait_ge(y_ready, t)
                nc.scalar.activation(sum_sb[:], f_ps[:, 2, :], ACT.Copy).then_inc(sum_copied, 1)

            def shared_tile(t, i, first=False):
                shared_silu(2 * t)
                shared_hidden(2 * t)
                if not isinstance(t, int) or t > 0:
                    shared_sum(t - 1, first)
                shared_silu(2 * t + 1)
                shared_x(t + 1, 1 - i)
                shared_hidden(2 * t + 1)

            shared_x(0, 0)
            shared_tile(0, 0)
            shared_tile(1, 1, first=True)
            shared_tile(2, 0)
            with act.Fori(1, TT // 2 - 1) as j:
                shared_tile(2 * j + 1, 1)
                shared_tile(2 * j + 2, 0)
            shared_silu(SS - 2)
            shared_hidden(SS - 2)
            act.wait_ge(raw_in, 16 * (SH + 1))
            split_high(0, 0)
            shared_sum(TT - 2)
            shared_silu(SS - 1)
            split_high(0, 1)
            x_high(TT, 0)
            shared_hidden(SS - 1)
            act.wait_ge(down_done, SS - 1)
            split_high(0, 2)

            def slot(r, i, last=False):
                if last:
                    silu(SS + r)
                    hidden_high(SS + r)
                    return
                new = act.value_load(ctl[0:1, 2, bass.ds(r, 1)], min_val=0, max_val=1)
                with act.If(new):
                    expert = act.value_load(ctl[0:1, 0, bass.ds(r, 1)], min_val=0, max_val=E - 1)
                    half = expert % 2
                    silu(SS + r)
                    act.wait_ge(raw_in, 16 * (SH + expert + 2))
                    x_high(TT + r + 1, 1 - i)
                    split_high(1 - half, 0)
                    hidden_high(SS + r)
                    split_high(1 - half, 1)
                    act.wait_ge(down_done, SS + r)
                    split_high(1 - half, 2)
                with act.Else():
                    silu(SS + r)
                    x_high(TT + r + 1, 1 - i)
                    hidden_high(SS + r)

            with act.Fori(0, (RS - 1) // 2) as j:
                slot(2 * j, 0)
                slot(2 * j + 1, 1)
            slot(RS - 1, 0, last=True)

        @block.vector
        def _(dve):
            made = [0]

            def then(ins):
                made[0] += 1
                ins.then_inc(setup_dve, 1)
                dve.wait_ge(setup_dve, made[0])

            dve.wait_ge(w_in, 16 * (1 + KC + 6))
            for l, w in ((0, w0_sb), (1, w1_sb)):
                for k in range(w.shape[1]):
                    for n in range(2):
                        then(nc.vector.tensor_tensor(prod[:], w[:, k, :, :].rearrange("p h o -> p (h o)"),
                                                     att_bc[:, 2 * l + n, :], ALU.mult))
                        then(nc.vector.tensor_reduce(out=wa[:, l + k, n * H:(n + 1) * H],
                                                     in_=prod[:].rearrange("p (h o) -> p h o", h=H),
                                                     op=ALU.add, axis=AX.X, negate=True))
            nc.vector.tensor_scalar(b_neg[:], b_col[:], -1.0, None, ALU.mult).then_inc(wa_ready, 1)
            for t in range(TT):
                if t % NC == 0:
                    dve.wait_ge(x_in[t // NC], 16)
                last = nc.vector.bn_stats(stats[:, t, :], x_sb[:, t, :])
            then(last)
            for t in range(TT):
                last = nc.vector.bn_aggr(mv[:, t, :], stats[:, t, :])
            then(last)
            nc.vector.tensor_scalar(rstd[:], mv[:, :, 1], EPS, None, ALU.add).then_inc(var_done, 1)
            dve.wait_ge(std_done, 1)
            then(nc.vector.reciprocal(rstd[:], rstd[:]))

            def score_step(L, j, k):
                s = 2 * k
                dve.wait_ge(x_ready, R * L + RING * j + s + 2)
                nc.vector.scalar_tensor_tensor(ring[:, s:s + 2, :], ring[:, s:s + 2, :], SLOPE,
                                               ring[:, s:s + 2, :], ALU.mult, ALU.min).then_inc(z_ready, 1)
                dve.wait_ge(z_ready, R // 2 * L + HP * j + k + 1)
                dve.sem_inc(dve_waited, 1)
                for m in range(2):
                    nc.vector.tensor_tensor_reduce(
                        out=ring[:, s + m, :], in0=ring[:, s + m, :], in1=nmask[:, (s + m) % NC, :],
                        scale=1.0, scalar=3.0e38, op0=ALU.add, op1=ALU.min,
                        accum_out=mx[:, s + m:s + m + 1]).then_inc(e_ready, 1)

            def reciprocal_step(L, j, k):
                s = (2 * k) % RING
                dve.wait_ge(p_ready, R * L + RING * j + 2 * k + 2)
                nc.vector.reciprocal(rec[:, s:s + 2], rsum[:, s:s + 2]).then_inc(rec_ready, 1)

            def column_step(h, i):
                nc.vector.tensor_copy(scol[:, i, :], negs[:, :, bass.ds(h, 1)].rearrange("p c a -> p (c a)")).then_inc(scol_ready, 1)

            def weight_step(L, h, i):
                dve.wait_ge(parts_ready, H * L + h - 1 + FREE)
                nc.vector.tensor_copy(head_feat[:, i, :, :], feat[:, :, bass.ds(O * h, O)]).then_inc(head_feat_ready, 1)

            def elu_step(L, j):
                dve.wait_ge(elu_parts, HP * L + j + 1)
                nc.vector.scalar_tensor_tensor(hT[:, bass.ds(j, 1), :].rearrange("p a n -> p (a n)"), neg[:], -1.0, pos[:],
                                               ALU.add, ALU.add).then_inc(hT_ready, 1)

            def head_pair(L, j, first, last):
                for k in range(1, HP):
                    score_step(L, j, k)
                    reciprocal_step(L, j, k - 1)
                    if k % 2 == 1 and not last:
                        column_step(2 * j + k // 2 + 2, k // 2)
                    if k == 1 and not first:
                        weight_step(L, 2 * j - 1, 1)
                    if k == 3:
                        weight_step(L, 2 * j, 0)
                if not last:
                    score_step(L, j + 1, 0)
                reciprocal_step(L, j, HP - 1)
                if not first:
                    elu_step(L, j - 1)

            with dve.Fori(0, G) as g:
                for c in range(NC):
                    t = NC * g + c
                    nc.vector.tensor_scalar(nmask[:, c, :], x_sb[:, bass.ds(t, 1), :].rearrange("p a d -> p (a d)"),
                                            mv[:, bass.ds(t, 1), 0:1].rearrange("p a d -> p (a d)"),
                                            rstd[:, bass.ds(t, 1)], ALU.subtract, ALU.mult).then_inc(mask_step, 1)
                for c in range(NC):
                    dve.wait_ge(mask_step, 2 * NC * g + c + 1)
                    nc.vector.tensor_scalar(nmask[:, c, :], nmask[:, c, :], -1.0, -MASK, ALU.add, ALU.mult).then_inc(mask_step, 1)
                for l in range(2):
                    L = 2 * g + l
                    dve.wait_ge(st_done, L + 1)
                    nc.vector.tensor_copy(st_sb[:], o_ps[0:2 * H, 0, :]).then_inc(st_copied, 1)
                    dve.wait_ge(s_turned, L + 1)
                    nc.vector.tensor_copy(negs[:], o_ps[:, 1, 0:NC * 2 * H].rearrange("p (c h) -> p c h", c=NC)[:, :, 0:H]).then_inc(s_copied, 1)
                    dve.wait_ge(s_copied, L + 1)
                    for i in range(2):
                        column_step(i, i)
                    dve.wait_ge(feat_done, L + 1 + FREE)
                    nc.vector.tensor_copy(feat[:], f_ps[:]).then_inc(feat_copied, 1)
                    dve.wait_ge(feat_copied, L + 1)
                    score_step(L, 0, 0)
                    head_pair(L, 0, True, False)
                    with dve.Fori(1, HP - 1) as j:
                        head_pair(L, j, False, False)
                    head_pair(L, HP - 1, False, True)
                    weight_step(L, H - 1, 1)
                    elu_step(L, HP - 1)
                for j in range(HP):
                    dve.wait_ge(h_turned, HP * g + j + 1)
                    xt = x_sb[:, bass.ds(NC * g, NC), j * P:(j + 1) * P]
                    nc.vector.tensor_tensor(xt, xt, f_ps[:, j, :].rearrange("p (c q) -> p c q", c=NC), ALU.add).then_inc(x2_ready, 1)

            steps = [0]

            def step(ins):
                steps[0] += 1
                ins.then_inc(route_step, 1)
                return steps[0]

            def after(n):
                dve.wait_ge(route_step, n)

            def wide(ap, n):
                return ap.unsqueeze(len(ap.shape)).to_broadcast(list(ap.shape) + [n])

            dve.wait_ge(x2_ready, G * HP)
            for t in range(TT):
                n = step(nc.vector.bn_stats(stats[:, t, :], x_sb[:, t, :]))
            after(n)
            for t in range(TT):
                n = step(nc.vector.bn_aggr(mv[:, t, :], stats[:, t, :]))
            after(n)
            nc.vector.tensor_scalar(rstd[:], mv[:, :, 1], EPS, None, ALU.add).then_inc(var2_done, 1)
            dve.wait_ge(std2_done, 1)
            after(step(nc.vector.reciprocal(rstd[:], rstd[:])))
            with dve.Fori(0, TT // 2) as j:
                for i in range(2):
                    t = 2 * j + i
                    dve.wait_ge(turned, t - 1 + FREE)
                    dve.wait_ge(xn_out[i], 16 * j + 16)
                    nc.vector.tensor_scalar(xg[:, i, :], x_sb[:, bass.ds(t, 1), :].rearrange("p a d -> p (a d)"),
                                            mv[:, bass.ds(t, 1), 0:1].rearrange("p a d -> p (a d)"),
                                            rstd[:, bass.ds(t, 1)], ALU.subtract, ALU.mult).then_inc(xn_ready, 1)

            dve.wait_ge(moe_consts, MC)
            dve.wait_ge(logits_done, TT)
            logits = f_ps[:, 3, 0:TT * E].rearrange("p (t e) -> p t e", e=E)
            after(step(nc.vector.tensor_reduce(out=rmax[:], in_=logits, op=ALU.max, axis=AX.X)))
            nc.vector.tensor_tensor(score[:], logits, wide(rmax[:], E), ALU.subtract).then_inc(shift_done, 1)
            dve.wait_ge(exp_done, 1)
            after(step(nc.vector.tensor_reduce(out=rtot[:], in_=score[:], op=ALU.add, axis=AX.X)))
            after(step(nc.vector.reciprocal(rtot[:], rtot[:])))
            after(step(nc.vector.tensor_tensor(score[:], score[:], wide(rtot[:], E), ALU.mult)))

            def ranks(out_, in_, scratch, n):
                last = step(nc.vector.memset(out_, 0.0))
                for f in range(n):
                    step(nc.vector.tensor_tensor(scratch[:, :, 0:f + 1], wide(in_[:, :, f], f + 1), in_[:, :, 0:f + 1], ALU.is_gt))
                    if f + 1 < n:
                        step(nc.vector.tensor_tensor(scratch[:, :, f + 1:n], wide(in_[:, :, f], n - f - 1), in_[:, :, f + 1:n], ALU.is_ge))
                    after(steps[0])
                    last = step(nc.vector.tensor_tensor(out_, out_, scratch, ALU.add))
                    after(last)

            after(step(nc.vector.tensor_reduce(out=gtop[:], in_=score[:].rearrange("p t (g e) -> p t g e", g=NGR), op=ALU.max, axis=AX.X)))
            ranks(grank[:], gtop[:], gcmp[:], NGR)
            after(step(nc.vector.tensor_scalar(grank[:], grank[:], float(TOPG), None, ALU.is_lt)))
            after(step(nc.vector.tensor_tensor(score[:].rearrange("p t (g e) -> p (t g) e", g=NGR),
                                               score[:].rearrange("p t (g e) -> p (t g) e", g=NGR),
                                               wide(grank[:].rearrange("p t g -> p (t g)"), EG), ALU.mult)))
            ranks(rank[:], score[:], cmp[:], E)
            nc.vector.tensor_scalar(sel[:], rank[:], float(TOPK), None, ALU.is_lt).then_inc(sel_ready, 1)
            dve.wait_ge(sel_ready, 1)
            after(step(nc.vector.tensor_tensor(comb[:], score[:], sel[:], ALU.mult)))
            after(step(nc.vector.tensor_reduce(out=rtot[:], in_=comb[:], op=ALU.add, axis=AX.X)))
            after(step(nc.vector.tensor_scalar(rtot[:], rtot[:], 1e-20, None, ALU.add)))
            after(step(nc.vector.reciprocal(rtot[:], rtot[:])))
            after(step(nc.vector.tensor_tensor(comb[:], comb[:], wide(rtot[:], E), ALU.mult)))

            dve.wait_ge(counted, 1)
            after(step(nc.vector.tensor_copy(load[:], f_ps[:, 1, 0:E])))
            after(step(nc.vector.tensor_tensor(sq[:], wide(load[:], E), count_p[:].unsqueeze(1).to_broadcast([P, E, E]), ALU.is_gt)))
            after(step(nc.vector.tensor_reduce(out=tiles[:], in_=sq[:], op=ALU.add, axis=AX.X)))
            after(step(nc.vector.tensor_scalar(tiles[:], tiles[:], 1.0, None, ALU.max)))
            after(step(nc.vector.tensor_tensor(sq[:], below[:], tiles[:].unsqueeze(1).to_broadcast([P, E, E]), ALU.mult)))
            after(step(nc.vector.tensor_reduce(out=first[:], in_=sq[:], op=ALU.add, axis=AX.X)))
            after(step(nc.vector.tensor_scalar(first_row[:], first[:], float(P), None, ALU.mult)))
            after(step(nc.vector.tensor_tensor(place[:], f_ps[:, 3, 0:TT * E].rearrange("p (t e) -> p t e", e=E),
                                               first_row[:].unsqueeze(1).to_broadcast([P, TT, E]), ALU.add)))
            for k in range(TOPK):
                after(step(nc.vector.tensor_scalar(eq[:], rank[:], float(k), None, ALU.is_equal)))
                step(nc.vector.tensor_tensor(cmp[:], eq[:], place[:], ALU.mult))
                after(step(nc.vector.tensor_tensor(sel[:], eq[:], comb[:], ALU.mult)))
                step(nc.vector.tensor_reduce(out=place_k[:, :, k], in_=cmp[:], op=ALU.add, axis=AX.X))
                after(step(nc.vector.tensor_reduce(out=w_k[:, :, k], in_=sel[:], op=ALU.add, axis=AX.X)))
            after(step(nc.vector.tensor_copy(place_i[:], place_k[:])))
            step(nc.vector.tensor_scalar(slot_i[:], place_i[:], 7, None, ALU.logical_shift_right))
            after(step(nc.vector.tensor_scalar(row_i[:], place_i[:], P - 1, None, ALU.bitwise_and)))
            step(nc.vector.tensor_copy(slot_f[:], slot_i[:]))
            after(step(nc.vector.tensor_copy(row_f[:], row_i[:])))
            after(step(nc.vector.tensor_tensor(tok_k[:], wide(token[:], TOPK), row_f[:], ALU.subtract)))
            after(step(nc.vector.tensor_scalar(tok_k[:], tok_k[:], float(-T), None, ALU.add)))
            for t in range(TT):
                i = t % 2
                if t >= 2:
                    dve.wait_ge(entered, t - 1)
                step(nc.vector.tensor_tensor(row_hot[:, i, :, :], count[:].unsqueeze(1).to_broadcast([P, TOPK, P]),
                                             wide(row_f[:, t, :], P), ALU.is_equal))
                after(step(nc.vector.tensor_tensor(slot_hot[:, i, :, :], count[:, 0:RS].unsqueeze(1).to_broadcast([P, TOPK, RS]),
                                                   wide(slot_f[:, t, :], RS), ALU.is_equal)))
                step(nc.vector.tensor_tensor(entry[:, i, :, 0, :], slot_hot[:, i, :, :], wide(tok_k[:, t, :], RS), ALU.mult))
                after(steps[0])
                nc.vector.tensor_tensor(entry[:, i, :, 1, :], slot_hot[:, i, :, :], wide(w_k[:, t, :], RS), ALU.mult).then_inc(entry_ready, 1)

            after(step(nc.vector.tensor_tensor(owner[:], wide(count[0:1, 0:RS], E), first[0:1, :].unsqueeze(1).to_broadcast([1, RS, E]), ALU.is_ge)))
            after(step(nc.vector.tensor_reduce(out=prior[:], in_=owner[:], op=ALU.add, axis=AX.X)))
            after(step(nc.vector.tensor_scalar(ctl_f[0:1, 0, :], prior[:], -1.0, None, ALU.add)))
            step(nc.vector.memset(ctl_f[0:1, 2, 0:1], 1.0))
            after(step(nc.vector.tensor_tensor(ctl_f[0:1, 2, 1:RS], ctl_f[0:1, 0, 1:RS], ctl_f[0:1, 0, 0:RS - 1], ALU.not_equal)))
            after(step(nc.vector.tensor_scalar(prior[:], ctl_f[0:1, 0, :], float(E - 1), None, ALU.is_lt)))
            step(nc.vector.tensor_tensor(ctl_f[0:1, 2, :], ctl_f[0:1, 2, :], prior[:], ALU.mult))
            after(step(nc.vector.tensor_copy(ctl[0:1, 0, :], ctl_f[0:1, 0, :])))
            step(nc.vector.tensor_copy(ctl[0:1, 2, :], ctl_f[0:1, 2, :]))
            after(step(nc.vector.tensor_scalar(ctl[0:1, 1, :], ctl[0:1, 0, :], 1, None, ALU.bitwise_and)))
            dve.wait_ge(entered, TT)
            after(step(nc.vector.tensor_scalar(idx_f[:], f_ps[:, 1, 0:RS], pad_row[:, 0:1], None, ALU.add)))
            step(nc.vector.tensor_copy(w_tab[:], f_ps[:, 1, RS:2 * RS]))
            after(steps[0])
            nc.vector.tensor_copy(idx_tab[:], idx_f[:]).then_inc(tables_ready, 1)
            dve.wait_ge(tables_ready, 1)

            def split_low(i, p, count_before):
                a, b = PIECES[p]
                dve.wait_ge(hi_ready, count_before + p + 1)
                nc.vector.tensor_tensor(split[:, bass.ds((i * 2 + 1) * WL + a, b - a)], w_stage[:, bass.ds(i * WL + a, b - a)],
                                        split[:, bass.ds(i * 2 * WL + a, b - a)].bitcast(f32), ALU.subtract).then_inc(lo_ready, 1)

            def gate(r):
                dve.wait_ge(silu_done, SS + r + 1)
                nc.vector.tensor_tensor(hid[:], sg[:], o_ps[:, 1, 0:I], ALU.mult).then_inc(hid_ready, 1)

            def x_low(r, i):
                dve.wait_ge(xT_ready, 2 * TT + r + 1)
                nc.vector.tensor_tensor(xT_lo[:, i, :, :], tr_ps[:, i, :, :], xT_hi[:, i, :, :].bitcast(f32), ALU.subtract).then_inc(xT_split, 1)

            def hidden_low(r):
                dve.wait_ge(hidT_ready, SS + r + 1)
                nc.vector.tensor_tensor(hidT_lo[:, 0:DC - 1, :], hidden_ps(0, DC - 1), hidT_hi[:, 0:DC - 1, :].bitcast(f32), ALU.subtract)
                nc.vector.tensor_tensor(hidT_lo[0:LASTD, DC - 1, :], f_ps[0:LASTD, 0, (DC - 1) * P:DC * P],
                                        hidT_hi[0:LASTD, DC - 1, :].bitcast(f32), ALU.subtract).then_inc(hidT_split, 1)

            def weigh(r, i, first=False):
                dve.wait_ge(down_done, SS + r + 1)
                if first:
                    dve.wait_ge(tile_out[i], 16 * (TT // 2 + 1))
                else:
                    dve.wait_ge(added, 16 * r - 16)
                nc.vector.tensor_scalar(y_sb[:, i, :], f_ps[:, 2, :], w_tab[:, bass.ds(r, 1)], None, ALU.mult).then_inc(y_ready, 1)

            def shared_add_last():
                dve.wait_ge(down_done, SS)
                dve.wait_ge(tile_out[1], 16 * (TT // 2))
                nc.vector.tensor_tensor(y_sb[:, 1, :], f_ps[:, 2, :], x_sb[:, TT - 1, :], ALU.add).then_inc(y_ready, 1)

            def slot(r, i, first=False, last=False):
                def weigh_before():
                    if first and i == 0:
                        shared_add_last()
                    else:
                        weigh(r - 1, 1 - i, first=first)

                if last:
                    gate(r)
                    weigh_before()
                    hidden_low(r)
                    return
                new = dve.value_load(ctl[0:1, 2, bass.ds(r, 1)], min_val=0, max_val=1)
                with dve.If(new):
                    expert = dve.value_load(ctl[0:1, 0, bass.ds(r, 1)], min_val=0, max_val=E - 1)
                    half = expert % 2
                    pieces = NP_ * SH + NP_ * (expert + 1)
                    gate(r)
                    x_low(r + 1, 1 - i)
                    split_low(1 - half, 0, pieces)
                    hidden_low(r)
                    weigh_before()
                    split_low(1 - half, 1, pieces)
                    split_low(1 - half, 2, pieces)
                with dve.Else():
                    gate(r)
                    x_low(r + 1, 1 - i)
                    weigh_before()
                    hidden_low(r)

            split_low(0, 0, NP_ * SH)
            split_low(0, 1, NP_ * SH)
            x_low(0, 0)
            split_low(0, 2, NP_ * SH)
            slot(0, 0, first=True)
            slot(1, 1, first=True)
            with dve.Fori(1, (RS - 1) // 2) as j:
                slot(2 * j, 0)
                slot(2 * j + 1, 1)
            slot(RS - 1, 0, last=True)
            weigh(RS - 1, 0)

        @block.tensor
        def _(pe):
            pe.wait_ge(consts, 1)
            pe.wait_ge(w_in, 16 * (1 + KC + 6))
            pe.wait_ge(wa_ready, 1)

            def transpose_step(L, j, s, wait_copy=True):
                r = RING * j + s
                pe.wait_ge(alpha_ready, R * L + r + 1)
                if wait_copy:
                    pe.wait_ge(evac_done, R * L + r - 1)
                for m in range(NC):
                    last = nc.tensor.transpose(tr_ps[:, s % 2, m, :], ring[:, s % RING, m * P:(m + 1) * P], ident[:])
                last.then_inc(T_done, 1)

            def mix_step(L, h, i, m):
                if m == 0:
                    pe.wait_ge(evac_done, R * L + NC * h + NC)
                    pe.wait_ge(head_feat_ready, H * L + h + 1)
                    pe.wait_ge(parts_ready, H * L + h - 1 + FREE)
                done = nc.tensor.matmul(o_ps[O * i:O * i + O, i, :], head_feat[:, i, m, :], eT[:, i, m, :],
                                        start=(m == 0), stop=(m == NC - 1))
                if m == NC - 1:
                    done.then_inc(mixed, 1)

            def head_pair(L, j, last):
                for s in range(RING):
                    if not (last and s + NC >= RING):
                        transpose_step(L, j, s + NC)
                    mix_step(L, 2 * j + s // NC, s // NC, s % NC)

            with pe.Fori(0, G) as g:
                for l in range(2):
                    L = 2 * g + l
                    w = w0_sb if l == 0 else w1_sb
                    K = 1 if l == 0 else KC

                    def lhs(k):
                        return ctx_sb[:] if l == 0 else hT[:, k, :]

                    if l == 0:
                        pe.wait_ge(ctx_in, 16 * g + 16)
                    else:
                        for k in range(K - 1):
                            pe.wait_ge(hT_ready, HP * (L - 1) + k + 2)
                            for c in range(NC):
                                nc.tensor.matmul(f_ps[:, c, :], lhs(k)[:, c * P:(c + 1) * P],
                                                 w[:, k, :, :].rearrange("p h o -> p (h o)"), start=(k == 0), stop=False)
                        pe.wait_ge(hT_ready, HP * (L - 1) + K + 1)
                    for k in range(K):
                        last = nc.tensor.matmul(o_ps[0:2 * H, 0, :], wa[:, l + k, :], lhs(k), start=(k == 0), stop=(k == K - 1))
                    last.then_inc(st_done, 1)
                    for c in range(NC):
                        last = nc.tensor.matmul(f_ps[:, c, :], lhs(K - 1)[:, c * P:(c + 1) * P],
                                                w[:, K - 1, :, :].rearrange("p h o -> p (h o)"), start=(K == 1), stop=True)
                    last.then_inc(feat_done, 1)
                    pe.wait_ge(st_copied, L + 1)
                    pe.sem_inc(pe_waited, 1)
                    for c in range(NC):
                        last = nc.tensor.transpose(o_ps[:, 1, c * 2 * H:(c + 1) * 2 * H], st_sb[:, c * P:(c + 1) * P], ident[0:2 * H, 0:2 * H])
                    last.then_inc(s_turned, 1)
                    for s in range(NC):
                        transpose_step(L, 0, s, wait_copy=s >= 2)
                    with pe.Fori(0, HP - 1) as j:
                        head_pair(L, j, False)
                    head_pair(L, HP - 1, True)
                for j in range(HP):
                    pe.wait_ge(hT_ready, HP * (2 * g + 1) + j + 2)
                    for c in range(NC):
                        last = nc.tensor.transpose(f_ps[:, j, c * P:(c + 1) * P], hT[:, j, c * P:(c + 1) * P], ident[:])
                    last.then_inc(h_turned, 1)
                pe.wait_ge(x2_ready, HP * (g + 1))

            pe.wait_ge(gate_in, 16)
            with pe.Fori(0, TT // 2) as j:
                for i in range(2):
                    pe.wait_ge(xn_ready, 2 * j + i + 1)
                    for k in range(KC):
                        last = nc.tensor.transpose(tr_ps[:, i, k, :], xg[:, i, k * P:(k + 1) * P], ident[:])
                    last.then_inc(turned, 1)
                for i in range(2):
                    pe.wait_ge(xT_ready, 2 * j + i + 1)
                    for k in range(KC):
                        last = nc.tensor.matmul(f_ps[:, 3, bass.ds((2 * j + i) * E, E)], xT[i][:, k, :], gate_sb[:, k, :],
                                                start=(k == 0), stop=(k == KC - 1))
                    last.then_inc(logits_done, 1)

            def counts():
                pe.wait_ge(moe_consts, MC)
                pe.wait_ge(sel_ready, 1)
                nc.tensor.matmul(f_ps[:, 3, 0:E], tri[:], sel[:, 0, :], start=True, stop=True)
                nc.tensor.matmul(f_ps[:, 3, E:TT * E], tri[:], sel[:, 1:TT, :].rearrange("p t e -> p (t e)"), start=True, stop=False)
                for t in reversed(range(TT - 1)):
                    nc.tensor.matmul(f_ps[:, 3, (t + 1) * E:TT * E].rearrange("p (t e) -> p t e", e=E), ones[:],
                                     sel[:, t:t + 1, :].to_broadcast([P, TT - 1 - t, E]), start=False, stop=(t == 0))
                for t in range(TT):
                    last = nc.tensor.matmul(f_ps[:, 1, 0:E], ones[:], sel[:, t, :], start=(t == 0), stop=(t == TT - 1))
                last.then_inc(counted, 1)

            def enter(t, i, first=False, last=False):
                pe.wait_ge(entry_ready, t + 1)
                for k in range(TOPK):
                    done = nc.tensor.matmul(f_ps[:, 1, 0:2 * RS], row_hot[:, i, k, :],
                                            entry[:, i, k, :, :].rearrange("p a s -> p (a s)"),
                                            start=(first and k == 0), stop=(last and k == TOPK - 1))
                done.then_inc(entered, 1)

            def turn(n, i, arrived, count):
                pe.wait_ge(arrived, count)
                for k in range(KC):
                    last = nc.tensor.transpose(tr_ps[:, i, k, :], xg[:, i, k * P:(k + 1) * P], ident[:])
                last.then_inc(turned, 1)

            def up(n, i, s, half):
                pe.wait_ge(xT_split, n + 1)
                for part in range(2):
                    for k in range(KC):
                        at = half * 2 * WL + (2 * k + part) * I
                        hi, lo = split[:, bass.ds(at, I)], split[:, bass.ds(at + WL, I)]
                        nc.tensor.matmul(o_ps[:, part, 0:I], xT_hi[:, i, k, :], hi, start=(k == 0), stop=False)
                        nc.tensor.matmul(o_ps[:, part, 0:I], xT_hi[:, i, k, :], lo, start=False, stop=False)
                        last = nc.tensor.matmul(o_ps[:, part, 0:I], xT_lo[:, i, k, :], hi, start=False, stop=(k == KC - 1))
                last.then_inc(up_done, 1)

            def down(s, half, free, first=True, final=True, load=lambda: None):
                pe.wait_ge(hidT_split, s + 1)
                if free is not None:
                    pe.wait_ge(y_ready, free)
                for c in range(DC):
                    rows = P if c < DC - 1 else LASTD
                    at = half * 2 * WL + UP + c * D
                    if c == DC - 1:
                        loaded = load()
                    hi, lo = split[0:rows, bass.ds(at, D)], split[0:rows, bass.ds(at + WL, D)]
                    nc.tensor.matmul(f_ps[:, 2, :], hidT_hi[0:rows, c, :], hi, start=(first and c == 0), stop=False)
                    nc.tensor.matmul(f_ps[:, 2, :], hidT_hi[0:rows, c, :], lo, start=False, stop=False)
                    last = nc.tensor.matmul(f_ps[:, 2, :], hidT_lo[0:rows, c, :], hi, start=False, stop=(final and c == DC - 1))
                last.then_inc(down_done, 1)
                return loaded

            def turn_hidden(s):
                pe.wait_ge(hid_ready, s + 1)
                for c in range(DC):
                    rows = P if c < DC - 1 else LASTD
                    last = nc.tensor.transpose(f_ps[0:rows, 0, c * P:(c + 1) * P], hid[:, c * P:c * P + rows], ident[:])
                last.then_inc(hid_turned, 1)

            def shared_up(t, i, u):
                up(t, i, 2 * t + u, u)

            def shared_down(t, u, **load):
                if u == 0 and (not isinstance(t, int) or t > 0):
                    pe.wait_ge(sum_copied, t)
                return down(2 * t + u, u, None, first=(u == 0), final=(u == 1), **load)

            def shared_tile(t, i, turn_next, between=lambda u: None):
                shared_down(t - 1, 0)
                turn_hidden(2 * t - 1)
                shared_up(t, i, 0)
                between(0)
                shared_down(t - 1, 1)
                turn_hidden(2 * t)
                shared_up(t, i, 1)
                between(1)
                turn_next()

            pe.wait_ge(lo_ready, NP_)
            turn(0, 0, tile_in[0], 16)
            shared_up(0, 0, 0)
            turn_hidden(0)
            pe.wait_ge(lo_ready, NP_ * SH)
            shared_up(0, 0, 1)
            turn(1, 1, tile_in[1], 16)

            def tile_pair(j, between=lambda t, i, u: None):
                for i in range(2):
                    t = 2 * j + 1 + i
                    shared_tile(t, 1 - i, lambda: turn(t + 1, i, tile_in[i], 16 * (j + 1) + 16),
                                lambda u: between(t, i, u))

            shared_tile(1, 1, lambda: turn(2, 0, tile_in[0], 32))
            shared_tile(2, 0, lambda: turn(3, 1, tile_in[1], 32))
            with pe.Fori(1, BEFORE_COUNTS) as j:
                tile_pair(j)
            counts()
            BT = BEFORE_COUNTS
            def enters(first, final=False):
                def between(t, i, u):
                    enter(2 * (t - (2 * BT + 1)) + u, u, first and i == 0 and u == 0, final and i == 1 and u == 1)
                return between

            tile_pair(BT, enters(True))
            with pe.Fori(BT + 1, TT // 2 - 2) as j:
                tile_pair(j, enters(False))
            tile_pair(TT // 2 - 2, enters(False, True))
            shared_tile(TT - 1, 1, lambda: turn(TT, 0, xg_in[0], 16))

            def expert_of(r):
                return pe.value_load(ctl[0:1, 0, bass.ds(r, 1)], min_val=0, max_val=E - 1)

            def routed_up(r, i, expert):
                pe.wait_ge(lo_ready, NP_ * (SH + expert) + NP_ - 1)
                up(TT + r, i, SS + r, expert % 2)

            def routed_down(r, expert, load=lambda: None):
                pe.wait_ge(lo_ready, NP_ * (SH + expert) + NP_)
                return down(SS + r, expert % 2, TT + r, load=load)

            shared_down(TT - 1, 0)
            turn_hidden(SS - 1)
            routed_up(0, 0, 0)
            turn(TT + 1, 1, xg_in[1], 16)
            e1 = shared_down(TT - 1, 1, load=lambda: expert_of(1))
            turn_hidden(SS)
            routed_up(1, 1, e1)
            turn(TT + 2, 0, xg_in[0], 32)
            carried = [pe.alloc_register(f"carried_expert{i}") for i in range(2)]
            pe.reg_mov(carried[0], 0)
            pe.reg_mov(carried[1], e1)
            with pe.Fori(0, (RS - 3) // 2) as j:
                for i in range(2):
                    r = 2 * j + i
                    expert = pe.snap(carried[i], min_val=0, max_val=E - 1)
                    later = routed_down(r, expert, load=lambda: expert_of(r + 2))
                    turn_hidden(SS + r + 1)
                    routed_up(r + 2, i, later)
                    pe.reg_mov(carried[i], later)
                    turn(TT + r + 3, 1 - i, xg_in[1 - i], 16 * (j + 2 + i))
            rest = [pe.snap(c, min_val=0, max_val=E - 1) for c in carried]
            last = routed_down(RS - 3, rest[0], load=lambda: expert_of(RS - 1))
            turn_hidden(SS + RS - 2)
            routed_up(RS - 1, 0, last)
            routed_down(RS - 2, rest[1])
            turn_hidden(SS + RS - 1)
            routed_down(RS - 1, last)


_IN = ("x", "ctxT", "W0", "as0", "an0", "b0", "W1", "as1", "an1", "b1", "gateT", "experts")


def kernel(**inputs):
    import numpy as np
    import concourse.bacc as bacc
    from concourse import mybir
    from concourse.bass_utils import run_bass_kernel_spmd

    a = {n.replace("L0_xattn_", "").replace("L0_ffn_", ""): np.asarray(v) for n, v in inputs.items()}
    P, D, I, E = 128, 512, 352, 16

    def up_rows(w):
        return w.T.reshape(D // P, P, 2 * I).transpose(1, 0, 2).reshape(P, -1)

    def down_rows(w):
        full = np.zeros((3 * P, D), w.dtype)
        full[:I] = w.T
        return full.reshape(3, P, D).transpose(1, 0, 2).reshape(P, -1)

    units = [(a["expert_up_w"][e], a["expert_down_w"][e]) for e in range(E)]
    S = 2 * I
    for u in range(2):
        rows = slice(u * I, (u + 1) * I)
        units.append((np.concatenate([a["shared_up_w"][0:S][rows], a["shared_up_w"][S:2 * S][rows]]),
                      a["shared_down_w"][:, rows]))
    experts = np.stack([np.concatenate([up_rows(u), down_rows(d)], axis=1) for u, d in units])
    arrays = dict(zip(_IN, (a["x"], a["ctx_512"].transpose(0, 2, 1), a["W0"], a["a_self0"], a["a_neigh0"], a["b0"],
                            a["W1"], a["a_self1"], a["a_neigh1"], a["b1"], a["gate_w"].T, experts)))
    arrays = {n: np.ascontiguousarray(v) for n, v in arrays.items()}
    nc = bacc.Bacc("TRN2", target_bir_lowering=False, num_devices=1)
    args = [nc.dram_tensor(f"in_{n}", v.shape, mybir.dt.from_np(v.dtype), kind="ExternalInput").ap() for n, v in arrays.items()]
    T = a["x"].shape[0] * a["x"].shape[1]
    out = nc.dram_tensor("out_rows", (T + P, D), mybir.dt.float32, kind="ExternalOutput").ap()
    gat_then_experts(nc, *args, out)
    r = run_bass_kernel_spmd(nc, [{f"in_{n}": v for n, v in arrays.items()}], core_ids=[0])
    return r.results[0]["out_rows"][:T].reshape(a["x"].shape)
```

```python
import concourse.bass as bass
from concourse import mybir
from contextlib import ExitStack


def gat_then_experts(nc, x, ctxT, W0, as0, an0, b0, W1, as1, an1, b1, gateT, experts, out):
    f32 = mybir.dt.float32
    ALU = mybir.AluOpType
    ACT = mybir.ActivationFunctionType
    AX = mybir.AxisListType
    i32 = mybir.dt.int32
    f32r = mybir.dt.float32r


    G, N, D = x.shape
    P = 128
    NC = N // P
    H, F_IN, O = W0.shape
    KC = D // P
    TT = G * NC
    R = H * NC
    SLOPE = 0.2
    MASK = 1e10
    EPS = 1e-5
    RING = 2 * NC
    HP = H // 2
    AHEAD_X = 5
    EXP_LAG = 1
    AHEAD_E = 4
    FREE = 2

    T = G * N
    E = gateT.shape[1]
    NGR, TOPG, TOPK = 4, 2, 4
    EG = E // NGR
    U = experts.shape[0]
    SH = U - E
    WL = experts.shape[2]
    DC = 3
    I = (WL - DC * D) // (2 * KC)
    LASTD = I - (DC - 1) * P
    SS = SH * TT
    RS = T * TOPK // P + E - 1
    ALWAYS = T * TOPK // P
    PAIRS = (RS + 1) // 2
    RT = 2 * PAIRS + 3
    TURNS_FREE = 4
    PADS = P
    UP = KC * 2 * I
    PIECES = ((0, UP // 2), (UP // 2, UP), (UP, WL))
    NP_ = len(PIECES)

    x_v = x.rearrange("g (c p) d -> p (g c) d", p=P)

    ctx = ExitStack()
    with ctx:
        def sb(name, shape, dt=f32):
            return ctx.enter_context(nc.sbuf_tensor(name, shape, dt))

        def pb(name, shape, dt=f32):
            return ctx.enter_context(nc.psum_tensor(name, shape, dt))

        def sem(name):
            return ctx.enter_context(nc.semaphore(name))

        x_sb = sb("x_sb", [P, TT, D])
        ctx_sb = sb("ctx_sb", [P, N])
        w0_sb = sb("w0_sb", [P, 1, H, O])
        with nc.sbuf_tensor("attention", [P, 4 * WL], f32) as attention:
            pass
        split = ctx.enter_context(nc.sbuf_tensor("split", [P, 4 * WL], f32r))
        w_stage = sb("w_stage", [P, 2 * WL])
        at = [0]

        def shared_space(cols):
            at[0] += cols
            return attention[:, at[0] - cols:at[0]]

        w1_sb = shared_space(KC * H * O).rearrange("p (k h o) -> p k h o", k=KC, h=H)
        att_bc = sb("att_bc", [P, 4, H * O])
        b_col = sb("b_col", [P, 2, HP])
        prod = sb("prod", [P, H * O])
        wa = sb("wa", [P, 1 + KC, 2 * H])
        ident = sb("ident", [P, P])
        stats = sb("stats", [P, TT, 6])
        mv = sb("mv", [P, TT, 2])
        rstd = sb("rstd", [P, TT])
        nmask = shared_space(NC * N).rearrange("p (c n) -> p c n", c=NC)
        feat_odd = shared_space(NC * H * O).rearrange("p (c n) -> p c n", c=NC)
        head_feat = sb("head_feat", [P, 2, NC, O])
        hT = shared_space(KC * N).rearrange("p (c n) -> p c n", c=KC)
        st_sb = sb("st_sb", [2 * H, N])
        negs = sb("negs", [P, 2, NC, H])
        scol = sb("scol", [P, 2, NC])
        t_sb = sb("t_sb", [P, 2, N])
        ring = shared_space(RING * N).rearrange("p (s n) -> p s n", n=N)
        mx = sb("mx", [P, RING])
        rsum = sb("rsum", [P, RING])
        rec = sb("rec", [P, RING])
        eT = shared_space(2 * NC * N).rearrange("p (i c n) -> p i c n", i=2, n=N)
        w1_products = w_stage[:, WL:WL + 2 * KC * H * O].rearrange("p (n k m) -> p n k m", n=2, k=KC)
        pos = sb("pos", [P, N])
        neg = sb("neg", [P, N])
        t_rows = nc.dram_tensor("t_rows", [2, H, N], f32, kind="Internal").ap()

        tri = sb("tri", [P, P])
        ones = sb("ones", [P, P])
        count = sb("count", [P, P])
        count_p = sb("count_p", [P, E])
        below = sb("below", [P, E, E])
        token = sb("token", [P, TT])
        pad_row = sb("pad_row", [P, 1])
        gate_sb = sb("gate_sb", [P, KC, E])
        xg = sb("xg", [P, 2, D])
        with nc.sbuf_tensor("feat_even", [P, NC, H * O], f32) as feat_even:
            pass
        feats = (feat_even, feat_odd)
        xT_hi = sb("xT_hi", [P, 2, KC, P], f32r)
        xT = [a[:].rearrange("p (k q) -> p k q", k=KC) for a in (pos, neg)]
        xT_lo = sb("xT_lo", [P, 2, KC, P], f32r)
        score = sb("score", [P, TT, E])
        rmax = sb("rmax", [P, TT])
        rtot = sb("rtot", [P, TT])
        gtop = sb("gtop", [P, TT, NGR])
        grank = sb("grank", [P, TT, NGR])
        gcmp = sb("gcmp", [P, TT, NGR])
        rank = sb("rank", [P, TT, E])
        cmp = sb("cmp", [P, TT, E])
        sel = sb("sel", [P, TT, E])
        comb = sb("comb", [P, TT, E])
        place = sb("place", [P, TT, E])
        eq = sb("eq", [P, TT, E])
        load = sb("load", [P, E])
        tiles = sb("tiles", [P, E])
        first = sb("first", [P, E])
        first_row = sb("first_row", [P, E])
        sq = sb("sq", [P, E, E])
        place_k = sb("place_k", [P, TT, TOPK])
        w_k = sb("w_k", [P, TT, TOPK])
        place_i = sb("place_i", [P, TT, TOPK], i32)
        slot_i = sb("slot_i", [P, TT, TOPK], i32)
        row_i = sb("row_i", [P, TT, TOPK], i32)
        slot_f = sb("slot_f", [P, TT, TOPK])
        row_f = sb("row_f", [P, TT, TOPK])
        tok_k = sb("tok_k", [P, TT, TOPK])
        row_hot = sb("row_hot", [P, 2, TOPK, P])
        spare = att_bc[:].rearrange("p a n -> p (a n)")
        slot_hot = spare[:, 0:2 * TOPK * RT].rearrange("p (i k s) -> p i k s", i=2, k=TOPK)
        entry = spare[:, 2 * TOPK * RT:6 * TOPK * RT].rearrange("p (i k a s) -> p i k a s", i=2, k=TOPK, a=2)
        idx_f = sb("idx_f", [P, RT])
        idx_tab = sb("idx_tab", [P, RT], i32)
        w_tab = sb("w_tab", [P, RT])
        owner = sb("owner", [1, RT, E])
        used_f = sb("used_f", [1, 1])
        used = sb("used", [1, 1], i32)
        prior = sb("prior", [1, RT])
        ctl = sb("ctl", [1, 3, RT], i32)
        ctl_f = sb("ctl_f", [1, 3, RT])
        gidx = sb("gidx", [P, 2], i32)
        sidx = sb("sidx", [P, 2], i32)
        sg = sb("sg", [P, I])
        hid = sb("hid", [P, I])
        hidT_hi = sb("hidT_hi", [P, DC, P], f32r)
        hidT_lo = sb("hidT_lo", [P, DC, P], f32r)
        up_sb = prod[:, 0:I]
        hidT = neg[:, 0:DC * P].rearrange("p (c q) -> p c q", q=P)
        xT_sb = pos[:].rearrange("p (c q) -> p c q", q=P)
        sum_sb = ctx_sb
        rows_sb = [xg[:, 0, :], xg[:, 1, :], t_sb[:, 0, :], t_sb[:, 1, :]]
        y_sb = t_sb
        zrow = sb("zrow", [PADS, D // 2])
        xn_rows = nc.dram_tensor("xn_rows", [T + PADS, D], f32, kind="Internal").ap()

        BEFORE_COUNTS = TT // 2 - 1 - TT // 4

        tr_ps = pb("tr_ps", [P, 2, NC, P])
        o_ps = pb("o_ps", [P, 2, N])
        f_ps = pb("f_ps", [P, NC, H * O])

        def hidden_ps(a, b):
            return f_ps[:, 0, a * P:b * P].rearrange("p (c q) -> p c q", q=P)

        w_in = sem("w_in")
        w1_in = sem("w1_in")
        products_ready = sem("products_ready")
        wa1_ready = sem("wa1_ready")
        x_in = [sem(f"x_in{g}") for g in range(G)]
        ctx_in = sem("ctx_in")
        t_out = sem("t_out")
        t_in = [sem(f"t_in{i}") for i in range(2)]
        setup_pool = sem("setup_pool")
        consts = sem("consts")
        setup_dve = sem("setup_dve")
        var_done = sem("var_done")
        std_done = sem("std_done")
        wa_ready = sem("wa_ready")
        mask_step = sem("mask_step")
        st_done = sem("st_done")
        st_copied = sem("st_copied")
        s_turned = sem("s_turned")
        s_copied = sem("s_copied")
        feat_done = sem("feat_done")
        feat_copied = sem("feat_copied")
        scol_ready = sem("scol_ready")
        head_feat_ready = sem("head_feat_ready")
        x_ready = sem("x_ready")
        z_ready = sem("z_ready")
        e_ready = sem("e_ready")
        p_ready = sem("p_ready")
        rec_ready = sem("rec_ready")
        alpha_ready = sem("alpha_ready")
        T_done = sem("T_done")
        evac_done = sem("evac_done")
        mixed = sem("mixed")
        parts_ready = sem("parts_ready")
        min_ready = sem("min_ready")
        elu_parts = sem("elu_parts")
        hT_ready = sem("hT_ready")
        h_turned = sem("h_turned")
        x2_ready = sem("x2_ready")
        stored = sem("stored")
        moe_set = sem("moe_set")
        moe_consts = sem("moe_consts")
        MC = 7
        var2_done = sem("var2_done")
        std2_done = sem("std2_done")
        xn_ready = sem("xn_ready")
        xn_out = [sem(f"xn_out{i}") for i in range(4)]
        tile_in = [sem(f"tile_in{i}") for i in range(2)]
        pads_out = sem("pads_out")
        tile_out = [sem(f"tile_out{i}") for i in range(2)]
        gate_in = sem("gate_in")
        turned = sem("turned")
        xT_ready = sem("xT_ready")
        xT_split = sem("xT_split")
        logits_done = sem("logits_done")
        route_step = sem("route_step")
        shift_done = sem("shift_done")
        exp_done = sem("exp_done")
        sel_ready = sem("sel_ready")
        counted = sem("counted")
        entry_ready = sem("entry_ready")
        entered = sem("entered")
        tables_ready = sem("tables_ready")
        idx_copied = sem("idx_copied")
        xg_in = [sem(f"xg_in{i}") for i in range(2)]
        raw_in = sem("raw_in")
        hi_ready = sem("hi_ready")
        lo_ready = sem("lo_ready")
        up_done = sem("up_done")
        silu_done = sem("silu_done")
        hid_ready = sem("hid_ready")
        hid_turned = sem("hid_turned")
        hidT_ready = sem("hidT_ready")
        hidT_split = sem("hidT_split")
        down_done = sem("down_done")
        sum_copied = sem("sum_copied")
        y_ready = sem("y_ready")
        added = sem("added")

        sp_waited, pool_waited, dve_waited, pe_waited = [sem(f"{n}_waited") for n in ("sp", "pool", "dve", "pe")]
        block = ctx.enter_context(nc.Block())

        @block.sync
        def _(sp):
            sp.dma_start(w0_sb[:, 0, :, :], W0.rearrange("h f o -> f h o")).then_inc(w_in, 16)
            for n, a in enumerate((as0, an0, as1, an1)):
                sp.dma_start(att_bc[:, n, :], a.rearrange("h o -> (h o)").partition_broadcast(P)).then_inc(w_in, 16)
            sp.dma_start(ctx_sb[:], ctxT[0, :, :]).then_inc(ctx_in, 16)
            for n, a in enumerate((b0, b1)):
                sp.dma_start(b_col[:, n, :], a.rearrange("(j i) o -> (i o) j", i=2),
                             allow_slow_non_contiguous=True).then_inc(w_in, 16)

            def load_graph(g):
                sp.dma_start(x_sb[:, NC * g:NC * (g + 1), :], x_v[:, NC * g:NC * (g + 1), :]).then_inc(x_in[g], 16)

            load_graph(0)
            for k in range(KC):
                sp.dma_start(w1_sb[:, k, :, :], W1[:, k * P:(k + 1) * P, :].rearrange("h f o -> f h o")).then_inc(w1_in, 16)
            for g in range(1, G):
                load_graph(g)

            def load_shared(u):
                if u:
                    sp.wait_ge(raw_in, 16 * u)
                sp.dma_start(w_stage[:, u * WL:(u + 1) * WL], experts[E + u, :, :]).then_inc(raw_in, 16)

            def load_context(g):
                sp.dma_start(ctx_sb[:], ctxT[bass.ds(g, 1), :, :].rearrange("a f n -> f (a n)")).then_inc(ctx_in, 16)

            def rows_out(L, l):
                sp.wait_ge(st_copied, L + 1)
                sp.dma_start(t_rows[l], st_sb[H:2 * H, :]).then_inc(t_out, 16)
                sp.wait_ge(t_out, 16 * L + 16)

            def row_in(L, l, h, i):
                if not (isinstance(L, int) and L == 0 and isinstance(h, int)):
                    sp.wait_ge(x_ready, R * L + NC * (h - 1))
                sp.dma_start(t_sb[:, i, :], t_rows[l, bass.ds(h, 1), :].rearrange("a n -> (a n)").partition_broadcast(P)).then_inc(t_in[i], 16)

            def graph(g, last=False):
                for l in range(2):
                    L = 2 * g + l
                    if l == 1:
                        rows_out(L, 1)
                        for i in range(2):
                            row_in(L, 1, i, i)
                        if not last:
                            sp.wait_ge(feat_done, L)
                            load_context(g + 1)
                    with sp.Fori(1, HP) as j:
                        for i in range(2):
                            row_in(L, l, 2 * j + i, i)
                if not last:
                    rows_out(L + 1, 0)
                    for i in range(2):
                        row_in(L + 1, 0, i, i)

            rows_out(0, 0)
            for i in range(2):
                row_in(0, 0, i, i)
            load_shared(0)
            with sp.Fori(0, G - 1) as g:
                graph(g)
            sp.wait_ge(wa1_ready, 2)
            load_shared(1)
            graph(G - 1, last=True)
            sp.dma_start(gate_sb[:], gateT.rearrange("(k p) e -> p k e", p=P)).then_inc(gate_in, 16)
            sp.wait_ge(moe_consts, MC)
            for rows in (xn_rows, out):
                for a in (0, D // 2):
                    sp.dma_start(rows[T:T + PADS, a:a + D // 2], zrow[:]).then_inc(pads_out, 16)
            with sp.Fori(0, TT // 4) as j:
                for i in range(4):
                    sp.wait_ge(xn_ready, 4 * j + i + 1)
                    sp.dma_start(xn_rows[bass.ds((4 * j + i) * P, P), :], rows_sb[i]).then_inc(xn_out[i], 16)
            for i in range(4):
                sp.wait_ge(xn_out[i], 16 * (TT // 4 + 1))
            sp.wait_ge(turned, TT + TURNS_FREE)

            def load_tile(t, i):
                sp.dma_start(xg[:, i, :], xn_rows[bass.ds(t * P, P), :]).then_inc(tile_in[i], 16)

            def load_expert(e, i, n):
                sp.wait_ge(raw_in, 16 * n)
                sp.sem_inc(sp_waited, 1)
                sp.wait_ge(lo_ready, NP_ * (n - 1))
                sp.dma_start(w_stage[:, i * WL:(i + 1) * WL],
                             experts[bass.ds(e, 1), :, :].rearrange("a p w -> p (a w)")).then_inc(raw_in, 16)

            load_tile(0, 0)
            load_tile(1, 1)
            for e in range(2):
                load_expert(e, e, SH + e)

            def store_tile(t, i):
                sp.wait_ge(y_ready, t + 1)
                sp.dma_start(out[bass.ds(t * P, P), :], y_sb[:, i, :]).then_inc(tile_out[i], 16)

            with sp.Fori(0, TT // 2 - 1) as j:
                for i in range(2):
                    sp.wait_ge(turned, TT + 2 * j + i + 1 + TURNS_FREE)
                    load_tile(2 * j + i + 2, i)
                    store_tile(2 * j + i, i)
            for i in range(2):
                store_tile(TT - 2 + i, i)
            with sp.Fori(1, E // 2) as j:
                for i in range(2):
                    load_expert(2 * j + i, i, SH + 2 * j + i)

        @block.gpsimd
        def _(pool):
            nc.gpsimd.memset(ident[:], 0.0).then_inc(setup_pool, 1)
            pool.wait_ge(setup_pool, 1)
            nc.gpsimd.affine_select(out=ident[:], in_=ident[:], compare_op=ALU.not_equal, fill=1.0,
                                    base=0, pattern=[[-1, P]], channel_multiplier=1).then_inc(consts, 1)
            pool.sem_inc(T_done, RING)
            pool.sem_inc(parts_ready, FREE)
            pool.sem_inc(hT_ready, 1)

            nc.gpsimd.memset(ones[:], 1.0).then_inc(moe_set, 1)
            nc.gpsimd.memset(below[:], 1.0).then_inc(moe_set, 1)
            nc.gpsimd.memset(zrow[:], 0.0).then_inc(moe_consts, 1)
            pool.wait_ge(moe_set, 2)
            nc.gpsimd.affine_select(out=tri[:], in_=ones[:], compare_op=ALU.is_gt, fill=0.0, base=0,
                                    pattern=[[1, P]], channel_multiplier=-1).then_inc(moe_consts, 1)
            nc.gpsimd.affine_select(out=below[:], in_=below[:], compare_op=ALU.is_gt, fill=0.0, base=0,
                                    pattern=[[1, E], [-1, E]], channel_multiplier=0).then_inc(moe_consts, 1)
            exact = dict(allow_small_or_imprecise_dtypes=True)
            nc.gpsimd.iota(count[:], pattern=[[1, P]], base=0, channel_multiplier=0, **exact).then_inc(moe_consts, 1)
            nc.gpsimd.iota(count_p[:], pattern=[[P, E]], base=0, channel_multiplier=0, **exact).then_inc(moe_consts, 1)
            nc.gpsimd.iota(token[:], pattern=[[P, TT]], base=0, channel_multiplier=1, **exact).then_inc(moe_consts, 1)
            nc.gpsimd.iota(pad_row[:], pattern=[[1, 1]], base=T, channel_multiplier=1, **exact).then_inc(moe_consts, 1)
            for i in range(2):
                pool.sem_inc(tile_out[i], 16)
            pool.sem_inc(turned, TURNS_FREE)
            for i in range(4):
                pool.sem_inc(xn_out[i], 16)

            pool.wait_ge(w_in, 16 * 7)
            pool.wait_ge(w1_in, 16 * KC)
            for k in range(KC):
                for n in range(2):
                    nc.gpsimd.tensor_tensor(w1_products[:, n, k, :], w1_sb[:, k, :, :].rearrange("p h o -> p (h o)"), att_bc[:, 2 + n, :],
                                            ALU.mult).then_inc(products_ready, 1)

            def sum_step(L, j, s):
                h, c = 2 * j + s // NC, s % NC
                i, slot = (s // NC) % 2, s % RING
                if c == 0:
                    pool.wait_ge(t_in[i], 16 * (HP * L + j + s // RING + 1))
                    pool.wait_ge(scol_ready, H * L + h + 1)
                pool.wait_ge(T_done, R * L + RING * j + s + 1)
                pool.sem_inc(pool_waited, 1)
                nc.gpsimd.tensor_scalar(ring[:, slot, :], t_sb[:, i, :], scol[:, i, c:c + 1], 1.0,
                                        ALU.add, ALU.mult).then_inc(x_ready, 1)

            def head_pair(L, j, last):
                for s in range(RING):
                    if not (last and s + AHEAD_X >= RING):
                        sum_step(L, j, s + AHEAD_X)
                    if s % 2 == 0:
                        pool.wait_ge(rec_ready, R // 2 * L + HP * j + s // 2 + 1)
                        pool.sem_inc(pool_waited, 1)
                    nc.gpsimd.tensor_scalar(ring[:, s, :], ring[:, s, :], rec[:, s:s + 1], 1.0,
                                            ALU.mult, ALU.mult).then_inc(alpha_ready, 1)

            with pool.Fori(0, G) as g:
                for l in range(2):
                    L = 2 * g + l
                    for s in range(AHEAD_X):
                        sum_step(L, 0, s)
                    with pool.Fori(0, HP - 1) as j:
                        head_pair(L, j, False)
                    head_pair(L, HP - 1, True)

            pool.wait_ge(x2_ready, G * HP)
            for u in range(SH):
                for n, (a, b) in enumerate(PIECES):
                    pool.wait_ge(hi_ready, NP_ * u + n + 1)
                    hi, lo = 2 * u * WL, (2 * u + 1) * WL
                    nc.gpsimd.tensor_tensor(split[:, lo + a:lo + b], w_stage[:, u * WL + a:u * WL + b],
                                            split[:, hi + a:hi + b].bitcast(f32), ALU.subtract).then_inc(lo_ready, 1)

            def shared_gate(s):
                pool.wait_ge(silu_done, s + 1)
                nc.gpsimd.tensor_tensor(hid[:], sg[:], up_sb, ALU.mult).then_inc(hid_ready, 1)

            def shared_x_low(t, i):
                pool.wait_ge(xT_ready, TT + t + 1)
                nc.gpsimd.tensor_tensor(xT_lo[:, i, :, :], xT_sb, xT_hi[:, i, :, :].bitcast(f32), ALU.subtract).then_inc(xT_split, 1)

            def shared_hidden_low(s):
                pool.wait_ge(hidT_ready, s + 1)
                nc.gpsimd.tensor_tensor(hidT_lo[:, 0:DC - 1, :], hidT[:, 0:DC - 1, :], hidT_hi[:, 0:DC - 1, :].bitcast(f32), ALU.subtract)
                nc.gpsimd.tensor_tensor(hidT_lo[0:LASTD, DC - 1, :], hidT[0:LASTD, DC - 1, :],
                                        hidT_hi[0:LASTD, DC - 1, :].bitcast(f32), ALU.subtract).then_inc(hidT_split, 1)

            def shared_add(t, i, nth):
                pool.wait_ge(sum_copied, t + 1)
                pool.wait_ge(tile_out[i], 16 * nth + 16)
                pool.sem_inc(pool_waited, 1)
                nc.gpsimd.tensor_tensor(y_sb[:, i, :], sum_sb[:], x_sb[:, bass.ds(t, 1), :].rearrange("p a d -> p (a d)"),
                                        ALU.add).then_inc(y_ready, 1)

            def shared_tile(t, i, nth, first=False):
                shared_gate(2 * t)
                shared_hidden_low(2 * t)
                if not first:
                    shared_add(t - 1, 1 - i, nth)
                shared_gate(2 * t + 1)
                shared_x_low(t + 1, 1 - i)
                shared_hidden_low(2 * t + 1)

            def gather(r, i, copies):
                pool.wait_ge(turned, 2 * TT + r - 1 + TURNS_FREE)
                nc.gpsimd.tensor_copy(gidx[:, i:i + 1], idx_tab[:, bass.ds(r, 1)]).then_inc(idx_copied, 1)
                pool.wait_ge(idx_copied, copies)
                pool.sem_inc(pool_waited, 1)
                nc.gpsimd.indirect_dma_start(xg[:, i, :], None, xn_rows, bass.IndirectOffsetOnAxis(ap=gidx[:, i:i + 1], axis=0),
                                             bounds_check=T + PADS - 1, oob_is_err=True).then_inc(xg_in[i], 16)

            def scatter(r, i, copies, first=False):
                nc.gpsimd.tensor_copy(sidx[:, i:i + 1], idx_tab[:, bass.ds(r, 1)]).then_inc(idx_copied, 1)
                if not first:
                    pool.wait_ge(added, 16 * r)
                pool.wait_ge(idx_copied, copies)
                pool.wait_ge(y_ready, TT + r + 1)
                pool.sem_inc(pool_waited, 1)
                nc.gpsimd.indirect_dma_start(out, bass.IndirectOffsetOnAxis(ap=sidx[:, i:i + 1], axis=0), y_sb[:, i, :], None,
                                             bounds_check=T + PADS - 1, oob_is_err=True, compute_op=ALU.add).then_inc(added, 16)

            shared_x_low(0, 0)
            shared_tile(0, 0, 0, first=True)
            with pool.Fori(0, TT // 2 - 1) as j:
                shared_tile(2 * j + 1, 1, j)
                shared_tile(2 * j + 2, 0, j)
            pool.wait_ge(pads_out, 64)
            pool.wait_ge(tables_ready, 1)
            gather(0, 0, 1)
            shared_gate(SS - 2)
            shared_hidden_low(SS - 2)
            shared_add(TT - 2, 0, TT // 2 - 1)
            gather(1, 1, 2)
            shared_gate(SS - 1)
            shared_hidden_low(SS - 1)
            gather(2, 0, 3)
            for i in range(2):
                pool.wait_ge(tile_out[i], 16 * (TT // 2 + 1))


            def slot_pair(j, first=False):
                for i in range(2):
                    r = 2 * j + i
                    gather(r + 3, 1 - i, 2 * r + 4)
                    scatter(r, i, 2 * r + 5, first=first and i == 0)

            slot_pair(0, first=True)
            with pool.Fori(1, ALWAYS // 2) as j:
                slot_pair(j)
            with pool.Fori(ALWAYS // 2, PAIRS) as j:
                in_use = pool.value_load(ctl[0:1, 1, bass.ds(2 * j, 1)], min_val=0, max_val=1)
                with pool.If(in_use):
                    slot_pair(j)
            scattered = pool.value_load(used[0:1, 0:1], min_val=ALWAYS, max_val=2 * PAIRS)
            pool.wait_ge(added, 16 * scattered)
            pool.sem_inc(pool_waited, 1)

        @block.scalar
        def _(act):
            act.wait_ge(wa_ready, 1)
            act.wait_ge(var_done, 1)
            nc.scalar.activation(rstd[:, 0:NC], rstd[:, 0:NC], ACT.Sqrt).then_inc(std_done, 1)

            def exp_step(L, r, slot):
                act.wait_ge(e_ready, R * L + r + 1)
                nc.scalar.activation(ring[:, slot, :], ring[:, slot, :], ACT.Exp, bias=mx[:, slot:slot + 1], scale=-1.0,
                                     accum_out=rsum[:, slot:slot + 1]).then_inc(p_ready, 1)

            def value_step(L, l, j, i):
                half = slice(O * i, O * i + O)
                act.wait_ge(mixed, H * L + 2 * j + i + 1)
                if i == 0:
                    act.wait_ge(hT_ready, HP * L + j + 1)
                nc.scalar.activation(pos[half, :], o_ps[half, i, :], ACT.Identity, bias=b_col[half, l, bass.ds(j, 1)]).then_inc(parts_ready, 1)

            def elu_exp_step(L, j):
                act.wait_ge(min_ready, HP * L + j + 1)
                nc.scalar.activation(neg[:], neg[:], ACT.Exp).then_inc(elu_parts, 1)

            def head_pair(L, l, j, first, last):
                for s in range(RING):
                    r = RING * j + s
                    act.wait_ge(T_done, R * L + r + 1 + RING)
                    c = s % NC
                    nc.scalar.activation(eT[:, s // NC, :, c * P:(c + 1) * P], tr_ps[:, s % 2, :, :], ACT.Copy).then_inc(evac_done, 1)
                    if c == 0 and not first:
                        value_step(L, l, j - 1, s // NC)
                    if s == NC + EXP_LAG and not first:
                        elu_exp_step(L, j - 1)
                    if not (last and s + AHEAD_E >= RING):
                        exp_step(L, r + AHEAD_E, (s + AHEAD_E) % RING)

            def graph(g, first=False, last=False):
                for l in range(2):
                    L = 2 * g + l
                    if l == 1:
                        if first:
                            act.wait_ge(var_done, 2)
                            nc.scalar.activation(rstd[:, NC:TT], rstd[:, NC:TT], ACT.Sqrt).then_inc(std_done, 1)
                        for s in range(AHEAD_E):
                            exp_step(L, s, s)
                    head_pair(L, l, 0, True, False)
                    with act.Fori(1, HP - 1) as j:
                        head_pair(L, l, j, False, False)
                    head_pair(L, l, HP - 1, False, True)
                    value_step(L, l, HP - 1, 0)
                    if l == 1 and not last:
                        exp_step(L + 1, 0, 0)
                        exp_step(L + 1, 1, 1)
                    value_step(L, l, HP - 1, 1)
                    elu_exp_step(L, HP - 1)
                if not last:
                    exp_step(L + 1, 2, 2)
                    exp_step(L + 1, 3, 3)

            for s in range(AHEAD_E):
                exp_step(0, s, s)
            graph(0, first=True)
            with act.Fori(1, G - 1) as g:
                graph(g)
            graph(G - 1, last=True)

            act.wait_ge(var2_done, 1)
            nc.scalar.activation(rstd[:], rstd[:], ACT.Sqrt).then_inc(std2_done, 1)

            def copy_turned(n, i):
                act.wait_ge(turned, n + 1 + TURNS_FREE)
                nc.scalar.activation(xT[i], tr_ps[:, i, :, :], ACT.Copy).then_inc(xT_ready, 1)

            for u in range(SH):
                act.wait_ge(raw_in, 16 * (u + 1))
                for a, b in PIECES:
                    nc.scalar.activation(split[:, 2 * u * WL + a:2 * u * WL + b], w_stage[:, u * WL + a:u * WL + b], ACT.Copy).then_inc(hi_ready, 1)
                with act.Fori(0, TT // 4) as j:
                    for i in range(2):
                        copy_turned(u * (TT // 2) + 2 * j + i, i)
            act.wait_ge(shift_done, 1)
            nc.scalar.activation(score[:], score[:], ACT.Exp).then_inc(exp_done, 1)

            def split_high(i, p):
                a, b = PIECES[p]
                nc.scalar.activation(split[:, bass.ds(i * 2 * WL + a, b - a)], w_stage[:, bass.ds(i * WL + a, b - a)], ACT.Copy).then_inc(hi_ready, 1)

            def silu(s):
                act.wait_ge(up_done, s + 1)
                nc.scalar.activation(sg[:], o_ps[:, 0, 0:I], ACT.Silu).then_inc(silu_done, 1)

            def x_high(n, i):
                act.wait_ge(turned, TT + n + 1 + TURNS_FREE)
                nc.scalar.activation(xT_hi[:, i, :, :], tr_ps[:, i, :, :], ACT.Copy).then_inc(xT_ready, 1)

            def hidden_high(s):
                act.wait_ge(hid_turned, s + 1)
                nc.scalar.activation(hidT_hi[:, 0:DC - 1, :], hidden_ps(0, DC - 1), ACT.Copy)
                nc.scalar.activation(hidT_hi[0:LASTD, DC - 1, :], f_ps[0:LASTD, 0, (DC - 1) * P:DC * P], ACT.Copy).then_inc(hidT_ready, 1)

            def shared_silu(s):
                act.wait_ge(up_done, s + 1)
                nc.scalar.activation(sg[:], o_ps[:, 0, 0:I], ACT.Silu)
                nc.scalar.activation(up_sb, o_ps[:, 1, 0:I], ACT.Copy).then_inc(silu_done, 1)

            def shared_x(t, i):
                act.wait_ge(turned, TT + t + 1 + TURNS_FREE)
                nc.scalar.activation(xT_sb, tr_ps[:, i, :, :], ACT.Copy)
                nc.scalar.activation(xT_hi[:, i, :, :], tr_ps[:, i, :, :], ACT.Copy).then_inc(xT_ready, 1)

            def shared_hidden(s):
                act.wait_ge(hid_turned, s + 1)
                for out_, in_ in ((hidT, hidden_ps), (hidT_hi, hidden_ps)):
                    nc.scalar.activation(out_[:, 0:DC - 1, :], in_(0, DC - 1), ACT.Copy)
                    last = nc.scalar.activation(out_[0:LASTD, DC - 1, :], in_(DC - 1, DC)[0:LASTD].rearrange("p c q -> p (c q)"), ACT.Copy)
                last.then_inc(hidT_ready, 1)

            def shared_sum(t, first=False):
                act.wait_ge(down_done, SH * (t + 1))
                if not first:
                    act.wait_ge(y_ready, t)
                nc.scalar.activation(sum_sb[:], f_ps[:, 2, :], ACT.Copy).then_inc(sum_copied, 1)

            def shared_tile(t, i, first=False):
                shared_silu(2 * t)
                shared_hidden(2 * t)
                if not isinstance(t, int) or t > 0:
                    shared_sum(t - 1, first)
                shared_silu(2 * t + 1)
                shared_x(t + 1, 1 - i)
                shared_hidden(2 * t + 1)

            shared_x(0, 0)
            shared_tile(0, 0)
            shared_tile(1, 1, first=True)
            shared_tile(2, 0)
            with act.Fori(1, TT // 2 - 1) as j:
                shared_tile(2 * j + 1, 1)
                shared_tile(2 * j + 2, 0)
            shared_silu(SS - 2)
            shared_hidden(SS - 2)
            act.wait_ge(raw_in, 16 * (SH + 1))
            split_high(0, 0)
            shared_sum(TT - 2)
            shared_silu(SS - 1)
            split_high(0, 1)
            x_high(TT, 0)
            shared_hidden(SS - 1)
            act.wait_ge(down_done, SS - 1)
            split_high(0, 2)

            def slot(r, i):
                new = act.value_load(ctl[0:1, 2, bass.ds(r, 1)], min_val=0, max_val=1)
                with act.If(new):
                    expert = act.value_load(ctl[0:1, 0, bass.ds(r, 1)], min_val=0, max_val=E - 1)
                    half = expert % 2
                    silu(SS + r)
                    act.wait_ge(raw_in, 16 * (SH + expert + 2))
                    x_high(TT + r + 1, 1 - i)
                    split_high(1 - half, 0)
                    hidden_high(SS + r)
                    split_high(1 - half, 1)
                    act.wait_ge(down_done, SS + r)
                    split_high(1 - half, 2)
                with act.Else():
                    silu(SS + r)
                    x_high(TT + r + 1, 1 - i)
                    hidden_high(SS + r)

            slot(0, 0)
            with act.Fori(0, ALWAYS // 2) as j:
                slot(2 * j + 1, 1)
                slot(2 * j + 2, 0)
            with act.Fori(ALWAYS // 2, PAIRS) as j:
                in_use = act.value_load(ctl[0:1, 1, bass.ds(2 * j, 1)], min_val=0, max_val=1)
                with act.If(in_use):
                    slot(2 * j + 1, 1)
                    slot(2 * j + 2, 0)

        @block.vector
        def _(dve):
            made = [0]

            def then(ins):
                made[0] += 1
                ins.then_inc(setup_dve, 1)
                dve.wait_ge(setup_dve, made[0])

            dve.wait_ge(w_in, 16 * 7)
            for n in range(2):
                then(nc.vector.tensor_tensor(prod[:], w0_sb[:, 0, :, :].rearrange("p h o -> p (h o)"), att_bc[:, n, :], ALU.mult))
                then(nc.vector.tensor_reduce(out=wa[:, 0, n * H:(n + 1) * H], in_=prod[:].rearrange("p (h o) -> p h o", h=H),
                                             op=ALU.add, axis=AX.X, negate=True))
            dve.sem_inc(wa_ready, 1)

            def column_step(l, h, i):
                nc.vector.tensor_copy(scol[:, i, :], negs[:, l, :, bass.ds(h, 1)].rearrange("p c a -> p (c a)")).then_inc(scol_ready, 1)

            def copy_terms(L, before):
                dve.wait_ge(st_done, L + 1)
                if before:
                    dve.wait_ge(t_out, 16 * L)
                nc.vector.tensor_copy(st_sb[:], f_ps[0:2 * H, 3, :]).then_inc(st_copied, 1)

            def copy_columns(L, l):
                dve.wait_ge(s_turned, L + 1)
                nc.vector.tensor_copy(negs[:, l, :, :], f_ps[:, 2, 0:NC * 2 * H].rearrange("p (c h) -> p c h", c=NC)[:, :, 0:H]).then_inc(s_copied, 1)
                dve.wait_ge(s_copied, L + 1)
                for i in range(2):
                    column_step(l, i, i)

            def statistics(g):
                dve.wait_ge(x_in[g], 16)
                for c in range(NC):
                    last = nc.vector.bn_stats(stats[:, NC * g + c, :], x_sb[:, NC * g + c, :])
                return last

            copy_terms(0, False)
            copy_columns(0, 0)
            last = statistics(0)
            def inverse_deviation(a, b, wait):
                if not wait:
                    for t in range(a, b):
                        last = nc.vector.bn_aggr(mv[:, t, :], stats[:, t, :])
                    then(last)
                    nc.vector.tensor_scalar(rstd[:, a:b], mv[:, a:b, 1], EPS, None, ALU.add).then_inc(var_done, 1)
                else:
                    dve.wait_ge(std_done, 1 if a == 0 else 2)
                    then(nc.vector.reciprocal(rstd[:, a:b], rstd[:, a:b]))

            then(last)
            for wait in (False, True):
                inverse_deviation(0, NC, wait)

            def score_step(L, j, k):
                s = 2 * k
                dve.wait_ge(x_ready, R * L + RING * j + s + 2)
                nc.vector.scalar_tensor_tensor(ring[:, s:s + 2, :], ring[:, s:s + 2, :], SLOPE,
                                               ring[:, s:s + 2, :], ALU.mult, ALU.min).then_inc(z_ready, 1)
                dve.wait_ge(z_ready, R // 2 * L + HP * j + k + 1)
                dve.sem_inc(dve_waited, 1)
                for m in range(2):
                    nc.vector.tensor_tensor_reduce(
                        out=ring[:, s + m, :], in0=ring[:, s + m, :], in1=nmask[:, (s + m) % NC, :],
                        scale=1.0, scalar=3.0e38, op0=ALU.add, op1=ALU.min,
                        accum_out=mx[:, s + m:s + m + 1]).then_inc(e_ready, 1)

            def reciprocal_step(L, j, k):
                s = (2 * k) % RING
                dve.wait_ge(p_ready, R * L + RING * j + 2 * k + 2)
                nc.vector.reciprocal(rec[:, s:s + 2], rsum[:, s:s + 2]).then_inc(rec_ready, 1)

            def weight_step(L, l, h, i):
                dve.wait_ge(parts_ready, H * L + h - 1 + FREE)
                nc.vector.tensor_copy(head_feat[:, i, :, :], feats[l][:, :, bass.ds(O * h, O)]).then_inc(head_feat_ready, 1)

            def min_step(L, j):
                dve.wait_ge(parts_ready, H * L + 2 * j + 2 + FREE)
                nc.vector.tensor_scalar(neg[:], pos[:], 0.0, None, ALU.min).then_inc(min_ready, 1)

            def elu_step(L, j):
                dve.wait_ge(elu_parts, HP * L + j + 1)
                nc.vector.scalar_tensor_tensor(hT[:, j, :], neg[:], -1.0, pos[:], ALU.add, ALU.max).then_inc(hT_ready, 1)

            def head_pair(L, l, j, residual=None):
                for k in range(1, HP):
                    score_step(L, j, k)
                    reciprocal_step(L, j, k - 1)
                    if k % 2 == 1 and j < HP - 1:
                        column_step(l, 2 * j + k // 2 + 2, k // 2)
                    if k == 1 and j >= 1:
                        weight_step(L, l, 2 * j - 1, 1)
                    if k == 1 and j >= 2:
                        if j == 2 and residual is not None:
                            dve.wait_ge(h_turned, HP * residual)
                        elu_step(L, j - 2)
                    if k == 3:
                        if j == 0:
                            copy_features(L, l)
                        weight_step(L, l, 2 * j, 0)
                if j < HP - 1:
                    score_step(L, j + 1, 0)
                reciprocal_step(L, j, HP - 1)
                if j >= 1:
                    min_step(L, j - 1)

            def mask(g, before):
                if before:
                    dve.wait_ge(e_ready, R * 2 * g)
                for c in range(NC):
                    t = NC * g + c
                    nc.vector.tensor_scalar(nmask[:, c, :], x_sb[:, bass.ds(t, 1), :].rearrange("p a d -> p (a d)"),
                                            mv[:, bass.ds(t, 1), 0:1].rearrange("p a d -> p (a d)"),
                                            rstd[:, bass.ds(t, 1)], ALU.subtract, ALU.mult).then_inc(mask_step, 1)
                for c in range(NC):
                    dve.wait_ge(mask_step, 2 * NC * g + c + 1)
                    nc.vector.tensor_scalar(nmask[:, c, :], nmask[:, c, :], -1.0, -MASK, ALU.add, ALU.mult).then_inc(mask_step, 1)

            def copy_features(L, l):
                dve.wait_ge(feat_done, L + 1)
                nc.vector.tensor_copy(feats[l][:], f_ps[:]).then_inc(feat_copied, 1)
                dve.wait_ge(feat_copied, L + 1)

            def add_residual(g):
                for j in range(HP):
                    dve.wait_ge(h_turned, HP * g + j + 1)
                    xt = x_sb[:, bass.ds(NC * g, NC), j * P:(j + 1) * P]
                    nc.vector.tensor_tensor(xt, xt, f_ps[:, j, :].rearrange("p (c q) -> p c q", c=NC), ALU.add).then_inc(x2_ready, 1)

            def graph(g, first=False, last=False):
                L = 2 * g
                for j in range(HP):
                    head_pair(L, 0, j, None if first else g)
                    if first and j == 0:
                        dve.wait_ge(products_ready, 2 * KC)
                        for n in range(2):
                            nc.vector.tensor_reduce(out=wa[:, 1:1 + KC, n * H:(n + 1) * H], in_=w1_products[:, n, :, :].rearrange("p k (h o) -> p k h o", h=H),
                                                    op=ALU.add, axis=AX.X, negate=True).then_inc(wa1_ready, 1)
                    if j == HP - 2 and not first:
                        add_residual(g - 1)
                weight_step(L, 0, H - 1, 1)
                elu_step(L, HP - 2)
                if first:
                    for n in range(1, G):
                        rest = statistics(n)
                    then(rest)
                    inverse_deviation(NC, TT, False)
                min_step(L, HP - 1)
                elu_step(L, HP - 1)

                L = 2 * g + 1
                copy_terms(L, True)
                copy_columns(L, 1)
                score_step(L, 0, 0)
                for j in range(HP):
                    if j == HP - 1 and not last:
                        copy_terms(L + 1, True)
                    head_pair(L, 1, j)
                weight_step(L, 1, H - 1, 1)
                elu_step(L, HP - 2)
                if not last:
                    copy_columns(L + 1, 0)
                    if first:
                        inverse_deviation(NC, TT, True)
                    mask(g + 1, True)
                    score_step(L + 1, 0, 0)
                min_step(L, HP - 1)
                elu_step(L, HP - 1)

            mask(0, False)
            score_step(0, 0, 0)
            graph(0, first=True)
            with dve.Fori(1, G - 1) as g:
                graph(g)
            graph(G - 1, last=True)
            add_residual(G - 1)

            steps = [0]

            def step(ins):
                steps[0] += 1
                ins.then_inc(route_step, 1)
                return steps[0]

            def after(n):
                dve.wait_ge(route_step, n)

            def wide(ap, n):
                return ap.unsqueeze(len(ap.shape)).to_broadcast(list(ap.shape) + [n])

            dve.wait_ge(x2_ready, G * HP)
            for t in range(TT):
                n = step(nc.vector.bn_stats(stats[:, t, :], x_sb[:, t, :]))
            after(n)
            for t in range(TT):
                n = step(nc.vector.bn_aggr(mv[:, t, :], stats[:, t, :]))
            after(n)
            nc.vector.tensor_scalar(rstd[:], mv[:, :, 1], EPS, None, ALU.add).then_inc(var2_done, 1)
            dve.wait_ge(std2_done, 1)
            after(step(nc.vector.reciprocal(rstd[:], rstd[:])))
            with dve.Fori(0, TT // 4) as j:
                for i in range(4):
                    t = 4 * j + i
                    dve.wait_ge(turned, t - 3 + TURNS_FREE)
                    dve.wait_ge(xn_out[i], 16 * j + 16)
                    nc.vector.tensor_scalar(rows_sb[i], x_sb[:, bass.ds(t, 1), :].rearrange("p a d -> p (a d)"),
                                            mv[:, bass.ds(t, 1), 0:1].rearrange("p a d -> p (a d)"),
                                            rstd[:, bass.ds(t, 1)], ALU.subtract, ALU.mult).then_inc(xn_ready, 1)

            dve.wait_ge(moe_consts, MC)
            dve.wait_ge(logits_done, TT)
            logits = f_ps[:, 3, 0:TT * E].rearrange("p (t e) -> p t e", e=E)
            after(step(nc.vector.tensor_reduce(out=rmax[:], in_=logits, op=ALU.max, axis=AX.X)))
            nc.vector.tensor_tensor(score[:], logits, wide(rmax[:], E), ALU.subtract).then_inc(shift_done, 1)
            dve.wait_ge(exp_done, 1)
            after(step(nc.vector.tensor_reduce(out=rtot[:], in_=score[:], op=ALU.add, axis=AX.X)))
            after(step(nc.vector.reciprocal(rtot[:], rtot[:])))
            after(step(nc.vector.tensor_tensor(score[:], score[:], wide(rtot[:], E), ALU.mult)))

            def ranks(out_, in_, scratch, n):
                last = step(nc.vector.memset(out_, 0.0))
                for f in range(n):
                    step(nc.vector.tensor_tensor(scratch[:, :, 0:f + 1], wide(in_[:, :, f], f + 1), in_[:, :, 0:f + 1], ALU.is_gt))
                    if f + 1 < n:
                        step(nc.vector.tensor_tensor(scratch[:, :, f + 1:n], wide(in_[:, :, f], n - f - 1), in_[:, :, f + 1:n], ALU.is_ge))
                    after(steps[0])
                    last = step(nc.vector.tensor_tensor(out_, out_, scratch, ALU.add))
                    after(last)

            after(step(nc.vector.tensor_reduce(out=gtop[:], in_=score[:].rearrange("p t (g e) -> p t g e", g=NGR), op=ALU.max, axis=AX.X)))
            ranks(grank[:], gtop[:], gcmp[:], NGR)
            after(step(nc.vector.tensor_scalar(grank[:], grank[:], float(TOPG), None, ALU.is_lt)))
            after(step(nc.vector.tensor_tensor(score[:].rearrange("p t (g e) -> p (t g) e", g=NGR),
                                               score[:].rearrange("p t (g e) -> p (t g) e", g=NGR),
                                               wide(grank[:].rearrange("p t g -> p (t g)"), EG), ALU.mult)))
            ranks(rank[:], score[:], cmp[:], E)
            nc.vector.tensor_scalar(sel[:], rank[:], float(TOPK), None, ALU.is_lt).then_inc(sel_ready, 1)
            dve.wait_ge(sel_ready, 1)
            after(step(nc.vector.tensor_tensor(comb[:], score[:], sel[:], ALU.mult)))
            after(step(nc.vector.tensor_reduce(out=rtot[:], in_=comb[:], op=ALU.add, axis=AX.X)))
            after(step(nc.vector.tensor_scalar(rtot[:], rtot[:], 1e-20, None, ALU.add)))
            after(step(nc.vector.reciprocal(rtot[:], rtot[:])))
            after(step(nc.vector.tensor_tensor(comb[:], comb[:], wide(rtot[:], E), ALU.mult)))

            dve.wait_ge(counted, 1)
            after(step(nc.vector.tensor_copy(load[:], f_ps[:, 1, 0:E])))
            after(step(nc.vector.tensor_tensor(sq[:], wide(load[:], E), count_p[:].unsqueeze(1).to_broadcast([P, E, E]), ALU.is_gt)))
            after(step(nc.vector.tensor_reduce(out=tiles[:], in_=sq[:], op=ALU.add, axis=AX.X)))
            after(step(nc.vector.tensor_scalar(tiles[:], tiles[:], 1.0, None, ALU.max)))
            after(step(nc.vector.tensor_tensor(sq[:], below[:], tiles[:].unsqueeze(1).to_broadcast([P, E, E]), ALU.mult)))
            after(step(nc.vector.tensor_reduce(out=first[:], in_=sq[:], op=ALU.add, axis=AX.X)))
            after(step(nc.vector.tensor_scalar(first_row[:], first[:], float(P), None, ALU.mult)))
            after(step(nc.vector.tensor_tensor(place[:], f_ps[:, 3, 0:TT * E].rearrange("p (t e) -> p t e", e=E),
                                               first_row[:].unsqueeze(1).to_broadcast([P, TT, E]), ALU.add)))
            for k in range(TOPK):
                after(step(nc.vector.tensor_scalar(eq[:], rank[:], float(k), None, ALU.is_equal)))
                step(nc.vector.tensor_tensor(cmp[:], eq[:], place[:], ALU.mult))
                after(step(nc.vector.tensor_tensor(sel[:], eq[:], comb[:], ALU.mult)))
                step(nc.vector.tensor_reduce(out=place_k[:, :, k], in_=cmp[:], op=ALU.add, axis=AX.X))
                after(step(nc.vector.tensor_reduce(out=w_k[:, :, k], in_=sel[:], op=ALU.add, axis=AX.X)))
            after(step(nc.vector.tensor_copy(place_i[:], place_k[:])))
            step(nc.vector.tensor_scalar(slot_i[:], place_i[:], 7, None, ALU.logical_shift_right))
            after(step(nc.vector.tensor_scalar(row_i[:], place_i[:], P - 1, None, ALU.bitwise_and)))
            step(nc.vector.tensor_copy(slot_f[:], slot_i[:]))
            after(step(nc.vector.tensor_copy(row_f[:], row_i[:])))
            after(step(nc.vector.tensor_tensor(tok_k[:], wide(token[:], TOPK), row_f[:], ALU.subtract)))
            after(step(nc.vector.tensor_scalar(tok_k[:], tok_k[:], float(-T), None, ALU.add)))
            for t in range(TT):
                i = t % 2
                if t >= 2:
                    dve.wait_ge(entered, t - 1)
                step(nc.vector.tensor_tensor(row_hot[:, i, :, :], count[:].unsqueeze(1).to_broadcast([P, TOPK, P]),
                                             wide(row_f[:, t, :], P), ALU.is_equal))
                after(step(nc.vector.tensor_tensor(slot_hot[:, i, :, :], count[:, 0:RT].unsqueeze(1).to_broadcast([P, TOPK, RT]),
                                                   wide(slot_f[:, t, :], RT), ALU.is_equal)))
                step(nc.vector.tensor_tensor(entry[:, i, :, 0, :], slot_hot[:, i, :, :], wide(tok_k[:, t, :], RT), ALU.mult))
                after(steps[0])
                nc.vector.tensor_tensor(entry[:, i, :, 1, :], slot_hot[:, i, :, :], wide(w_k[:, t, :], RT), ALU.mult).then_inc(entry_ready, 1)

            after(step(nc.vector.tensor_tensor(owner[:], wide(count[0:1, 0:RT], E), first[0:1, :].unsqueeze(1).to_broadcast([1, RT, E]), ALU.is_ge)))
            after(step(nc.vector.tensor_reduce(out=prior[:], in_=owner[:], op=ALU.add, axis=AX.X)))
            after(step(nc.vector.tensor_scalar(ctl_f[0:1, 0, :], prior[:], -1.0, None, ALU.add)))
            step(nc.vector.memset(ctl_f[0:1, 2, 0:1], 1.0))
            after(step(nc.vector.tensor_tensor(ctl_f[0:1, 2, 1:RT], ctl_f[0:1, 0, 1:RT], ctl_f[0:1, 0, 0:RT - 1], ALU.not_equal)))
            after(step(nc.vector.tensor_scalar(prior[:], ctl_f[0:1, 0, :], float(E - 1), None, ALU.is_lt)))
            step(nc.vector.tensor_tensor(ctl_f[0:1, 2, :], ctl_f[0:1, 2, :], prior[:], ALU.mult))
            after(step(nc.vector.tensor_copy(ctl[0:1, 0, :], ctl_f[0:1, 0, :])))
            step(nc.vector.tensor_copy(ctl[0:1, 2, :], ctl_f[0:1, 2, :]))
            after(step(nc.vector.tensor_tensor(used_f[:], first[0:1, E - 1:E], tiles[0:1, E - 1:E], ALU.add)))
            step(nc.vector.tensor_scalar(ctl_f[0:1, 1, :], count[0:1, 0:RT], used_f[:, 0:1], None, ALU.is_lt))
            after(step(nc.vector.tensor_scalar(used_f[:], used_f[:], 1.0, None, ALU.add)))
            step(nc.vector.tensor_copy(used[:], used_f[:]))
            after(step(nc.vector.tensor_copy(ctl[0:1, 1, :], ctl_f[0:1, 1, :])))
            after(step(nc.vector.tensor_scalar(used[:], used[:], -2, None, ALU.bitwise_and)))
            dve.wait_ge(entered, TT)
            after(step(nc.vector.tensor_scalar(idx_f[:], f_ps[:, 1, 0:RT], pad_row[:, 0:1], None, ALU.add)))
            step(nc.vector.tensor_copy(w_tab[:], f_ps[:, 1, RT:2 * RT]))
            after(steps[0])
            nc.vector.tensor_copy(idx_tab[:], idx_f[:]).then_inc(tables_ready, 1)
            dve.wait_ge(tables_ready, 1)

            def split_low(i, p, count_before):
                a, b = PIECES[p]
                dve.wait_ge(hi_ready, count_before + p + 1)
                nc.vector.tensor_tensor(split[:, bass.ds((i * 2 + 1) * WL + a, b - a)], w_stage[:, bass.ds(i * WL + a, b - a)],
                                        split[:, bass.ds(i * 2 * WL + a, b - a)].bitcast(f32), ALU.subtract).then_inc(lo_ready, 1)

            def gate(r):
                dve.wait_ge(silu_done, SS + r + 1)
                nc.vector.tensor_tensor(hid[:], sg[:], o_ps[:, 1, 0:I], ALU.mult).then_inc(hid_ready, 1)

            def x_low(r, i):
                dve.wait_ge(xT_ready, 2 * TT + r + 1)
                nc.vector.tensor_tensor(xT_lo[:, i, :, :], tr_ps[:, i, :, :], xT_hi[:, i, :, :].bitcast(f32), ALU.subtract).then_inc(xT_split, 1)

            def hidden_low(r):
                dve.wait_ge(hidT_ready, SS + r + 1)
                nc.vector.tensor_tensor(hidT_lo[:, 0:DC - 1, :], hidden_ps(0, DC - 1), hidT_hi[:, 0:DC - 1, :].bitcast(f32), ALU.subtract)
                nc.vector.tensor_tensor(hidT_lo[0:LASTD, DC - 1, :], f_ps[0:LASTD, 0, (DC - 1) * P:DC * P],
                                        hidT_hi[0:LASTD, DC - 1, :].bitcast(f32), ALU.subtract).then_inc(hidT_split, 1)

            def weigh(r, i, first=False):
                dve.wait_ge(down_done, SS + r + 1)
                if first:
                    dve.wait_ge(tile_out[i], 16 * (TT // 2 + 1))
                else:
                    dve.wait_ge(added, 16 * r - 16)
                nc.vector.tensor_scalar(y_sb[:, i, :], f_ps[:, 2, :], w_tab[:, bass.ds(r, 1)], None, ALU.mult).then_inc(y_ready, 1)

            def shared_add_last():
                dve.wait_ge(down_done, SS)
                dve.wait_ge(tile_out[1], 16 * (TT // 2))
                nc.vector.tensor_tensor(y_sb[:, 1, :], f_ps[:, 2, :], x_sb[:, TT - 1, :], ALU.add).then_inc(y_ready, 1)

            def slot(r, i, first=False):
                def weigh_before():
                    if first and r == 0:
                        shared_add_last()
                    else:
                        weigh(r - 1, 1 - i, first=first)

                new = dve.value_load(ctl[0:1, 2, bass.ds(r, 1)], min_val=0, max_val=1)
                with dve.If(new):
                    expert = dve.value_load(ctl[0:1, 0, bass.ds(r, 1)], min_val=0, max_val=E - 1)
                    half = expert % 2
                    pieces = NP_ * SH + NP_ * (expert + 1)
                    gate(r)
                    x_low(r + 1, 1 - i)
                    split_low(1 - half, 0, pieces)
                    hidden_low(r)
                    weigh_before()
                    split_low(1 - half, 1, pieces)
                    split_low(1 - half, 2, pieces)
                with dve.Else():
                    gate(r)
                    x_low(r + 1, 1 - i)
                    weigh_before()
                    hidden_low(r)

            split_low(0, 0, NP_ * SH)
            split_low(0, 1, NP_ * SH)
            x_low(0, 0)
            split_low(0, 2, NP_ * SH)
            slot(0, 0, first=True)
            slot(1, 1, first=True)
            slot(2, 0, first=True)
            with dve.Fori(1, ALWAYS // 2) as j:
                slot(2 * j + 1, 1)
                slot(2 * j + 2, 0)
            with dve.Fori(ALWAYS // 2, PAIRS) as j:
                in_use = dve.value_load(ctl[0:1, 1, bass.ds(2 * j, 1)], min_val=0, max_val=1)
                with dve.If(in_use):
                    slot(2 * j + 1, 1)
                    slot(2 * j + 2, 0)

        @block.tensor
        def _(pe):
            pe.wait_ge(consts, 1)
            pe.wait_ge(w_in, 16 * 7)
            pe.wait_ge(wa_ready, 1)

            def transpose_step(L, j, s, wait_copy=True):
                r = RING * j + s
                pe.wait_ge(alpha_ready, R * L + r + 1)
                if wait_copy:
                    pe.wait_ge(evac_done, R * L + r - 1)
                for m in range(NC):
                    last = nc.tensor.transpose(tr_ps[:, s % 2, m, :], ring[:, s % RING, m * P:(m + 1) * P], ident[:])
                last.then_inc(T_done, 1)

            def mix_step(L, h, i, m):
                if m == 0:
                    pe.wait_ge(evac_done, R * L + NC * h + NC)
                    pe.wait_ge(head_feat_ready, H * L + h + 1)
                    pe.wait_ge(parts_ready, H * L + h - 1 + FREE)
                done = nc.tensor.matmul(o_ps[O * i:O * i + O, i, :], head_feat[:, i, m, :], eT[:, i, m, :],
                                        start=(m == 0), stop=(m == NC - 1))
                if m == NC - 1:
                    done.then_inc(mixed, 1)

            def head_pair(L, j, last):
                for s in range(RING):
                    if not (last and s + NC >= RING):
                        transpose_step(L, j, s + NC)
                    mix_step(L, 2 * j + s // NC, s // NC, s % NC)

            def rows(w, k):
                return w[:, k, :, :].rearrange("p h o -> p (h o)")

            def terms_turned(L):
                pe.wait_ge(st_copied, L + 1)
                pe.sem_inc(pe_waited, 1)
                for c in range(NC):
                    last = nc.tensor.transpose(f_ps[:, 2, c * 2 * H:(c + 1) * 2 * H], st_sb[:, c * P:(c + 1) * P], ident[0:2 * H, 0:2 * H])
                last.then_inc(s_turned, 1)

            def terms_even(g):
                pe.wait_ge(ctx_in, 16 * g + 16)
                if not (isinstance(g, int) and g == 0):
                    pe.wait_ge(feat_copied, 2 * g)
                nc.tensor.matmul(f_ps[0:2 * H, 3, :], wa[:, 0, :], ctx_sb[:], start=True, stop=True).then_inc(st_done, 1)

            def features_even(g):
                terms_turned(2 * g)
                for c in range(2):
                    nc.tensor.matmul(f_ps[:, c, :], ctx_sb[:, c * P:(c + 1) * P], rows(w0_sb, 0), start=True, stop=True)
                nc.tensor.matmul(f_ps[:, 3, :], ctx_sb[:, 3 * P:4 * P], rows(w0_sb, 0), start=True, stop=True)

            def features_even_rest(g):
                pe.wait_ge(s_copied, 2 * g + 1)
                nc.tensor.matmul(f_ps[:, 2, :], ctx_sb[:, 2 * P:3 * P], rows(w0_sb, 0), start=True, stop=True).then_inc(feat_done, 1)

            def features_odd(g, first):
                L = 2 * g + 1
                if first:
                    pe.wait_ge(wa1_ready, 2)
                if not first:
                    pe.wait_ge(x2_ready, HP * g)

                def terms(k):
                    return nc.tensor.matmul(f_ps[0:2 * H, 3, :], wa[:, 1 + k, :], hT[:, k, :], start=(k == 0), stop=(k == KC - 1))

                def features(c, k):
                    return nc.tensor.matmul(f_ps[:, c, :], hT[:, k, c * P:(c + 1) * P], rows(w1_sb, k), start=(k == 0), stop=(k == KC - 1))

                for k in range(KC - 1):
                    pe.wait_ge(hT_ready, HP * (L - 1) + k + 2)
                    terms(k)
                for k in range(KC - 1):
                    features(0, k)
                pe.wait_ge(hT_ready, HP * (L - 1) + KC + 1)
                terms(KC - 1).then_inc(st_done, 1)
                features(0, KC - 1)
                terms_turned(L)
                for k in range(KC):
                    features(1, k)
                pe.wait_ge(s_copied, L + 1)
                for c in (2, 3):
                    for k in range(KC):
                        last = features(c, k)
                last.then_inc(feat_done, 1)

            def nodes_back(g, last):
                if not last:
                    pe.wait_ge(feat_copied, 2 * g + 3)
                for j in range(HP):
                    pe.wait_ge(hT_ready, HP * (2 * g + 1) + j + 2)
                    for c in range(NC):
                        done = nc.tensor.transpose(f_ps[:, j, c * P:(c + 1) * P], hT[:, j, c * P:(c + 1) * P], ident[:])
                    done.then_inc(h_turned, 1)

            def graph(g, first=False, last=False):
                L = 2 * g
                for s in range(NC):
                    transpose_step(L, 0, s, wait_copy=s >= 2)
                head_pair(L, 0, False)
                if not first:
                    nodes_back(g - 1, False)
                with pe.Fori(1, HP - 1) as j:
                    head_pair(L, j, False)
                head_pair(L, HP - 1, True)
                features_odd(g, first)
                L = 2 * g + 1
                for s in range(NC):
                    transpose_step(L, 0, s, wait_copy=s >= 2)
                head_pair(L, 0, False)
                if not last:
                    terms_even(g + 1)
                with pe.Fori(1, HP - 1) as j:
                    head_pair(L, j, False)
                if not last:
                    features_even(g + 1)
                head_pair(L, HP - 1, True)
                if not last:
                    features_even_rest(g + 1)

            terms_even(0)
            features_even(0)
            features_even_rest(0)
            graph(0, first=True)
            with pe.Fori(1, G - 1) as g:
                graph(g)
            graph(G - 1, last=True)
            nodes_back(G - 1, True)
            pe.wait_ge(x2_ready, HP * G)

            pe.wait_ge(gate_in, 16)
            def turn_tile(t, i):
                pe.wait_ge(xn_ready, t + 1)
                for k in range(KC):
                    last = nc.tensor.transpose(tr_ps[:, i % 2, k, :], rows_sb[i][:, k * P:(k + 1) * P], ident[:])
                last.then_inc(turned, 1)

            def tile_logits(t, i):
                pe.wait_ge(xT_ready, t + 1)
                for k in range(KC):
                    last = nc.tensor.matmul(f_ps[:, 3, bass.ds(t * E, E)], xT[i][:, k, :], gate_sb[:, k, :],
                                            start=(k == 0), stop=(k == KC - 1))
                last.then_inc(logits_done, 1)

            with pe.Fori(0, TT // 4) as j:
                for i in range(0, 4, 2):
                    for n in range(2):
                        turn_tile(4 * j + i + n, i + n)
                    for n in range(2):
                        tile_logits(4 * j + i + n, n)

            def counts():
                pe.wait_ge(moe_consts, MC)
                pe.wait_ge(sel_ready, 1)
                nc.tensor.matmul(f_ps[:, 3, 0:E], tri[:], sel[:, 0, :], start=True, stop=True)
                nc.tensor.matmul(f_ps[:, 3, E:TT * E], tri[:], sel[:, 1:TT, :].rearrange("p t e -> p (t e)"), start=True, stop=False)
                for t in reversed(range(TT - 1)):
                    nc.tensor.matmul(f_ps[:, 3, (t + 1) * E:TT * E].rearrange("p (t e) -> p t e", e=E), ones[:],
                                     sel[:, t:t + 1, :].to_broadcast([P, TT - 1 - t, E]), start=False, stop=(t == 0))
                for t in range(TT):
                    last = nc.tensor.matmul(f_ps[:, 1, 0:E], ones[:], sel[:, t, :], start=(t == 0), stop=(t == TT - 1))
                last.then_inc(counted, 1)

            def enter(t, i, first=False, last=False):
                pe.wait_ge(entry_ready, t + 1)
                for k in range(TOPK):
                    done = nc.tensor.matmul(f_ps[:, 1, 0:2 * RT], row_hot[:, i, k, :],
                                            entry[:, i, k, :, :].rearrange("p a s -> p (a s)"),
                                            start=(first and k == 0), stop=(last and k == TOPK - 1))
                done.then_inc(entered, 1)

            def turn(n, i, arrived, count):
                pe.wait_ge(arrived, count)
                for k in range(KC):
                    last = nc.tensor.transpose(tr_ps[:, i, k, :], xg[:, i, k * P:(k + 1) * P], ident[:])
                last.then_inc(turned, 1)

            def up(n, i, s, half):
                pe.wait_ge(xT_split, n + 1)
                for part in range(2):
                    for k in range(KC):
                        at = half * 2 * WL + (2 * k + part) * I
                        hi, lo = split[:, bass.ds(at, I)], split[:, bass.ds(at + WL, I)]
                        nc.tensor.matmul(o_ps[:, part, 0:I], xT_hi[:, i, k, :], hi, start=(k == 0), stop=False)
                        nc.tensor.matmul(o_ps[:, part, 0:I], xT_hi[:, i, k, :], lo, start=False, stop=False)
                        last = nc.tensor.matmul(o_ps[:, part, 0:I], xT_lo[:, i, k, :], hi, start=False, stop=(k == KC - 1))
                last.then_inc(up_done, 1)

            def down(s, half, free, first=True, final=True, load=lambda: None):
                pe.wait_ge(hidT_split, s + 1)
                if free is not None:
                    pe.wait_ge(y_ready, free)
                for c in range(DC):
                    rows = P if c < DC - 1 else LASTD
                    at = half * 2 * WL + UP + c * D
                    if c == DC - 1:
                        loaded = load()
                    hi, lo = split[0:rows, bass.ds(at, D)], split[0:rows, bass.ds(at + WL, D)]
                    nc.tensor.matmul(f_ps[:, 2, :], hidT_hi[0:rows, c, :], hi, start=(first and c == 0), stop=False)
                    nc.tensor.matmul(f_ps[:, 2, :], hidT_hi[0:rows, c, :], lo, start=False, stop=False)
                    last = nc.tensor.matmul(f_ps[:, 2, :], hidT_lo[0:rows, c, :], hi, start=False, stop=(final and c == DC - 1))
                last.then_inc(down_done, 1)
                return loaded

            def turn_hidden(s):
                pe.wait_ge(hid_ready, s + 1)
                for c in range(DC):
                    rows = P if c < DC - 1 else LASTD
                    last = nc.tensor.transpose(f_ps[0:rows, 0, c * P:(c + 1) * P], hid[:, c * P:c * P + rows], ident[:])
                last.then_inc(hid_turned, 1)

            def shared_up(t, i, u):
                up(t, i, 2 * t + u, u)

            def shared_down(t, u, **load):
                if u == 0 and (not isinstance(t, int) or t > 0):
                    pe.wait_ge(sum_copied, t)
                return down(2 * t + u, u, None, first=(u == 0), final=(u == 1), **load)

            def shared_tile(t, i, turn_next, between=lambda u: None):
                shared_down(t - 1, 0)
                turn_hidden(2 * t - 1)
                shared_up(t, i, 0)
                between(0)
                shared_down(t - 1, 1)
                turn_hidden(2 * t)
                shared_up(t, i, 1)
                between(1)
                turn_next()

            pe.wait_ge(lo_ready, NP_)
            turn(0, 0, tile_in[0], 16)
            shared_up(0, 0, 0)
            turn_hidden(0)
            pe.wait_ge(lo_ready, NP_ * SH)
            shared_up(0, 0, 1)
            turn(1, 1, tile_in[1], 16)

            def tile_pair(j, between=lambda t, i, u: None):
                for i in range(2):
                    t = 2 * j + 1 + i
                    shared_tile(t, 1 - i, lambda: turn(t + 1, i, tile_in[i], 16 * (j + 1) + 16),
                                lambda u: between(t, i, u))

            shared_tile(1, 1, lambda: turn(2, 0, tile_in[0], 32))
            shared_tile(2, 0, lambda: turn(3, 1, tile_in[1], 32))
            with pe.Fori(1, BEFORE_COUNTS) as j:
                tile_pair(j)
            counts()
            BT = BEFORE_COUNTS
            def enters(first, final=False):
                def between(t, i, u):
                    enter(2 * (t - (2 * BT + 1)) + u, u, first and i == 0 and u == 0, final and i == 1 and u == 1)
                return between

            tile_pair(BT, enters(True))
            with pe.Fori(BT + 1, TT // 2 - 2) as j:
                tile_pair(j, enters(False))
            tile_pair(TT // 2 - 2, enters(False, True))
            shared_tile(TT - 1, 1, lambda: turn(TT, 0, xg_in[0], 16))

            def expert_of(r):
                return pe.value_load(ctl[0:1, 0, bass.ds(r, 1)], min_val=0, max_val=E - 1)

            def routed_up(r, i, expert):
                pe.wait_ge(lo_ready, NP_ * (SH + expert) + NP_ - 1)
                up(TT + r, i, SS + r, expert % 2)

            def routed_down(r, expert, load=lambda: None):
                pe.wait_ge(lo_ready, NP_ * (SH + expert) + NP_)
                return down(SS + r, expert % 2, TT + r, load=load)

            shared_down(TT - 1, 0)
            turn_hidden(SS - 1)
            routed_up(0, 0, 0)
            turn(TT + 1, 1, xg_in[1], 16)
            e1 = shared_down(TT - 1, 1, load=lambda: expert_of(1))
            turn_hidden(SS)
            routed_up(1, 1, e1)
            turn(TT + 2, 0, xg_in[0], 32)
            carried = [pe.alloc_register(f"carried_expert{i}") for i in range(2)]
            pe.reg_mov(carried[0], 0)
            pe.reg_mov(carried[1], e1)

            def slot_pair(j):
                for i in range(2):
                    r = 2 * j + i
                    expert = pe.snap(carried[i], min_val=0, max_val=E - 1)
                    later = routed_down(r, expert, load=lambda: expert_of(r + 2))
                    turn_hidden(SS + r + 1)
                    routed_up(r + 2, i, later)
                    pe.reg_mov(carried[i], later)
                    turn(TT + r + 3, 1 - i, xg_in[1 - i], 16 * (j + 2 + i))

            with pe.Fori(0, ALWAYS // 2) as j:
                slot_pair(j)
            with pe.Fori(ALWAYS // 2, PAIRS) as j:
                in_use = pe.value_load(ctl[0:1, 1, bass.ds(2 * j, 1)], min_val=0, max_val=1)
                with pe.If(in_use):
                    slot_pair(j)


_IN = ("x", "ctxT", "W0", "as0", "an0", "b0", "W1", "as1", "an1", "b1", "gateT", "experts")


def kernel(**inputs):
    import numpy as np
    import concourse.bacc as bacc
    from concourse import mybir
    from concourse.bass_utils import run_bass_kernel_spmd

    a = {n.replace("L0_xattn_", "").replace("L0_ffn_", ""): np.asarray(v) for n, v in inputs.items()}
    P, D, I, E = 128, 512, 352, 16

    def up_rows(w):
        return w.T.reshape(D // P, P, 2 * I).transpose(1, 0, 2).reshape(P, -1)

    def down_rows(w):
        full = np.zeros((3 * P, D), w.dtype)
        full[:I] = w.T
        return full.reshape(3, P, D).transpose(1, 0, 2).reshape(P, -1)

    units = [(a["expert_up_w"][e], a["expert_down_w"][e]) for e in range(E)]
    S = 2 * I
    for u in range(2):
        rows = slice(u * I, (u + 1) * I)
        units.append((np.concatenate([a["shared_up_w"][0:S][rows], a["shared_up_w"][S:2 * S][rows]]),
                      a["shared_down_w"][:, rows]))
    experts = np.stack([np.concatenate([up_rows(u), down_rows(d)], axis=1) for u, d in units])
    arrays = dict(zip(_IN, (a["x"], a["ctx_512"].transpose(0, 2, 1), a["W0"], a["a_self0"], a["a_neigh0"], a["b0"],
                            a["W1"], a["a_self1"], a["a_neigh1"], a["b1"], a["gate_w"].T, experts)))
    arrays = {n: np.ascontiguousarray(v) for n, v in arrays.items()}
    nc = bacc.Bacc("TRN2", target_bir_lowering=False, num_devices=1)
    args = [nc.dram_tensor(f"in_{n}", v.shape, mybir.dt.from_np(v.dtype), kind="ExternalInput").ap() for n, v in arrays.items()]
    T = a["x"].shape[0] * a["x"].shape[1]
    out = nc.dram_tensor("out_rows", (T + P, D), mybir.dt.float32, kind="ExternalOutput").ap()
    gat_then_experts(nc, *args, out)
    r = run_bass_kernel_spmd(nc, [{f"in_{n}": v for n, v in arrays.items()}], core_ids=[0])
    return r.results[0]["out_rows"][:T].reshape(a["x"].shape)
```
